# Optimizing a Trainium2 kernel written in Bass

```python
import numpy as np
import jax
import jax.numpy as jnp

def _softmax(x, axis=-1):
    return jax.nn.softmax(x, axis=axis)

def _gelu(x):
    return jax.nn.gelu(x, approximate=True)

def _silu(x):
    return jax.nn.silu(x)

def _sigmoid(x):
    return jax.nn.sigmoid(x)

def _layernorm(x, axis=-1, eps=1e-05):
    m = jnp.mean(x, axis=axis, keepdims=True)
    v = jnp.var(x, axis=axis, keepdims=True)
    return (x - m) / jnp.sqrt(v + eps)

def _scatter_add(tgt, idx, src, axis=0):
    return tgt.at[idx].add(src)

def _segment_sum(src, seg, n):
    return jax.ops.segment_sum(src, seg, n)
kernel_name = 'mk_lm_tower_d1_tok_ids1024_r4_35dbb4'

def setup_inputs(seed: int=0):
    np.random.seed(seed)
    _w = jnp.asarray

    def _rec_inputs():
        import jax
        import jax.numpy as jnp
        _rk = jax.random.key(seed)
        x = jax.random.randint(jax.random.fold_in(_rk, 1), (16, 256), 0, 267694, jnp.int32)
        return x
    x = _rec_inputs()

    def _L0_tok_setup():
        import jax, jax.numpy as jnp
        import numpy as np
        N_TOKEN = 267735
        D_PROJ = 256
        CUTOFF_ENDS = [0, 5000, 10000, 50000, N_TOKEN]
        DIV_VAL = 4
        D_EMBS = [256 // DIV_VAL ** i for i in range(4)]
        EMB_SCALE = float(D_PROJ) ** 0.5
        key = jax.random.key(seed)
        ks = jax.random.split(key, 9)
        inp = jax.random.randint(ks[0], (4, 1024), 0, N_TOKEN, dtype=jnp.int64)
        out = {'inp': inp}
        for i in range(4):
            l, r = (CUTOFF_ENDS[i], CUTOFF_ENDS[i + 1])
            d_i = D_EMBS[i]
            out[f'emb{i}'] = jax.random.normal(ks[1 + i], (r - l, d_i), dtype=jnp.float32) * d_i ** (-0.5)
            out[f'proj{i}'] = jax.random.normal(ks[5 + i], (D_PROJ, d_i), dtype=jnp.float32) * D_PROJ ** (-0.5)
        return out
    _L0_tok_all = _L0_tok_setup()
    _L0_tok_in = {k: v for k, v in _L0_tok_all.items() if k in ('emb0', 'emb1', 'emb2', 'emb3', 'proj0', 'proj1', 'proj2', 'proj3')}
    del _L0_tok_all

    def _L0_attn_setup():
        import jax, jax.numpy as jnp
        import numpy as np
        EPS_NORM = 1e-12
        RMS_EPS = 1e-05

        def _rmsnorm(x, w):
            var = jnp.mean(jnp.square(x), axis=-1, keepdims=True)
            return x * jax.lax.rsqrt(var + RMS_EPS) * w

        def _path_attention(x, Wq, Wk, Wv, Wo, wA, wB, conv_w, beta_w, g_w, g_b, qnorm_w, knorm_w):
            B, T, D = x.shape
            d = qnorm_w.shape[0]
            H = D // d
            scale = d ** (-0.5)
            q = (x @ Wq).reshape(B, T, H, d)
            k = (x @ Wk).reshape(B, T, H, d)
            v = (x @ Wv).reshape(B, T, H, d)
            w = x @ wA @ wB
            wp = jnp.pad(w, ((0, 0), (2, 0), (0, 0)))
            w = wp[:, 0:T] * conv_w[:, 0] + wp[:, 1:T + 1] * conv_w[:, 1] + wp[:, 2:T + 2] * conv_w[:, 2]
            w = jax.nn.silu(w).reshape(B, T, H, d)
            w = w * jax.lax.rsqrt(jnp.sum(jnp.square(w), -1, keepdims=True) + EPS_NORM)
            beta = 2.0 * jax.nn.sigmoid(x @ beta_w)
            g = jax.nn.log_sigmoid(x @ g_w + g_b)
            q = _rmsnorm(q, qnorm_w)
            k = _rmsnorm(k, knorm_w)
            q, k, v, w = (t.transpose(0, 2, 1, 3) for t in (q, k, v, w))
            beta = beta.transpose(0, 2, 1)
            g = g.transpose(0, 2, 1)
            tri_s = jnp.tril(jnp.ones((T, T), bool), -1)
            C = jnp.einsum('bhtd,bhsd->bhts', w, w) * beta[:, :, None, :]
            L = jnp.where(tri_s, C, 0.0) + jnp.eye(T, dtype=x.dtype)
            Rhs = jnp.where(tri_s, jnp.einsum('bhtd,bhjd->bhtj', w, k), 0.0)
            A = jax.scipy.linalg.solve_triangular(L, Rhs, lower=True, unit_diagonal=True)
            tri = jnp.tril(jnp.ones((T, T), bool))
            qw = jnp.where(tri, jnp.einsum('bhid,bhtd->bhit', q, w), 0.0)
            S = jnp.einsum('bhid,bhjd->bhij', q, k) - jnp.einsum('bhit,bhtj->bhij', qw, beta[..., None] * A)
            G = jnp.cumsum(g, axis=-1)
            logits = S * scale + (G[..., :, None] - G[..., None, :])
            logits = jnp.where(tri, logits, -1e+30)
            P = jax.nn.softmax(logits, axis=-1)
            o = jnp.einsum('bhij,bhjd->bhid', P, v)
            return o.transpose(0, 2, 1, 3).reshape(B, T, D) @ Wo
        key = jax.random.key(seed)
        B, T, D, H, R, K = (2, 128, 256, 16, 32, 3)
        d = D // H
        ks = jax.random.split(key, 11)
        s = 0.02
        return dict(x=jax.random.normal(ks[0], (B, T, D), jnp.float32), Wq=jax.random.normal(ks[1], (D, D), jnp.float32) * s, Wk=jax.random.normal(ks[2], (D, D), jnp.float32) * s, Wv=jax.random.normal(ks[3], (D, D), jnp.float32) * s, Wo=jax.random.normal(ks[4], (D, D), jnp.float32) * s, wA=jax.random.normal(ks[5], (D, R), jnp.float32) * s, wB=jax.random.normal(ks[6], (R, D), jnp.float32) * s, conv_w=jax.random.normal(ks[7], (D, K), jnp.float32) * 0.5, beta_w=jax.random.normal(ks[8], (D, H), jnp.float32) * s, g_w=jax.random.normal(ks[9], (D, H), jnp.float32) * s, g_b=jnp.zeros((H,), jnp.float32), qnorm_w=jnp.ones((d,), jnp.float32), knorm_w=jnp.ones((d,), jnp.float32))
    _L0_attn_all = _L0_attn_setup()
    _L0_attn_in = {k: v for k, v in _L0_attn_all.items() if k in ('Wq', 'Wk', 'Wv', 'Wo', 'wA', 'wB', 'conv_w', 'beta_w', 'g_w', 'g_b', 'qnorm_w', 'knorm_w')}
    del _L0_attn_all

    def _L0_ffn_setup():
        import jax, jax.numpy as jnp
        import numpy as np
        E, K = (8, 4)
        B, S, D = (4, 256, 256)
        H = D * 2 * 4 // 3

        def _swiglu(u, w1, w2, w3):
            h = jnp.einsum('...d,hd->...h', u, w1)
            v = jnp.einsum('...d,hd->...h', u, w2)
            return jnp.einsum('...h,dh->...d', jax.nn.sigmoid(h) * h * v, w3)
        key = jax.random.key(seed)
        ks = jax.random.split(key, 9)
        std = 0.02
        return {'x': jax.random.normal(ks[0], (B, S, D), jnp.float32), 'Wg': jax.random.normal(ks[1], (E, D), jnp.float32) * std, 'routing_bias': jnp.zeros((E,), jnp.float32), 'W1': jax.random.normal(ks[2], (E, H, D), jnp.float32) * std, 'W2': jax.random.normal(ks[3], (E, H, D), jnp.float32) * std, 'W3': jax.random.normal(ks[4], (E, D, H), jnp.float32) * std, 'Ws1': jax.random.normal(ks[5], (H, D), jnp.float32) * std, 'Ws2': jax.random.normal(ks[6], (H, D), jnp.float32) * std, 'Ws3': jax.random.normal(ks[7], (D, H), jnp.float32) * std}
    _L0_ffn_all = _L0_ffn_setup()
    _L0_ffn_in = {k: v for k, v in _L0_ffn_all.items() if k in ('Wg', 'routing_bias', 'W1', 'W2', 'W3', 'Ws1', 'Ws2', 'Ws3')}
    del _L0_ffn_all
    return {'x': x, 'L0_tok_emb0': _L0_tok_in['emb0'], 'L0_tok_emb1': _L0_tok_in['emb1'], 'L0_tok_emb2': _L0_tok_in['emb2'], 'L0_tok_emb3': _L0_tok_in['emb3'], 'L0_tok_proj0': _L0_tok_in['proj0'], 'L0_tok_proj1': _L0_tok_in['proj1'], 'L0_tok_proj2': _L0_tok_in['proj2'], 'L0_tok_proj3': _L0_tok_in['proj3'], 'L0_attn_Wq': _L0_attn_in['Wq'], 'L0_attn_Wk': _L0_attn_in['Wk'], 'L0_attn_Wv': _L0_attn_in['Wv'], 'L0_attn_Wo': _L0_attn_in['Wo'], 'L0_attn_wA': _L0_attn_in['wA'], 'L0_attn_wB': _L0_attn_in['wB'], 'L0_attn_conv_w': _L0_attn_in['conv_w'], 'L0_attn_beta_w': _L0_attn_in['beta_w'], 'L0_attn_g_w': _L0_attn_in['g_w'], 'L0_attn_g_b': _L0_attn_in['g_b'], 'L0_attn_qnorm_w': _L0_attn_in['qnorm_w'], 'L0_attn_knorm_w': _L0_attn_in['knorm_w'], 'L0_ffn_Wg': _L0_ffn_in['Wg'], 'L0_ffn_routing_bias': _L0_ffn_in['routing_bias'], 'L0_ffn_W1': _L0_ffn_in['W1'], 'L0_ffn_W2': _L0_ffn_in['W2'], 'L0_ffn_W3': _L0_ffn_in['W3'], 'L0_ffn_Ws1': _L0_ffn_in['Ws1'], 'L0_ffn_Ws2': _L0_ffn_in['Ws2'], 'L0_ffn_Ws3': _L0_ffn_in['Ws3']}

def reference(x, L0_tok_emb0, L0_tok_emb1, L0_tok_emb2, L0_tok_emb3, L0_tok_proj0, L0_tok_proj1, L0_tok_proj2, L0_tok_proj3, L0_attn_Wq, L0_attn_Wk, L0_attn_Wv, L0_attn_Wo, L0_attn_wA, L0_attn_wB, L0_attn_conv_w, L0_attn_beta_w, L0_attn_g_w, L0_attn_g_b, L0_attn_qnorm_w, L0_attn_knorm_w, L0_ffn_Wg, L0_ffn_routing_bias, L0_ffn_W1, L0_ffn_W2, L0_ffn_W3, L0_ffn_Ws1, L0_ffn_Ws2, L0_ffn_Ws3):
    import jax
    import jax.numpy as jnp

    def _L0_tok_ref(inp, emb0, emb1, emb2, emb3, proj0, proj1, proj2, proj3):
        import jax, jax.numpy as jnp
        import numpy as np
        N_TOKEN = 267735
        D_PROJ = 256
        CUTOFF_ENDS = [0, 5000, 10000, 50000, N_TOKEN]
        DIV_VAL = 4
        D_EMBS = [256 // DIV_VAL ** i for i in range(4)]
        EMB_SCALE = float(D_PROJ) ** 0.5
        embs = [emb0, emb1, emb2, emb3]
        projs = [proj0, proj1, proj2, proj3]
        B, S = inp.shape
        out = jnp.zeros((B, S, D_PROJ), dtype=emb0.dtype)
        for i in range(4):
            l, r = (CUTOFF_ENDS[i], CUTOFF_ENDS[i + 1])
            mask = (inp >= l) & (inp < r)
            idx = jnp.clip(inp - l, 0, r - l - 1)
            e = embs[i][idx]
            p = jnp.einsum('bsd,pd->bsp', e, projs[i])
            out = out + jnp.where(mask[..., None], p, jnp.zeros((), dtype=p.dtype))
        return out * jnp.asarray(EMB_SCALE, dtype=out.dtype)

    def _L0_attn_ref(x, Wq, Wk, Wv, Wo, wA, wB, conv_w, beta_w, g_w, g_b, qnorm_w, knorm_w):
        import jax, jax.numpy as jnp
        import numpy as np
        EPS_NORM = 1e-12
        RMS_EPS = 1e-05

        def _rmsnorm(x, w):
            var = jnp.mean(jnp.square(x), axis=-1, keepdims=True)
            return x * jax.lax.rsqrt(var + RMS_EPS) * w

        def _path_attention(x, Wq, Wk, Wv, Wo, wA, wB, conv_w, beta_w, g_w, g_b, qnorm_w, knorm_w):
            B, T, D = x.shape
            d = qnorm_w.shape[0]
            H = D // d
            scale = d ** (-0.5)
            q = (x @ Wq).reshape(B, T, H, d)
            k = (x @ Wk).reshape(B, T, H, d)
            v = (x @ Wv).reshape(B, T, H, d)
            w = x @ wA @ wB
            wp = jnp.pad(w, ((0, 0), (2, 0), (0, 0)))
            w = wp[:, 0:T] * conv_w[:, 0] + wp[:, 1:T + 1] * conv_w[:, 1] + wp[:, 2:T + 2] * conv_w[:, 2]
            w = jax.nn.silu(w).reshape(B, T, H, d)
            w = w * jax.lax.rsqrt(jnp.sum(jnp.square(w), -1, keepdims=True) + EPS_NORM)
            beta = 2.0 * jax.nn.sigmoid(x @ beta_w)
            g = jax.nn.log_sigmoid(x @ g_w + g_b)
            q = _rmsnorm(q, qnorm_w)
            k = _rmsnorm(k, knorm_w)
            q, k, v, w = (t.transpose(0, 2, 1, 3) for t in (q, k, v, w))
            beta = beta.transpose(0, 2, 1)
            g = g.transpose(0, 2, 1)
            tri_s = jnp.tril(jnp.ones((T, T), bool), -1)
            C = jnp.einsum('bhtd,bhsd->bhts', w, w) * beta[:, :, None, :]
            L = jnp.where(tri_s, C, 0.0) + jnp.eye(T, dtype=x.dtype)
            Rhs = jnp.where(tri_s, jnp.einsum('bhtd,bhjd->bhtj', w, k), 0.0)
            A = jax.scipy.linalg.solve_triangular(L, Rhs, lower=True, unit_diagonal=True)
            tri = jnp.tril(jnp.ones((T, T), bool))
            qw = jnp.where(tri, jnp.einsum('bhid,bhtd->bhit', q, w), 0.0)
            S = jnp.einsum('bhid,bhjd->bhij', q, k) - jnp.einsum('bhit,bhtj->bhij', qw, beta[..., None] * A)
            G = jnp.cumsum(g, axis=-1)
            logits = S * scale + (G[..., :, None] - G[..., None, :])
            logits = jnp.where(tri, logits, -1e+30)
            P = jax.nn.softmax(logits, axis=-1)
            o = jnp.einsum('bhij,bhjd->bhid', P, v)
            return o.transpose(0, 2, 1, 3).reshape(B, T, D) @ Wo
        return _path_attention(x, Wq, Wk, Wv, Wo, wA, wB, conv_w, beta_w, g_w, g_b, qnorm_w, knorm_w)

    def _L0_ffn_ref(x, Wg, routing_bias, W1, W2, W3, Ws1, Ws2, Ws3):
        import jax, jax.numpy as jnp
        import numpy as np
        E, K = (8, 4)
        B, S, D = (4, 256, 256)
        H = D * 2 * 4 // 3

        def _swiglu(u, w1, w2, w3):
            h = jnp.einsum('...d,hd->...h', u, w1)
            v = jnp.einsum('...d,hd->...h', u, w2)
            return jnp.einsum('...h,dh->...d', jax.nn.sigmoid(h) * h * v, w3)
        gate = jnp.einsum('bsd,ed->bse', x, Wg) + routing_bias
        _, top_idx = jax.lax.top_k(gate, K)
        mask = jax.nn.one_hot(top_idx, E, dtype=gate.dtype).sum(-2)
        masked_gate = jnp.where(mask > 0, gate, -jnp.inf)
        probs = jax.nn.softmax(masked_gate, axis=-1)
        weights = probs * mask
        out = _swiglu(x, Ws1, Ws2, Ws3)
        h1 = jnp.einsum('bsd,ehd->ebsh', x, W1)
        h2 = jnp.einsum('bsd,ehd->ebsh', x, W2)
        eo = jnp.einsum('ebsh,edh->ebsd', jax.nn.sigmoid(h1) * h1 * h2, W3)
        out = out + jnp.einsum('ebsd,bse->bsd', eo, weights)
        return out
    h = _L0_tok_ref(x, L0_tok_emb0, L0_tok_emb1, L0_tok_emb2, L0_tok_emb3, L0_tok_proj0, L0_tok_proj1, L0_tok_proj2, L0_tok_proj3)
    h = h + _L0_attn_ref(_layernorm(h, axis=-1), L0_attn_Wq, L0_attn_Wk, L0_attn_Wv, L0_attn_Wo, L0_attn_wA, L0_attn_wB, L0_attn_conv_w, L0_attn_beta_w, L0_attn_g_w, L0_attn_g_b, L0_attn_qnorm_w, L0_attn_knorm_w)
    h = h + _L0_ffn_ref(_layernorm(h, axis=-1), L0_ffn_Wg, L0_ffn_routing_bias, L0_ffn_W1, L0_ffn_W2, L0_ffn_W3, L0_ffn_Ws1, L0_ffn_Ws2, L0_ffn_Ws3)
    return h

_drawn_inputs = setup_inputs


def setup_inputs(seed=0):
    import zlib

    import numpy as np

    out = dict(_drawn_inputs(seed))
    spreads = {'L0_attn_g_b': (0.0, 0.8),
     'L0_attn_qnorm_w': (1.0, 0.6),
     'L0_attn_knorm_w': (1.0, 0.6),
     'L0_ffn_routing_bias': (0.0, 0.8)}
    factors = {'L0_attn_wA': 6.198,
     'L0_attn_wB': 6.002,
     'L0_attn_conv_w': 6.088,
     'L0_attn_beta_w': 23.082,
     'L0_attn_g_w': 8.0,
     'L0_ffn_Wg': 5.163,
     'L0_ffn_W1': 3.889,
     'L0_ffn_W2': 3.852,
     'L0_ffn_W3': 3.881,
     'L0_ffn_Ws1': 3.284,
     'L0_ffn_Ws2': 3.241,
     'L0_ffn_Ws3': 3.28}
    for name, (base, spread) in spreads.items():
        noise = np.random.default_rng([zlib.crc32(name.encode()), seed]).standard_normal(out[name].shape)
        drawn = base * np.exp(spread * noise) if base else spread * noise
        out[name] = jnp.asarray(drawn.astype(out[name].dtype))
    for name, factor in factors.items():
        out[name] = (out[name] * factor).astype(out[name].dtype)
    return out
```

```python
from contextlib import ExitStack

import concourse.bass as bass
from concourse import mybir

P = 128
F32 = mybir.dt.float32
BF16 = mybir.dt.bfloat16
I32 = mybir.dt.int32
U32 = mybir.dt.uint32
ALU = mybir.AluOpType
ACT = mybir.ActivationFunctionType
X = mybir.AxisListType.X
DS = bass.ds

B, T, D = 16, 256, 256
H, DH = 16, 16
HP = 32
NT = B * T // P
NA = T // P
KC = D // P
NG, HG = 4, 4
CH = 32
NCH = B * T // CH
ENDS = (0, 5000, 10000, 50000, 267735)
EW = (256, 64, 16, 4)
EO = (0, 256, 320, 336)
EC = sum(EW)
EB = EC - 2 * P
TM = 2 * D + H
E1, HF, HT, NHT = 9, 682, 114, 6
NE, TOPK = 8, 4


class Signal:

    def __init__(self, nc, ctx, name, per, first=1):
        self.sem = ctx.enter_context(nc.semaphore(name))
        self.per, self.first = per, first

    def at(self, it, k):
        return it * self.per + (k + self.first)

    def count(self, n):
        return n + self.first


def start(eng, signals):
    for signal in signals:
        eng.sem_inc(signal.sem, 1)


def wait(eng, it, signal, k):
    eng.wait_ge(signal.sem, signal.at(it, k))


def wait_apart(eng, it, signal, k, passed):
    eng.wait_ge(signal.sem, signal.at(it, k))
    eng.sem_inc(passed.sem, 1)


def sbufs(nc, ctx):
    return lambda name, shape, dt=F32: ctx.enter_context(nc.sbuf_tensor(name, shape, dt))


def psums(nc, ctx):
    return lambda name, shape, dt=F32: ctx.enter_context(nc.psum_tensor(name, shape, dt))


def embed_and_project(nc, sems, ids, emb, projT, wkq, wvbg, wA, wB, conv, gb, norms_w, h_d, F_d, tm_d):
    with ExitStack() as ctx:
        sb, ps = sbufs(nc, ctx), psums(nc, ctx)

        signals = []

        def sig(name, per=1):
            signals.append(Signal(nc, sems, name, per))
            return signals[-1]

        ids_i = sb("ids_i", [P, NT], I32)
        idx_all = sb("idx_all", [P, NT, 4], I32)
        msk_all = sb("msk_all", [P, NT, 4])
        idx = sb("idx", [P, NA, 4], I32)
        msk = sb("msk", [P, NA, 4])
        lt = sb("lt", [P, NT])
        ident = sb("ident", [P, P])
        upto = sb("upto", [P, P])
        ones = sb("ones", [P, P])
        projT_s = sb("projT_s", [P, 3, D])
        wkq_s = sb("wkq_s", [P, KC, 2 * D])
        wvbg_s = sb("wvbg_s", [P, KC, D + 2 * H])
        wA_s = sb("wA_s", [P, KC, 32])
        wB_s = sb("wB_s", [32, D])
        conv_s = sb("conv_s", [P, KC, 3])
        gb_s = sb("gb_s", [P, H])
        norms_s = sb("norms_s", [P, 2, DH])
        norms = sb("norms", [P, 2, DH])
        zero = sb("zero", [P, 1])
        step, pstep = sb("step", [P, 1]), sb("pstep", [P, 1])
        E = sb("E", [P, NA, EC])
        Em = sb("Em", [P, NA, EC])
        ET = sb("ET", [P, NA, 3 * P])
        hs = sb("hs", [P, NA, D])
        st = sb("st", [P, NA, 6])
        mv = sb("mv", [P, NA, 2])
        ve = sb("ve", [P, NA])
        lnv = sb("lnv", [P, NA])
        rstd = sb("rstd", [P, NA])
        xn = sb("xn", [P, NA, D])
        xT = sb("xT", [P, KC, T])
        xAT = sb("xAT", [32, T])
        wpad = sb("wpad", [P, KC, 2 + T])
        cv = sb("cv", [P, 3, KC, T])
        ex = sb("ex", [P, KC, T])
        ex1 = sb("ex1", [P, KC, T])
        sg = sb("sg", [P, KC, T])
        ws = sb("ws", [P, KC, T])
        sq = sb("sq", [P, NA, 3 * D])
        ss = sb("ss", [P, NA, 3 * H])
        sse = sb("sse", [P, NA, 3 * H])
        lns = sb("lns", [P, NA, 3 * H])
        rs = sb("rs", [P, NA, 3 * H])
        qkt = sb("qkt", [P, NA, 2 * D])
        bgt = sb("bgt", [P, NA, 8, H])
        Ft = sb("Ft", [P, NA, 3, H, HP])
        FT = sb("FT", [P, NG, NA, 3, P])
        tm = sb("tm", [P, NA, TM])

        pE = ps("pE", [P, NA, 512])
        pH = ps("pH", [P, NA, D])
        pX = ps("pX", [P, KC, T])
        pA = ps("pA", [P, 512])
        pV = ps("pV", [P, NA, 512])
        pF = ps("pF", [P, 512])

        g = sig
        loaded, consts = g("p1_loaded"), g("p1_consts")
        ids_ready, idx_ready = g("p1_ids_ready"), g("p1_idx", 2)
        gathered = Signal(nc, sems, "p1_gathered", 16 * 4 * NA, first=0)
        masked, et_p, et, h_p, h_s = g("p1_masked", 4), g("p1_et_p"), g("p1_et", 2), g("p1_h_p"), g("p1_h_s")
        h_out, mean, ln_r, normed = g("p1_h_out", 16), g("p1_mean", 5), g("p1_ln_r", 2), g("p1_normed", 2)
        xt_p, xt, xa_p, xa, w_p, w_s = g("p1_xt_p"), g("p1_xt"), g("p1_xa_p"), g("p1_xa"), g("p1_w_p"), g("p1_w_s")
        qk_p, v_p, conved, wexp, silu = g("p1_qk_p"), g("p1_v_p"), g("p1_conved", 6), g("p1_wexp"), g("p1_silu", 3)
        wt_p, squared, sums, logs, scaled = g("p1_wt_p"), g("p1_squared", 2), g("p1_sums", 3), g("p1_logs", 2), g("p1_scaled", 6)
        gates, gexp, gsum, heads, v_s = g("p1_gates", 8), g("p1_gexp", 4), g("p1_gsum"), g("p1_heads", 4), g("p1_v_s")
        f_p, f_even, f_odd, f_out, tm_out = g("p1_f_p", 6), g("p1_f_even", 3), g("p1_f_odd", 3), g("p1_f_out", 16), g("p1_tm_out", 16)

        block = ctx.enter_context(nc.Block())

        @block.sync
        def _(sp):
            n = 0
            for dst, src in ((ids_i[:], ids), (projT_s[:, 0:2, :], projT[0:2 * P, :].rearrange("(c p) n -> p c n", p=P)),
                             (projT_s[0:EB, 2, :], projT[2 * P:EC, :]),
                             (wkq_s[:], wkq.rearrange("(c p) n -> p c n", p=P)),
                             (wvbg_s[:], wvbg.rearrange("(c p) n -> p c n", p=P)),
                             (wA_s[:], wA.rearrange("(c p) n -> p c n", p=P)), (wB_s[:], wB),
                             (conv_s[:], conv.rearrange("(c p) n -> p c n", p=P)),
                             (gb_s[:], gb.partition_broadcast(P)), (norms_s[:], norms_w.partition_broadcast(P))):
                sp.dma_start(dst, src).then_inc(loaded.sem, 16)
            with sp.Fori(0, B) as it:
                wait(sp, it, h_s, 1)
                sp.dma_start(h_d[DS(it, 1)].rearrange("o (a p) n -> p (o a) n", p=P), hs[:]).then_inc(h_out.sem, 16)
                wait(sp, it, heads, 4)
                wait(sp, it, scaled, 6)
                wait(sp, it, gates, 8)
                wait(sp, it, v_s, 1)
                sp.dma_start(tm_d[DS(it, 1)].rearrange("o (a p) n -> p (o a) n", p=P), tm[:]).then_inc(tm_out.sem, 16)
                wait(sp, it, f_even, 3)
                wait(sp, it, f_odd, 3)
                sp.dma_start(F_d[DS(it, 1)].rearrange("o p n -> p (o n)"), FT[:].rearrange("p g a m t -> p (g a m t)")).then_inc(f_out.sem, 16)
            sp.wait_ge(h_out.sem, h_out.count(16 * B))
            sp.wait_ge(tm_out.sem, tm_out.count(16 * B))
            sp.wait_ge(f_out.sem, f_out.count(16 * B))

        @block.gpsimd
        def _(pool):
            start(pool, signals)
            pool.memset(zero[:], 0.0).then_inc(consts.sem, 1)
            pool.memset(ident[:], 0.0).then_inc(consts.sem, 1)
            pool.memset(ones[:], 1.0).then_inc(consts.sem, 1)
            pool.memset(wpad[:], 0.0).then_inc(consts.sem, 1)
            pool.memset(Ft[:], 0.0).then_inc(consts.sem, 1)
            pool.wait_ge(consts.sem, consts.count(5))
            pool.memset(Ft[:, :, 1, :, DH + 1:DH + 2], 1.0).then_inc(consts.sem, 1)
            pool.memset(Ft[:, :, 0, :, DH:DH + 1], 1.0).then_inc(consts.sem, 1)
            pool.affine_select(out=ident[:], in_=ident[:], compare_op=ALU.not_equal, fill=1.0, base=0,
                               pattern=[[-1, P]], channel_multiplier=1).then_inc(consts.sem, 1)
            pool.affine_select(out=upto[:], in_=ones[:], compare_op=ALU.is_ge, fill=0.0, base=0,
                               pattern=[[1, P]], channel_multiplier=-1).then_inc(consts.sem, 1)
            pool.wait_ge(consts.sem, consts.count(9))
            with pool.Fori(0, B) as it:
                wait(pool, it, idx_ready, 2)
                wait(pool, it, masked, 0)
                pool.tensor_tensor(out=pstep[:], in0=zero[:], in1=zero[:], op=ALU.add)
                for a in range(NA):
                    for i in range(4):
                        pool.indirect_dma_start(
                            out=E[:, a, EO[i]:EO[i] + EW[i]], out_offset=None, in_=emb[i],
                            in_offset=bass.IndirectOffsetOnAxis(ap=idx[:, a, i:i + 1], axis=0),
                        ).then_inc(gathered.sem, 16)
                wait(pool, it, scaled, 6)
                wait(pool, it, f_p, 0)
                for a in range(NA):
                    for m in range(2):
                        pool.tensor_tensor(
                            out=Ft[:, a, m, :, 0:DH],
                            in0=qkt[:, a, m * D:(m + 1) * D].rearrange("p (h d) -> p h d", d=DH),
                            in1=norms[:, m:m + 1, :].broadcast_to([P, H, DH]), op=ALU.mult).then_inc(heads.sem, 1)

        @block.vector
        def _(dve):
            dve.wait_ge(loaded.sem, loaded.count(160))
            n = 0
            for i in range(4):
                lo, hi = ENDS[i], ENDS[i + 1]
                dve.tensor_scalar(lt[:], ids_i[:], float(-lo), 0.0, ALU.add, ALU.max).then_inc(ids_ready.sem, 1)
                dve.wait_ge(ids_ready.sem, ids_ready.count(4 * i + 1))
                dve.tensor_scalar(idx_all[:, :, i], lt[:], float(hi - lo - 1), None, ALU.min).then_inc(ids_ready.sem, 1)
                dve.wait_ge(ids_ready.sem, ids_ready.count(4 * i + 2))
                dve.tensor_scalar(lt[:], ids_i[:], float(lo), None, ALU.is_ge).then_inc(ids_ready.sem, 1)
                dve.wait_ge(ids_ready.sem, ids_ready.count(4 * i + 3))
                dve.scalar_tensor_tensor(out=msk_all[:, :, i], in0=ids_i[:], scalar=float(hi), in1=lt[:],
                                         op0=ALU.is_lt, op1=ALU.mult).then_inc(ids_ready.sem, 1)
                dve.wait_ge(ids_ready.sem, ids_ready.count(4 * i + 4))
            dve.tensor_scalar(norms[:, 1, :], norms_s[:, 1, :], DH ** -0.5, None, ALU.mult).then_inc(ids_ready.sem, 1)
            dve.tensor_copy(norms[:, 0, :], norms_s[:, 0, :]).then_inc(ids_ready.sem, 1)
            dve.wait_ge(ids_ready.sem, ids_ready.count(18))
            dve.wait_ge(consts.sem, consts.count(9))
            with dve.Fori(0, B) as it:
                dve.tensor_copy(idx[:], idx_all[:, DS(it * NA, NA), :]).then_inc(idx_ready.sem, 1)
                dve.tensor_copy(msk[:], msk_all[:, DS(it * NA, NA), :]).then_inc(idx_ready.sem, 1)
                wait(dve, it, gathered, 16 * 4 * NA)
                wait(dve, it, idx_ready, 2)
                wait(dve, it, et_p, 0)
                for i in range(4):
                    dve.tensor_tensor(Em[:, :, EO[i]:EO[i] + EW[i]], E[:, :, EO[i]:EO[i] + EW[i]],
                                      msk[:, :, i:i + 1].broadcast_to([P, NA, EW[i]]), ALU.mult).then_inc(masked.sem, 1)
                wait(dve, it, h_s, 1)
                for a in range(NA):
                    dve.bn_stats(st[:, a, :], hs[:, a, :]).then_inc(mean.sem, 1)
                wait(dve, it, mean, NA)
                dve.tensor_copy(step[:], zero[:])
                for a in range(NA):
                    dve.bn_aggr(mv[:, a, :], st[:, a, :]).then_inc(mean.sem, 1)
                wait(dve, it, mean, 2 * NA)
                dve.tensor_scalar(ve[:], mv[:, :, 1], 1e-5, None, ALU.add).then_inc(mean.sem, 1)
                wait(dve, it, ln_r, 2)
                wait(dve, it, xt_p, 0)
                for a in range(NA):
                    dve.tensor_scalar(xn[:, a, :], hs[:, a, :], mv[:, a, 0:1], rstd[:, a:a + 1],
                                      ALU.subtract, ALU.mult).then_inc(normed.sem, 1)
                wait(dve, it, v_p, 1)
                dve.tensor_copy(bgt[:, :, 0, :], pV[:, :, D:D + H]).then_inc(gates.sem, 1)
                dve.tensor_tensor(bgt[:, :, 1, :], pV[:, :, D + H:D + 2 * H],
                                  gb_s[:, None, :].broadcast_to([P, NA, H]), ALU.add).then_inc(gates.sem, 1)
                wait(dve, it, gexp, 3)
                dve.tensor_scalar(bgt[:, :, 4, :], bgt[:, :, 3, :], 1.0, None, ALU.add).then_inc(gates.sem, 1)
                wait(dve, it, gates, 3)
                dve.reciprocal(bgt[:, :, 5, :], bgt[:, :, 4, :]).then_inc(gates.sem, 1)
                wait(dve, it, gates, 4)
                wait(dve, it, tm_out, 0)
                dve.tensor_scalar(tm[:, :, 2 * D:TM], bgt[:, :, 5, :], 2.0, None, ALU.mult).then_inc(gates.sem, 1)
                wait(dve, it, gexp, 4)
                wait(dve, it, gsum, 0)
                dve.scalar_tensor_tensor(out=bgt[:, :, 7, :], in0=bgt[:, :, 1, :], scalar=0.0, in1=bgt[:, :, 6, :],
                                         op0=ALU.min, op1=ALU.subtract).then_inc(gates.sem, 1)
                wait(dve, it, w_s, 1)
                for c in range(KC):
                    dve.tensor_scalar(cv[:, 0, c, :], wpad[:, c, 0:T], conv_s[:, c, 0:1], None, ALU.mult).then_inc(conved.sem, 1)
                for k in (1, 2):
                    wait(dve, it, conved, 2 * k)
                    for c in range(KC):
                        dve.scalar_tensor_tensor(out=cv[:, k, c, :], in0=wpad[:, c, k:k + T], scalar=conv_s[:, c, k:k + 1],
                                                 in1=cv[:, k - 1, c, :], op0=ALU.mult, op1=ALU.add).then_inc(conved.sem, 1)
                wait(dve, it, wexp, 1)
                dve.tensor_scalar(ex1[:], ex[:], 1.0, None, ALU.add).then_inc(silu.sem, 1)
                wait(dve, it, silu, 1)
                dve.reciprocal(sg[:], ex1[:]).then_inc(silu.sem, 1)
                wait(dve, it, silu, 2)
                wait(dve, it, wt_p, 0)
                dve.tensor_tensor(ws[:], cv[:, 2, :, :], sg[:], ALU.mult).then_inc(silu.sem, 1)
                wait(dve, it, squared, 2)
                dve.reduce_sum(ss[:].rearrange("p a h -> p (a h)"), sq[:].rearrange("p a (h d) -> p (a h) d", d=DH), X).then_inc(sums.sem, 1)
                wait(dve, it, sums, 1)
                dve.tensor_scalar(sse[:, :, 0:2 * H], ss[:, :, 0:2 * H], 1.0 / DH, 1e-5, ALU.mult, ALU.add).then_inc(sums.sem, 1)
                dve.tensor_scalar(sse[:, :, 2 * H:3 * H], ss[:, :, 2 * H:3 * H], 1e-12, None, ALU.add).then_inc(sums.sem, 1)
                wait(dve, it, logs, 2)
                wait(dve, it, heads, 0)
                for a in range(NA):
                    dve.tensor_tensor(qkt[:, a, :].rearrange("p (h d) -> p h d", d=DH),
                                      pE[:, a, :].rearrange("p (h d) -> p h d", d=DH),
                                      rs[:, a, 0:2 * H].unsqueeze(2).broadcast_to([P, 2 * H, DH]), ALU.mult).then_inc(scaled.sem, 1)
                wait(dve, it, f_p, 0)
                for a in range(NA):
                    wrow = pF[:, a * D:(a + 1) * D].rearrange("p (h d) -> p h d", d=DH)
                    wrs = rs[:, a, 2 * H:3 * H].unsqueeze(2).broadcast_to([P, H, DH])
                    dve.tensor_tensor(Ft[:, a, 2, :, 0:DH], wrow, wrs, ALU.mult).then_inc(scaled.sem, 1)
                    dve.tensor_tensor(tm[:, a, 0:D].rearrange("p (h d) -> p h d", d=DH), wrow, wrs, ALU.mult).then_inc(scaled.sem, 1)
                wait(dve, it, gsum, 1)
                G = pA[:, 256:256 + NA * H].rearrange("p (a h) -> p a h", h=H)
                dve.tensor_copy(Ft[:, :, 1, :, DH], G).then_inc(gates.sem, 1)
                dve.tensor_scalar(Ft[:, :, 0, :, DH + 1], G, -1.0, None, ALU.mult).then_inc(gates.sem, 1)
                for n in (0, 2, 4):
                    wait(dve, it, f_p, n + 1)
                    wait(dve, it, f_out, 0)
                    dve.tensor_copy(FT[:].rearrange("p g a m t -> p (g a m t)")[:, 512 * n:512 * (n + 1)], pF[:]).then_inc(f_even.sem, 1)
                    

        @block.scalar
        def _(act):
            act.wait_ge(consts.sem, consts.count(9))
            with act.Fori(0, B) as it:
                wait(act, it, et_p, 1)
                wait(act, it, h_p, 0)
                act.activation(ET[:, :, 0:2 * P], pE[:, :, 0:2 * P], ACT.Copy).then_inc(et.sem, 1)
                act.activation(ET[0:EB, :, 2 * P:3 * P], pE[0:EB, :, 2 * P:3 * P], ACT.Copy).then_inc(et.sem, 1)
                wait(act, it, h_p, 1)
                wait(act, it, h_out, 0)
                wait(act, it, normed, 0)
                act.activation(hs[:], pH[:], ACT.Copy, scale=float(D) ** 0.5).then_inc(h_s.sem, 1)
                wait(act, it, mean, 5)
                act.activation(lnv[:], ve[:], ACT.Ln).then_inc(ln_r.sem, 1)
                wait(act, it, ln_r, 1)
                act.activation(rstd[:], lnv[:], ACT.Exp, scale=-0.5).then_inc(ln_r.sem, 1)
                wait(act, it, xt_p, 1)
                wait(act, it, v_p, 0)
                act.activation(xT[:], pX[:], ACT.Copy).then_inc(xt.sem, 1)
                wait(act, it, xa_p, 1)
                act.activation(xAT[:], pA[0:32, 0:T], ACT.Copy).then_inc(xa.sem, 1)
                wait(act, it, w_p, 1)
                wait(act, it, conved, 0)
                act.activation(wpad[:, :, 2:2 + T], pX[:], ACT.Copy).then_inc(w_s.sem, 1)
                wait(act, it, gates, 2)
                act.activation(bgt[:, :, 2, :], bgt[:, :, 1, :], ACT.Abs).then_inc(gexp.sem, 1)
                act.activation(bgt[:, :, 3, :], bgt[:, :, 0, :], ACT.Exp, scale=-1.0).then_inc(gexp.sem, 1)
                wait(act, it, gexp, 1)
                act.activation(bgt[:, :, 5 + 1, :], bgt[:, :, 2, :], ACT.Exp, scale=-1.0).then_inc(gexp.sem, 1)
                wait(act, it, gexp, 3)
                act.activation(bgt[:, :, 6, :], bgt[:, :, 6, :], ACT.Ln, bias=1.0).then_inc(gexp.sem, 1)
                wait(act, it, conved, 6)
                act.activation(ex[:], cv[:, 2, :, :], ACT.Exp, scale=-1.0).then_inc(wexp.sem, 1)
                wait(act, it, tm_out, 0)
                act.activation(tm[:, :, D:2 * D], pV[:, :, 0:D], ACT.Copy).then_inc(v_s.sem, 1)
                wait(act, it, qk_p, 1)
                wait(act, it, sums, 0)
                act.activation(sq[:, :, 0:2 * D], pE[:], ACT.Square).then_inc(squared.sem, 1)
                wait(act, it, wt_p, 1)
                act.activation(sq[:, :, 2 * D:3 * D], pF[:].rearrange("p (a n) -> p a n", a=NA), ACT.Square).then_inc(squared.sem, 1)
                wait(act, it, sums, 3)
                act.activation(lns[:], sse[:], ACT.Ln).then_inc(logs.sem, 1)
                wait(act, it, logs, 1)
                act.activation(rs[:], lns[:], ACT.Exp, scale=-0.5).then_inc(logs.sem, 1)
                for n in (1, 3, 5):
                    wait(act, it, f_p, n + 1)
                    wait(act, it, f_out, 0)
                    act.activation(FT[:].rearrange("p g a m t -> p (g a m t)")[:, 512 * n:512 * (n + 1)], pV[:, 0, :], ACT.Copy).then_inc(f_odd.sem, 1)

        @block.tensor
        def _(pe):
            pe.wait_ge(consts.sem, consts.count(9))
            pe.wait_ge(loaded.sem, loaded.count(160))
            mm = nc.tensor.matmul
            with pe.Fori(0, B) as it:
                wait(pe, it, masked, 4)
                wait(pe, it, scaled, 0)
                for a in range(NA):
                    for c in range(3):
                        w = P if c < 2 else EB
                        last = pe.transpose(pE[0:w, a, c * P:(c + 1) * P], Em[:, a, c * P:c * P + w], ident[:])
                last.then_inc(et_p.sem, 1)
                wait(pe, it, et, 2)
                wait(pe, it, h_s, 0)
                for a in range(NA):
                    for c in range(3):
                        w = P if c < 2 else EB
                        last = mm(pH[:, a, :], ET[0:w, a, c * P:(c + 1) * P], projT_s[0:w, c, :], start=(c == 0), stop=(c == 2))
                last.then_inc(h_p.sem, 1)
                wait(pe, it, normed, 2)
                wait(pe, it, w_s, 0)
                for c in range(KC):
                    for a in range(NA):
                        last = pe.transpose(pX[:, c, a * P:(a + 1) * P], xn[:, a, c * P:(c + 1) * P], ident[:])
                last.then_inc(xt_p.sem, 1)
                wait(pe, it, xt, 1)
                wait(pe, it, gates, 0)
                for c in range(KC):
                    last = mm(pA[0:32, 0:T], wA_s[:, c, :], xT[:, c, :], start=(c == 0), stop=(c == KC - 1))
                last.then_inc(xa_p.sem, 1)
                for a in range(NA):
                    for c in range(KC):
                        last = mm(pE[:, a, :], xT[:, c, a * P:(a + 1) * P], wkq_s[:, c, :], start=(c == 0), stop=(c == KC - 1))
                last.then_inc(qk_p.sem, 1)
                wait(pe, it, f_odd, 0)
                for a in range(NA):
                    for c in range(KC):
                        last = mm(pV[:, a, 0:D + 2 * H], xT[:, c, a * P:(a + 1) * P], wvbg_s[:, c, :], start=(c == 0), stop=(c == KC - 1))
                last.then_inc(v_p.sem, 1)
                wait(pe, it, xa, 1)
                for c in range(KC):
                    last = mm(pX[:, c, :], wB_s[:, c * P:(c + 1) * P], xAT[:], start=True, stop=True)
                last.then_inc(w_p.sem, 1)
                wait(pe, it, silu, 3)
                wait(pe, it, f_even, 0)
                for a in range(NA):
                    for c in range(KC):
                        last = pe.transpose(pF[:, a * D + c * P:a * D + (c + 1) * P], ws[:, c, a * P:(a + 1) * P], ident[:])
                last.then_inc(wt_p.sem, 1)
                wait(pe, it, gates, 6)
                mm(pA[:, 256:256 + H], upto[:], bgt[:, 0, 7, :], start=True, stop=True)
                mm(pA[:, 256 + H:256 + 2 * H], ones[:], bgt[:, 0, 7, :], start=True, stop=False)
                mm(pA[:, 256 + H:256 + 2 * H], upto[:], bgt[:, 1, 7, :], start=False, stop=True).then_inc(gsum.sem, 1)
                wait(pe, it, heads, 4)
                wait(pe, it, scaled, 6)
                wait(pe, it, gates, 8)
                wait(pe, it, v_s, 1)
                for n in range(6):
                    dst = pF[:] if n % 2 == 0 else pV[:, 0, :]
                    if n >= 2:
                        wait(pe, it, f_even if n % 2 == 0 else f_odd, n // 2)
                    for j in range(4):
                        r = 4 * n + j
                        gg, a, m = r // 6, r % 6 // 3, r % 3
                        last = pe.transpose(dst[:, j * P:(j + 1) * P],
                                            Ft[:, a, m, 4 * gg:4 * gg + 4, :].rearrange("p h d -> p (h d)"), ident[:])
                    last.then_inc(f_p.sem, 1)


def invert_chunks(nc, sems, tm_d, xt_d, bx_d):
    G2 = 8
    with ExitStack() as ctx:
        sb = sbufs(nc, ctx)
        w = sb("lane_w", [P, CH, D])
        nbw = sb("lane_nbw", [P, CH, D])
        bt = sb("lane_beta", [P, CH, H])
        L = sb("lane_L", [P, G2, CH, CH])
        Xt = sb("lane_Xt", [P, G2, CH, CH])
        bX = sb("lane_bX", [P, G2, CH, CH])
        tmp = sb("lane_tmp", [P, G2 * (CH - 1) * (CH - 1)])

        signals = []

        def sig(name, per=1):
            signals.append(Signal(nc, sems, name, per))
            return signals[-1]

        loaded, nbw_ready = sig("p2_loaded"), sig("p2_nbw")
        cleared, prod, summed = sig("p2_cleared", 2), sig("p2_prod", 2 * (CH - 1)), sig("p2_summed", 2 * (CH - 1))
        scaled, stored = sig("p2_scaled", 1), sig("p2_stored", 32)
        block = ctx.enter_context(nc.Block())
        rows = tm_d.rearrange("b (c t) n -> (b c) t n", t=CH)

        @block.gpsimd
        def _(pool):
            start(pool, signals)

        @block.sync
        def _(sp):
            sp.dma_start(w[:], rows[:, :, 0:D]).then_inc(loaded.sem, 16)
            sp.dma_start(bt[:], rows[:, :, 2 * D:TM]).then_inc(loaded.sem, 16)
            with sp.Fori(0, H // G2) as it:
                wait(sp, it, scaled, 1)
                sp.dma_start(xt_d[:, DS(it * G2, G2)], Xt[:]).then_inc(stored.sem, 16)
                sp.dma_start(bx_d[:, DS(it * G2, G2)], bX[:]).then_inc(stored.sem, 16)
            sp.wait_ge(stored.sem, stored.count(32 * (H // G2)))

        @block.vector
        def _(dve):
            dve.wait_ge(loaded.sem, loaded.count(32))
            dve.scalar_tensor_tensor(out=nbw[:].rearrange("p t (h d) -> p (t h) d", d=DH),
                                     in0=w[:].rearrange("p t (h d) -> p (t h) d", d=DH), scalar=-1.0,
                                     in1=bt[:].rearrange("p t h -> p (t h)").unsqueeze(2).broadcast_to([P, CH * H, DH]),
                                     op0=ALU.mult, op1=ALU.mult).then_inc(nbw_ready.sem, 1)
            dve.wait_ge(nbw_ready.sem, nbw_ready.count(1))
            with dve.Fori(0, H // G2) as it:
                wh = w[:, :, DS(it * (G2 * DH), G2 * DH)].rearrange("p t (h d) -> p h t d", d=DH)
                nh = nbw[:, :, DS(it * (G2 * DH), G2 * DH)].rearrange("p t (h d) -> p h t d", d=DH)
                wait(dve, it, stored, 0)
                dve.memset(Xt[:], 0.0).then_inc(cleared.sem, 1)
                wait(dve, it, cleared, 1)
                dve.memset(Xt[:].rearrange("p h s t -> p h (s t)")[:, :, ::CH + 1], 1.0).then_inc(cleared.sem, 1)
                wait(dve, it, cleared, 2)
                n = 0
                for t in range(1, CH):
                    pr = tmp[:, 0:G2 * t * DH].rearrange("p (h s d) -> p h s d", h=G2, d=DH)
                    if n:
                        wait(dve, it, summed, n)
                    dve.tensor_tensor(pr, nh[:, :, 0:t, :], wh[:, :, t:t + 1, :].broadcast_to([P, G2, t, DH]),
                                      ALU.mult).then_inc(prod.sem, 1)
                    n += 1
                    wait(dve, it, prod, n)
                    dve.reduce_sum(L[:, :, t, 0:t], pr, X).then_inc(summed.sem, 1)
                for t in range(1, CH):
                    pr = tmp[:, 0:G2 * t * t].rearrange("p (h j s) -> p h j s", h=G2, s=t)
                    wait(dve, it, summed, n)
                    dve.tensor_tensor(pr, Xt[:, :, 0:t, 0:t], L[:, :, t:t + 1, 0:t].broadcast_to([P, G2, t, t]),
                                      ALU.mult).then_inc(prod.sem, 1)
                    n += 1
                    wait(dve, it, prod, n)
                    dve.reduce_sum(Xt[:, :, 0:t, t], pr, X).then_inc(summed.sem, 1)
                wait(dve, it, summed, n)
                bth = bt[:, :, DS(it * G2, G2)].rearrange("p t h -> p h t").unsqueeze(3).broadcast_to([P, G2, CH, CH])
                dve.tensor_tensor(bX[:], Xt[:].rearrange("p h s t -> p h t s"), bth, ALU.mult).then_inc(scaled.sem, 1)


def attend(nc, sems, F_d, tm_d, xt_d, bx_d, h_d, wo, h2_d):
    NS = NG * NA
    W0, R0, Q0, G0, MW = 0, HP, HP + P, HP + 2 * P, HP + 3 * P
    HB = P // 2
    with ExitStack() as ctx:
        sb, ps = sbufs(nc, ctx), psums(nc, ctx)

        signals = []

        def sig(name, per=1):
            signals.append(Signal(nc, sems, "p3_" + name, per))
            return signals[-1]

        Fs = sb("Fs", [P, NG, NA, 3, P])
        XTs = sb("XTs", [P, NA, H, HB])
        BXs = sb("BXs", [P, NA, H, HB])
        tms = sb("tms", [P, NA, TM])
        wt = sb("wt", [P, NA, H, DH])
        va = sb("va", [P, NA, H, DH + 1])
        nbeta = sb("nbeta", [P, NA, H])
        hres = sb("hres", [P, NA, D])
        wo_s = sb("wo_s", [P, KC, D])
        ident3 = sb("ident3", [P, P])
        identb = sb("identb", [P, P], BF16)
        future = sb("future", [P, 2, P], BF16)
        ones3 = sb("ones3", [P, 3, P])
        keep = sb("keep", [P, 3, P])
        Ms = sb("Ms", [P, HG, MW])
        Ys = sb("Ys", [P, 2, 2, HB])
        X64 = sb("X64", [P, 2, 2, HB])
        nb = sb("nb", [P, HG, HP + P])
        hats = sb("hats", [P, 2, P])
        nm = sb("nm", [P, HG])
        Ps = sb("Ps", [P, HG, 2 * P])
        PTs = sb("PTs", [P, HG, 2, P])
        rec = sb("rec", [P, HG])
        Os = sb("Os", [P, NA, D])
        OT = sb("OT", [P, KC, T])
        h2s = sb("h2s", [P, NA, D])

        pG = ps("pG", [P, 2, 512])
        pC = ps("pC", [P, 2, 512])
        pS = ps("pS", [P, 2, 512])
        pT = ps("pT", [P, 2, 512])

        loaded, cleared, consts = sig("loaded"), sig("cleared", 6), sig("consts")
        f_in, x_in, tm_in, h_in = [sig(f"f_in{i}", 16) for i in range(NG)], [sig(f"x_in{i}", 16 * 16) for i in range(NG)], sig("tm_in", 16), sig("h_in", 16)
        copied, w_in, gram, masked = sig("copied", 3), sig("w_in", NS), sig("gram", NS * HG), sig("masked", NS * HG)

        def two(name):
            return [sig(f"{name}{i}", NS) for i in range(2)]

        y_p, y_s, xy_p, x64, top_p, top = two("y_p"), two("y_s"), two("xy_p"), two("x64"), two("top_p"), two("top")
        rhs_p, rhs, low_p, low = two("rhs_p"), two("rhs"), two("low_p"), two("low")
        hat_p, hat, first, score, peak, weight = two("hat_p"), two("hat"), two("first"), two("score"), two("peak"), two("weight")
        wT_p, wT, out_p, inv, outs = two("wT_p"), two("wT"), two("out_p"), two("inv"), two("outs")
        oT_p, oT, y_out, h2, h2_out = sig("oT_p"), sig("oT"), sig("y_out"), sig("h2"), sig("h2_out", 16)
        pe_passed, pool_passed = sig("pe_passed"), sig("pool_passed")

        block = ctx.enter_context(nc.Block())

        def load_group(sp, it, g):
            sp.dma_start(Fs[:, g].rearrange("p a m t -> p (a m t)"),
                         F_d[DS(it, 1), :, g * NA * 3 * P:(g + 1) * NA * 3 * P].rearrange("o p n -> p (o n)")).then_inc(f_in[g].sem, 16)
            for dst, src in ((XTs, xt_d), (BXs, bx_d)):
                chunks = src[DS(it * (T // CH), T // CH)].rearrange("c h s t -> c s h t")
                for n in range(T // CH):
                    a, c = divmod(n, P // CH)
                    sp.dma_start(dst[CH * c:CH * (c + 1), a, HG * g:HG * (g + 1), CH * (c % 2):CH * (c % 2 + 1)],
                                 chunks[n, :, HG * g:HG * (g + 1), :]).then_inc(x_in[g].sem, 16)

        def rows_of(x, it):
            return x[DS(it, 1)].rearrange("o (a p) n -> p (o a) n", p=P)

        @block.sync
        def _(sp):
            sp.dma_start(wo_s[:], wo.rearrange("(c p) n -> p c n", p=P)).then_inc(loaded.sem, 16)
            sp.dma_start(tms[:], rows_of(tm_d, 0)).then_inc(tm_in.sem, 16)
            sp.dma_start(hres[:], rows_of(h_d, 0)).then_inc(h_in.sem, 16)
            sp.wait_ge(cleared.sem, cleared.count(6))
            for g in range(NG):
                load_group(sp, 0, g)
            with sp.Fori(0, B - 1) as it:
                wait(sp, it, copied, 3)
                wait(sp, it, w_in, 1)
                sp.dma_start(tms[:], rows_of(tm_d, it + 1)).then_inc(tm_in.sem, 16)
                for g in range(NG):
                    wait(sp, it, score[0], NA * (g + 1))
                    wait(sp, it, score[1], NA * (g + 1))
                    wait(sp, it, hat[0], NA * (g + 1))
                    wait(sp, it, hat[1], NA * (g + 1))
                    load_group(sp, it + 1, g)
                wait(sp, it, h2, 1)
                sp.dma_start(rows_of(h2_d, it), h2s[:]).then_inc(h2_out.sem, 16)
                sp.dma_start(hres[:], rows_of(h_d, it + 1)).then_inc(h_in.sem, 16)
            sp.wait_ge(h2.sem, h2.count(B))
            sp.dma_start(rows_of(h2_d, B - 1), h2s[:]).then_inc(h2_out.sem, 16)
            sp.wait_ge(h2_out.sem, h2_out.count(16 * B))

        @block.gpsimd
        def _(pool):
            start(pool, signals)
            for x in (XTs, BXs, Ms, nb, ident3):
                pool.memset(x[:], 0.0).then_inc(cleared.sem, 1)
            pool.memset(va[:, :, :, DH:DH + 1], 1.0).then_inc(cleared.sem, 1)
            pool.memset(ones3[:], 1.0).then_inc(consts.sem, 1)
            pool.memset(future[:], 0.0).then_inc(consts.sem, 1)
            pool.wait_ge(cleared.sem, cleared.count(6))
            pool.wait_ge(consts.sem, consts.count(2))
            pool.affine_select(out=ident3[:], in_=ident3[:], compare_op=ALU.not_equal, fill=1.0, base=0,
                               pattern=[[-1, P]], channel_multiplier=1).then_inc(consts.sem, 1)
            pool.affine_select(out=keep[:, 0, :], in_=ones3[:, 0, :], compare_op=ALU.is_gt, fill=0.0, base=0,
                               pattern=[[-1, P]], channel_multiplier=1).then_inc(consts.sem, 1)
            pool.affine_select(out=keep[:, 1, :], in_=ones3[:, 1, :], compare_op=ALU.is_ge, fill=0.0, base=0,
                               pattern=[[1, P]], channel_multiplier=-1).then_inc(consts.sem, 1)
            pool.affine_select(out=keep[:, 2, :].rearrange("p (c t) -> p c t", t=CH), in_=ones3[:, 2, :].rearrange("p (c t) -> p c t", t=CH),
                               compare_op=ALU.is_gt, fill=0.0, base=0, pattern=[[CH, P // CH], [0, CH]], channel_multiplier=-1).then_inc(consts.sem, 1)
            pool.affine_select(out=future[:], in_=future[:], compare_op=ALU.is_ge, fill=-1e30, base=0,
                               pattern=[[0, 2], [-1, P]], channel_multiplier=1).then_inc(consts.sem, 1)
            pool.wait_ge(consts.sem, consts.count(7))
            pool.tensor_copy(identb[:], ident3[:]).then_inc(consts.sem, 1)
            pool.wait_ge(consts.sem, consts.count(8))
            with pool.Fori(0, B) as it:
                pool.wait_ge(tm_in.sem, tm_in.count(it * 16 + 16))
                wait(pool, it, out_p[0], 0)
                wait(pool, it, out_p[1], 0)
                wait(pool, it, low[0], 0)
                wait_apart(pool, it, low[1], 0, pool_passed)
                pool.tensor_copy(va[:, :, :, 0:DH], tms[:, :, D:2 * D].rearrange("p a (h d) -> p a h d", d=DH)).then_inc(copied.sem, 1)
                pool.tensor_scalar(nbeta[:], tms[:, :, 2 * D:TM], -1.0, None, ALU.mult).then_inc(copied.sem, 1)
                pool.tensor_copy(wt[:], tms[:, :, 0:D].rearrange("p a (h d) -> p a h d", d=DH)).then_inc(copied.sem, 1)
                for k in range(NS):
                    g, a = divmod(k, NA)
                    if k == 0:
                        wait(pool, it, copied, 3)
                    wait(pool, it, score[0], k)
                    wait(pool, it, score[1], k)
                    pool.tensor_tensor(out=Ms[:, :, W0:W0 + DH], in0=wt[:, a, HG * g:HG * (g + 1), :],
                                       in1=ones3[:, 0, 0:1].unsqueeze(2).broadcast_to([P, HG, DH]), op=ALU.mult).then_inc(w_in.sem, 1)

        def each(f):
            f(0)
            f(1)

        def c0(k):
            return R0 if k % NA == 0 else W0

        @block.tensor
        def _(pe):
            mm = nc.tensor.matmul
            pe.wait_ge(consts.sem, consts.count(8))
            pe.wait_ge(loaded.sem, loaded.count(16))
            with pe.Fori(0, B) as it:
                def grams(k):
                    g, a = divmod(k, NA)
                    if a == 0:
                        pe.wait_ge(f_in[g].sem, f_in[g].count(it * 16 + 16))
                        pe.wait_ge(x_in[g].sem, x_in[g].count(it * 256 + 256))
                    for h in range(HG):
                        wait(pe, it, masked, max(0, HG * k + h - 1))
                        r = slice(HP * h, HP * (h + 1))
                        mm(pG[:, h % 2, 0:3 * P], Fs[r, g, a, 2, :], Fs[r, g, a, :, :].rearrange("p m t -> p (m t)"),
                           start=True, stop=True, tile_position=(HP * h, 0)).then_inc(gram.sem, 1)

                def blocks(pr, f):
                    for hh in range(2):
                        for r in (slice(0, HB), slice(HB, P)):
                            last = f(2 * pr + hh, hh, r)
                    return last

                def y_of(k, pr):
                    g, a = divmod(k, NA)
                    wait(pe, it, masked, HG * k + 2 * pr + 2)
                    wait_apart(pe, it, hat[pr], k, pe_passed)
                    blocks(pr, lambda h, hh, r: mm(pC[r, pr, hh * HB:(hh + 1) * HB], Ms[r, h, G0 + r.start:G0 + r.stop],
                                                   BXs[r, a, HG * g + h, :], start=True, stop=True)).then_inc(y_p[pr].sem, 1)

                def xy_of(k, pr):
                    g, a = divmod(k, NA)
                    wait_apart(pe, it, y_s[pr], k + 1, pe_passed)
                    blocks(pr, lambda h, hh, r: mm(pC[r, pr, hh * HB:(hh + 1) * HB], Ys[r, pr, hh, :],
                                                   XTs[r, a, HG * g + h, :], start=True, stop=True)).then_inc(xy_p[pr].sem, 1)

                def top_of(k, pr):
                    wait(pe, it, x64[pr], k + 1)
                    wait_apart(pe, it, w_in, k + 1, pe_passed)
                    for hh in range(2):
                        last = mm(pC[0:HB, pr, 160 * hh + c0(k):160 * hh + R0 + HB], X64[0:HB, pr, hh, :],
                                  Ms[0:HB, 2 * pr + hh, c0(k):R0 + HB], start=True, stop=True)
                    last.then_inc(top_p[pr].sem, 1)

                def rhs_of(k, pr):
                    wait_apart(pe, it, top[pr], k + 1, pe_passed)
                    for hh in range(2):
                        last = mm(pC[HB:P, pr, 160 * hh + c0(k):160 * hh + R0 + HB], Ms[0:HB, 2 * pr + hh, G0 + HB:G0 + P],
                                  nb[0:HB, 2 * pr + hh, c0(k):R0 + HB], start=True, stop=True)
                    last.then_inc(rhs_p[pr].sem, 1)

                def low_of(k, pr):
                    wait_apart(pe, it, rhs[pr], k + 1, pe_passed)
                    for hh in range(2):
                        last = mm(pC[HB:P, pr, 160 * hh + c0(k):160 * hh + R0 + P], X64[HB:P, pr, hh, :],
                                  Ms[HB:P, 2 * pr + hh, c0(k):R0 + P], start=True, stop=True)
                    last.then_inc(low_p[pr].sem, 1)

                def hat_of(k, pr):
                    wait(pe, it, low[pr], k + 1)
                    for h in (2 * pr, 2 * pr + 1):
                        if k % NA == 0:
                            l, r = Ms[:, h, W0:W0 + HP], nb[:, h, R0:R0 + P]
                        else:
                            l, r = nb[:, h, W0:W0 + HP], Ms[:, h, Q0:Q0 + P]
                        last = mm(pC[HP * h:HP * (h + 1), pr, 0:P], l, r, start=True, stop=True, tile_position=(0, HP * h))
                    last.then_inc(hat_p[pr].sem, 1)

                def score_of(k, hh):
                    g, a = divmod(k, NA)
                    for pr in range(2):
                        h = 2 * pr + hh
                        r = slice(HP * h, HP * (h + 1))
                        sc = pS[:, pr, :].rearrange("p (h j) -> p h j", h=2)
                        if hh == 0:
                            wait(pe, it, weight[pr], k)
                            mm(sc[:, :, P:2 * P], identb[:], future[:], start=True, stop=False)
                        else:
                            wait(pe, it, first[pr], k + 1)
                        mm(sc[:, hh, P:2 * P], Fs[r, g, a, 1, :], Fs[r, g, a, 0, :], start=False, stop=False, tile_position=(HP * h, 0))
                        if a == 1:
                            if hh == 0:
                                wait(pe, it, hat[pr], k + 1)
                            mm(sc[:, hh, 0:P], hats[r, 1, :], hats[r, 0, :], start=False, stop=False, tile_position=(HP * h, 0))
                        mm(sc[:, hh, P:2 * P], Ms[:, h, Q0:Q0 + P], nb[:, h, R0:R0 + P], start=False, stop=(hh == 1)
                           ).then_inc((first, score)[hh][pr].sem, 1)

                def weights_T(k, pr):
                    a = k % NA
                    wait(pe, it, weight[pr], k + 1)
                    if k == 0:
                        wait(pe, it, oT, 0)
                        wait(pe, it, h2, 0)
                    wait(pe, it, outs[pr], k)
                    for hh in range(2):
                        for j in range(1 - a, 2):
                            last = pe.transpose(pT[:, pr, (2 * hh + j) * P:(2 * hh + j + 1) * P], Ps[:, 2 * pr + hh, j * P:(j + 1) * P], ident3[:])
                    last.then_inc(wT_p[pr].sem, 1)

                def out_of(k, pr):
                    g, a = divmod(k, NA)
                    wait(pe, it, wT[pr], k + 1)
                    for hh in range(2):
                        for j in range(1 - a, 2):
                            jt = j - 1 + a
                            last = mm(pT[:, pr, hh * HP:hh * HP + DH + 1], PTs[:, 2 * pr + hh, j, :], va[:, jt, HG * g + 2 * pr + hh, :],
                                      start=(j == 1 - a), stop=(j == 1))
                    last.then_inc(out_p[pr].sem, 1)

                for k in range(NS + 1):
                    if k < NS:
                        grams(k)
                        y_of(k, 0)
                    if k:
                        weights_T(k - 1, 0)
                    if k < NS:
                        y_of(k, 1)
                    if k:
                        weights_T(k - 1, 1)
                    if k < NS:
                        xy_of(k, 0)
                        xy_of(k, 1)
                    if k:
                        out_of(k - 1, 0)
                    if k < NS:
                        top_of(k, 0)
                        top_of(k, 1)
                    if k:
                        out_of(k - 1, 1)
                    if k < NS:
                        each(lambda pr: rhs_of(k, pr))
                        each(lambda pr: low_of(k, pr))
                        each(lambda pr: hat_of(k, pr))
                        each(lambda hh: score_of(k, hh))
                wait(pe, it, outs[0], NS)
                wait(pe, it, outs[1], NS)
                for c in range(KC):
                    for a in range(NA):
                        last = pe.transpose(pT[:, 0, c * T + a * P:c * T + (a + 1) * P], Os[:, a, c * P:(c + 1) * P], ident3[:])
                last.then_inc(oT_p.sem, 1)
                wait(pe, it, oT, 1)
                for a in range(NA):
                    for c in range(KC):
                        last = mm(pT[:, 1, a * D:(a + 1) * D], OT[:, c, a * P:(a + 1) * P], wo_s[:, c, :], start=(c == 0), stop=(c == KC - 1))
                last.then_inc(y_out.sem, 1)

        @block.vector
        def _(dve):
            dve.wait_ge(consts.sem, consts.count(8))
            with dve.Fori(0, B) as it:
                def peak_of(k, pr):
                    a = k % NA
                    wait(dve, it, score[pr], k + 1)
                    sc = pS[:, pr, :].rearrange("p (h j) -> p h j", h=2)
                    dve.tensor_reduce(out=nm[:, 2 * pr:2 * pr + 2], in_=sc[:, :, (1 - a) * P:2 * P], axis=X, op=ALU.max, negate=True).then_inc(peak[pr].sem, 1)

                def mask(k, h):
                    wait(dve, it, gram, HG * k + h + 1)
                    wait(dve, it, score[h // 2], k)
                    dve.tensor_tensor(Ms[:, h, R0:MW], pG[:, h % 2, 0:3 * P], keep[:].rearrange("p m t -> p (m t)"), ALU.mult).then_inc(masked.sem, 1)

                def x64_of(k, pr):
                    g, a = divmod(k, NA)
                    wait(dve, it, xy_p[pr], k + 1)
                    dve.tensor_tensor(X64[:, pr, :, :], XTs[:, a, HG * g + 2 * pr:HG * g + 2 * pr + 2, :],
                                      pC[:, pr, 0:2 * HB].rearrange("p (h t) -> p h t", h=2), ALU.subtract).then_inc(x64[pr].sem, 1)

                def rhs_of(k, pr):
                    wait(dve, it, rhs_p[pr], k + 1)
                    m = Ms[HB:P, 2 * pr:2 * pr + 2, c0(k):R0 + HB]
                    dve.tensor_tensor(m, pC[HB:P, pr, 0:320].rearrange("p (h n) -> p h n", h=2)[:, :, c0(k):R0 + HB], m, ALU.add).then_inc(rhs[pr].sem, 1)

                def hat_of(k, pr):
                    g, a = divmod(k, NA)
                    r = slice(2 * HP * pr, 2 * HP * (pr + 1))
                    wait(dve, it, hat_p[pr], k + 1)
                    dve.tensor_tensor(hats[r, a, :], pC[r, pr, 0:P], Fs[r, g, a, a, :], ALU.add).then_inc(hat[pr].sem, 1)

                def outs_of(k, pr):
                    g, a = divmod(k, NA)
                    o = pT[:, pr, 0:2 * HP].rearrange("p (h n) -> p h n", h=2)
                    wait(dve, it, out_p[pr], k + 1)
                    dve.reciprocal(rec[:, 2 * pr:2 * pr + 2], o[:, :, DH]).then_inc(inv[pr].sem, 1)
                    wait(dve, it, inv[pr], k + 1)
                    at = DH * (HG * g + 2 * pr)
                    dve.tensor_tensor(Os[:, a, at:at + 2 * DH].rearrange("p (h d) -> p h d", d=DH), o[:, :, 0:DH],
                                      rec[:, 2 * pr:2 * pr + 2].unsqueeze(2).broadcast_to([P, 2, DH]), ALU.mult).then_inc(outs[pr].sem, 1)

                for k in range(NS + 1):
                    if k:
                        each(lambda pr: peak_of(k - 1, pr))
                    if k < NS:
                        for h in range(HG):
                            mask(k, h)
                        each(lambda pr: x64_of(k, pr))
                    if k:
                        each(lambda pr: outs_of(k - 1, pr))
                    if k < NS:
                        each(lambda pr: rhs_of(k, pr))
                        each(lambda pr: hat_of(k, pr))
                wait(dve, it, y_out, 1)
                wait(dve, it, h2_out, 0)
                dve.wait_ge(h_in.sem, h_in.count(it * 16 + 16))
                dve.tensor_tensor(h2s[:], pT[:, 1, :].rearrange("p (a n) -> p a n", a=NA), hres[:], ALU.add).then_inc(h2.sem, 1)

        @block.scalar
        def _(act):
            act.wait_ge(consts.sem, consts.count(8))
            with act.Fori(0, B) as it:
                def weight_of(k, pr):
                    a = k % NA
                    wait(act, it, peak[pr], k + 1)
                    for hh in range(2):
                        h = 2 * pr + hh
                        last = act.activation(Ps[:, h, (1 - a) * P:2 * P], pS[:, pr, (2 * hh + 1 - a) * P:(2 * hh + 2) * P], ACT.Exp, bias=nm[:, h:h + 1])
                    last.then_inc(weight[pr].sem, 1)

                def y_of(k, pr):
                    wait(act, it, y_p[pr], k + 1)
                    act.activation(Ys[:, pr, :, :].rearrange("p h t -> p (h t)"), pC[:, pr, 0:2 * HB], ACT.Copy).then_inc(y_s[pr].sem, 1)

                def wT_of(k, pr):
                    a = k % NA
                    wait(act, it, wT_p[pr], k + 1)
                    act.activation(PTs[:, 2 * pr:2 * pr + 2, 1 - a:2, :], pT[:, pr, :].rearrange("p (h j t) -> p h j t", h=2, j=2)[:, :, 1 - a:2, :],
                                   ACT.Copy).then_inc(wT[pr].sem, 1)

                def scaled_of(k, pr, rows, cols, before, after):
                    g, a = divmod(k, NA)
                    wait(act, it, before[pr], k + 1)
                    if k == 0:
                        wait(act, it, copied, 3)
                    for hh in range(2):
                        h = 2 * pr + hh
                        last = act.activation(nb[rows, h, cols], pC[rows, pr, 160 * hh + cols.start:160 * hh + cols.stop], ACT.Copy,
                                              scale=nbeta[rows, a, HG * g + h:HG * g + h + 1])
                    last.then_inc(after[pr].sem, 1)

                for k in range(NS + 1):
                    if k:
                        each(lambda pr: weight_of(k - 1, pr))
                    if k < NS:
                        y_of(k, 0)
                    if k:
                        wT_of(k - 1, 0)
                    if k < NS:
                        y_of(k, 1)
                    if k:
                        wT_of(k - 1, 1)
                    if k < NS:
                        each(lambda pr: scaled_of(k, pr, slice(0, HB), slice(c0(k), R0 + HB), top_p, top))
                        each(lambda pr: scaled_of(k, pr, slice(HB, P), slice(c0(k), R0 + P), low_p, low))
                wait(act, it, oT_p, 1)
                act.activation(OT[:].rearrange("p c t -> p (c t)"), pT[:, 0, :], ACT.Copy).then_inc(oT.sem, 1)


def experts(nc, sems, h2_d, w12, w3, wg, bias, out):
    NU = E1 * NHT
    MID = 4
    with ExitStack() as ctx:
        sb, ps = sbufs(nc, ctx), psums(nc, ctx)

        signals = []

        def sig(name, per=1):
            signals.append(Signal(nc, sems, "p4_" + name, per))
            return signals[-1]

        W12 = sb("W12", [P, E1, KC, 2, NHT * HT])
        W3 = sb("W3", [HT, E1, NHT, D])
        wg_s = sb("wg_s", [P, KC, NE])
        bias_s = sb("bias_s", [P, NE])
        ident4 = sb("ident4", [P, P])
        lower = sb("lower", [P, NE, NE])
        h2s = sb("h2in", [P, NA, D])
        st = sb("st4", [P, NA, 6])
        mv = sb("mv4", [P, NA, 2])
        ve = sb("ve4", [P, NA])
        lnv = sb("lnv4", [P, NA])
        rstd = sb("rstd4", [P, NA])
        xn = sb("xn4", [P, NA, D])
        xT = sb("xT4", [P, KC, T])
        gl = sb("gl", [P, NA, NE])
        cmp = sb("cmp", [P, 3, NA, NE, NE])
        rank = sb("rank", [P, NA, NE])
        top = sb("topmask", [P, NA, NE])
        mx = sb("mx", [P, NA])
        ge = sb("ge", [P, NA, NE])
        gx = sb("gx", [P, NA, NE])
        gm = sb("gmask", [P, NA, NE])
        gs = sb("gs", [P, NA])
        gr = sb("gr", [P, NA])
        route = sb("route", [P, NA, NE])
        sl = sb("sl", [HT, 3, T])
        gT = sb("gT", [HT, 3, NHT, T])
        acc = sb("acc", [P, 2, NA, D])
        zero4, step4 = sb("zero4", [P, 1]), sb("step4", [P, 1])

        pU = ps("pU", [P, 3, 2, T])
        pD = ps("pD", [P, 3, NA, D])
        pX = ps("pX4", [P, KC, T])
        pR = ps("pR", [P, NA, NE])

        loaded, consts = sig("loaded"), sig("consts")
        w_in = [sig(f"w_in{e}") for e in range(E1)]
        h2_in, mean, ln_r, normed, xt_p, xt = sig("h2_in", 16), sig("mean", 5), sig("ln_r", 2), sig("normed", NA), sig("xt_p"), sig("xt")
        gate, router, gexp = sig("gate"), sig("router", 12), sig("gexp")
        up, silu, hidden = sig("up", NU), sig("silu", NU), sig("hidden", NU)
        down, summed, stored = sig("down", E1), sig("summed", NA * E1), sig("stored", 16)
        block = ctx.enter_context(nc.Block())

        def rows_of(x, it):
            return x[DS(it, 1)].rearrange("o (a p) n -> p (o a) n", p=P)

        @block.sync
        def _(sp):
            sp.dma_start(wg_s[:], wg.rearrange("(c p) n -> p c n", p=P)).then_inc(loaded.sem, 16)
            sp.dma_start(bias_s[:], bias.partition_broadcast(P)).then_inc(loaded.sem, 16)
            sp.dma_start(h2s[:], rows_of(h2_d, 0)).then_inc(h2_in.sem, 16)
            for e in range(E1):
                sp.dma_start(W12[:, e].rearrange("p c m n -> p (c m n)"), w12[:, e, :]).then_inc(w_in[e].sem, 16)
                sp.dma_start(W3[:, e].rearrange("p t n -> p (t n)"), w3[:, e, :]).then_inc(w_in[e].sem, 16)
            with sp.Fori(0, B) as it:
                wait(sp, it, summed, NA)
                sp.dma_start(h2s[:], rows_of(h2_d, (it + 1) % B)).then_inc(h2_in.sem, 16)
                wait(sp, it, summed, NA * E1)
                sp.dma_start(rows_of(out, it), acc[:, 0]).then_inc(stored.sem, 16)
            sp.wait_ge(stored.sem, stored.count(16 * B))

        @block.gpsimd
        def _(pool):
            start(pool, signals)
            pool.memset(zero4[:], 0.0).then_inc(consts.sem, 1)
            pool.memset(ident4[:], 0.0).then_inc(consts.sem, 1)
            pool.memset(lower[:], 1.0).then_inc(consts.sem, 1)
            pool.wait_ge(consts.sem, consts.count(3))
            pool.affine_select(out=ident4[:], in_=ident4[:], compare_op=ALU.not_equal, fill=1.0, base=0,
                               pattern=[[-1, P]], channel_multiplier=1).then_inc(consts.sem, 1)
            pool.affine_select(out=lower[:], in_=lower[:], compare_op=ALU.is_gt, fill=0.0, base=0,
                               pattern=[[1, NE], [-1, NE]], channel_multiplier=0).then_inc(consts.sem, 1)

        @block.tensor
        def _(pe):
            mm = nc.tensor.matmul

            def transposes():
                for c in range(KC):
                    for a in range(NA):
                        last = pe.transpose(pX[:, c, a * P:(a + 1) * P], xn[:, a, c * P:(c + 1) * P], ident4[:])
                return last

            pe.wait_ge(consts.sem, consts.count(5))
            pe.wait_ge(loaded.sem, loaded.count(32))
            pe.wait_ge(normed.sem, normed.count(NA))
            transposes().then_inc(xt_p.sem, 1)
            with pe.Fori(0, B) as it:
                def up_of(e):
                    pe.wait_ge(w_in[e].sem, w_in[e].count(32))
                    for t in range(NHT):
                        n = NHT * e + t
                        wait(pe, it, hidden, max(0, n - 2))
                        for m in range(2):
                            for c in range(KC):
                                last = mm(pU[0:HT, n % 3, m, :], W12[:, e, c, m, t * HT:(t + 1) * HT], xT[:, c, :],
                                          start=(c == 0), stop=(c == KC - 1))
                        last.then_inc(up.sem, 1)

                def down_of(e):
                    wait(pe, it, hidden, NHT * (e + 1))
                    wait(pe, it, summed, max(0, NA * (e - 2)))
                    for a in range(NA):
                        for t in range(NHT):
                            last = mm(pD[:, e % 3, a, :], gT[:, e % 3, t, a * P:(a + 1) * P], W3[:, e, t, :],
                                      start=(t == 0), stop=(t == NHT - 1))
                    last.then_inc(down.sem, 1)

                wait(pe, it, xt, 1)
                wait(pe, it, router, 0)
                for a in range(NA):
                    for c in range(KC):
                        last = mm(pR[:, a, :], xT[:, c, a * P:(a + 1) * P], wg_s[:, c, :], start=(c == 0), stop=(c == KC - 1))
                last.then_inc(gate.sem, 1)
                for e in range(E1):
                    up_of(e)
                    if e:
                        down_of(e - 1)
                    if e == MID + 1:
                        pe.wait_ge(normed.sem, normed.count((it + 2) * NA))
                        transposes().then_inc(xt_p.sem, 1)
                down_of(E1 - 1)

        @block.vector
        def _(dve):
            def stats(it):
                dve.wait_ge(h2_in.sem, h2_in.count(it * 16 + 16))
                for a in range(NA):
                    dve.bn_stats(st[:, a, :], h2s[:, a, :]).then_inc(mean.sem, 1)
                wait(dve, it, mean, NA)
                dve.tensor_copy(step4[:], zero4[:])
                for a in range(NA):
                    dve.bn_aggr(mv[:, a, :], st[:, a, :]).then_inc(mean.sem, 1)
                wait(dve, it, mean, 2 * NA)
                dve.tensor_scalar(ve[:], mv[:, :, 1], 1e-5, None, ALU.add).then_inc(mean.sem, 1)

            def norm(it):
                wait(dve, it, ln_r, 2)
                wait(dve, it, xt_p, 0)
                for a in range(NA):
                    dve.tensor_scalar(xn[:, a, :], h2s[:, a, :], mv[:, a, 0:1], rstd[:, a:a + 1],
                                      ALU.subtract, ALU.mult).then_inc(normed.sem, 1)

            dve.wait_ge(consts.sem, consts.count(5))
            dve.wait_ge(loaded.sem, loaded.count(32))
            stats(0)
            norm(0)
            with dve.Fori(0, B) as it:
                def hidden_of(e):
                    for t in range(NHT):
                        n = NHT * e + t
                        wait(dve, it, silu, n + 1)
                        wait(dve, it, down, max(0, e - 2))
                        dve.tensor_tensor(gT[:, e % 3, t, :], sl[:, n % 3, :], pU[0:HT, n % 3, 1, :], ALU.mult).then_inc(hidden.sem, 1)

                def sum_of(e):
                    wait(dve, it, down, e + 1)
                    if e == 0:
                        wait(dve, it, stored, 0)
                    else:
                        wait(dve, it, summed, NA * e)
                    for a in range(NA):
                        dst = acc[:, e % 2, a, :]
                        if e == 0:
                            dve.tensor_tensor(dst, pD[:, 0, a, :], h2s[:, a, :], ALU.add).then_inc(summed.sem, 1)
                        else:
                            dve.scalar_tensor_tensor(out=dst, in0=pD[:, e % 3, a, :], scalar=route[:, a, e - 1:e],
                                                     in1=acc[:, (e - 1) % 2, a, :], op0=ALU.mult, op1=ALU.add).then_inc(summed.sem, 1)

                def chained(n):
                    wait(dve, it, router, n)

                wait(dve, it, gate, 1)
                dve.tensor_tensor(gl[:], pR[:], bias_s[:, None, :].broadcast_to([P, NA, NE]), ALU.add).then_inc(router.sem, 1)
                chained(1)
                mine = gl[:].unsqueeze(3).broadcast_to([P, NA, NE, NE])
                other = gl[:].unsqueeze(2).broadcast_to([P, NA, NE, NE])
                dve.tensor_tensor(cmp[:, 0], other, mine, ALU.is_gt).then_inc(router.sem, 1)
                dve.tensor_tensor(cmp[:, 1], other, mine, ALU.is_equal).then_inc(router.sem, 1)
                dve.reduce_max(mx[:], gl[:], X).then_inc(router.sem, 1)
                chained(4)
                dve.tensor_tensor(cmp[:, 2], cmp[:, 1], lower[:, None, :, :].broadcast_to([P, NA, NE, NE]), ALU.mult).then_inc(router.sem, 1)
                dve.tensor_tensor(ge[:], gl[:], mx[:].unsqueeze(2).broadcast_to([P, NA, NE]), ALU.subtract).then_inc(router.sem, 1)
                chained(6)
                dve.tensor_tensor(cmp[:, 1], cmp[:, 0], cmp[:, 2], ALU.add).then_inc(router.sem, 1)
                chained(7)
                dve.reduce_sum(rank[:], cmp[:, 1], X).then_inc(router.sem, 1)
                chained(8)
                wait(dve, it, gexp, 1)
                dve.scalar_tensor_tensor(out=gm[:], in0=rank[:], scalar=float(TOPK), in1=gx[:], op0=ALU.is_lt, op1=ALU.mult).then_inc(router.sem, 1)
                chained(9)
                dve.reduce_sum(gs[:], gm[:], X).then_inc(router.sem, 1)
                chained(10)
                dve.reciprocal(gr[:], gs[:]).then_inc(router.sem, 1)
                chained(11)
                wait(dve, it, summed, 0)
                dve.tensor_tensor(route[:], gm[:], gr[:].unsqueeze(2).broadcast_to([P, NA, NE]), ALU.mult).then_inc(router.sem, 1)
                chained(12)
                for e in range(E1):
                    hidden_of(e)
                    if e:
                        sum_of(e - 1)
                    if e == MID - 1:
                        stats(it + 1)
                    if e == MID:
                        norm(it + 1)
                sum_of(E1 - 1)

        @block.scalar
        def _(act):
            def root(it):
                wait(act, it, mean, 5)
                act.activation(lnv[:], ve[:], ACT.Ln).then_inc(ln_r.sem, 1)
                wait(act, it, ln_r, 1)
                act.activation(rstd[:], lnv[:], ACT.Exp, scale=-0.5).then_inc(ln_r.sem, 1)

            root(0)
            act.wait_ge(xt_p.sem, xt_p.count(1))
            act.activation(xT[:], pX[:], ACT.Copy).then_inc(xt.sem, 1)
            with act.Fori(0, B) as it:
                wait(act, it, router, 6)
                act.activation(gx[:], ge[:], ACT.Exp).then_inc(gexp.sem, 1)
                for e in range(E1):
                    for t in range(NHT):
                        n = NHT * e + t
                        wait(act, it, up, n + 1)
                        wait(act, it, hidden, max(0, n - 2))
                        act.activation(sl[:, n % 3, :], pU[0:HT, n % 3, 0, :], ACT.Silu).then_inc(silu.sem, 1)
                    if e == MID - 1:
                        root(it + 1)
                act.wait_ge(xt_p.sem, xt_p.count(it + 2))
                act.activation(xT[:], pX[:], ACT.Copy).then_inc(xt.sem, 1)


def kernel(**inputs):
    import numpy as np
    import concourse.bacc as bacc
    from concourse.bass_utils import run_bass_kernel_spmd

    a = {k.replace("L0_", ""): np.asarray(v) for k, v in inputs.items()}
    def stacked(shared, routed):
        return np.concatenate([a[shared][None], a[routed]], 0)

    def padded(x):
        return np.pad(x, [(0, 0), (0, NHT * HT - HF), (0, 0)])

    w12 = np.stack([padded(stacked(f"ffn_Ws{m}", f"ffn_W{m}")) for m in (1, 2)])
    w12 = w12.reshape(2, E1, NHT * HT, KC, P).transpose(4, 1, 3, 0, 2).reshape(P, E1, -1)
    w3 = padded(stacked("ffn_Ws3", "ffn_W3").transpose(0, 2, 1))
    w3 = w3.reshape(E1, NHT, HT, D).transpose(2, 0, 1, 3).reshape(HT, E1, -1)
    arrays = {
        "w12": w12, "w3": w3, "wg": a["ffn_Wg"].T, "bias": a["ffn_routing_bias"],
        "ids": np.ascontiguousarray(a["x"].reshape(NT, P).T),
        "emb0": a["tok_emb0"], "emb1": a["tok_emb1"], "emb2": a["tok_emb2"], "emb3": a["tok_emb3"],
        "projT": np.ascontiguousarray(np.concatenate([a[f"tok_proj{i}"].T for i in range(4)], 0)),
        "wkq": np.concatenate([a["attn_Wk"], a["attn_Wq"]], 1),
        "wvbg": np.concatenate([a["attn_Wv"], a["attn_beta_w"], a["attn_g_w"]], 1),
        "wA": a["attn_wA"], "wB": a["attn_wB"], "conv": a["attn_conv_w"], "gb": a["attn_g_b"],
        "wo": a["attn_Wo"],
        "norms_w": np.stack([a["attn_knorm_w"], a["attn_qnorm_w"]]),
    }
    nc = bacc.Bacc("TRN2", target_bir_lowering=False, num_devices=1)
    t = {}
    arrays = {f"in_{n}": np.ascontiguousarray(v) for n, v in arrays.items()}
    for n, v in arrays.items():
        t[n[3:]] = nc.dram_tensor(n, v.shape, mybir.dt.from_np(v.dtype), kind="ExternalInput").ap()
    out = nc.dram_tensor("out", (B, T, D), F32, kind="ExternalOutput").ap()
    build(nc, t, out)
    r = run_bass_kernel_spmd(nc, [arrays], core_ids=[0])
    return r.results[0]["out"]


def build(nc, t, out):
    h_d = nc.dram_tensor("h_scratch", (B, T, D), F32).ap()
    F_d = nc.dram_tensor("heads_scratch", (B, P, NG * NA * 3 * P), F32).ap()
    tm_d = nc.dram_tensor("token_scratch", (B, T, TM), F32).ap()
    with ExitStack() as sems:
        embed_and_project(nc, sems, t["ids"], [t[f"emb{i}"] for i in range(4)], t["projT"], t["wkq"], t["wvbg"],
                          t["wA"], t["wB"], t["conv"], t["gb"], t["norms_w"], h_d, F_d, tm_d)
        xt_d = nc.dram_tensor("xt_scratch", (NCH, H, CH, CH), F32).ap()
        bx_d = nc.dram_tensor("bx_scratch", (NCH, H, CH, CH), F32).ap()
        invert_chunks(nc, sems, tm_d, xt_d, bx_d)
        h2_d = nc.dram_tensor("h2_scratch", (B, T, D), F32).ap()
        attend(nc, sems, F_d, tm_d, xt_d, bx_d, h_d, t["wo"], h2_d)
        experts(nc, sems, h2_d, t["w12"], t["w3"], t["wg"], t["bias"], out)
```

```python
from contextlib import ExitStack

import concourse.bass as bass
from concourse import mybir

P = 128
F32 = mybir.dt.float32
BF16 = mybir.dt.bfloat16
I32 = mybir.dt.int32
U32 = mybir.dt.uint32
ALU = mybir.AluOpType
ACT = mybir.ActivationFunctionType
X = mybir.AxisListType.X
DS = bass.ds

B, T, D = 16, 256, 256
H, DH = 16, 16
HP = 32
NT = B * T // P
NA = T // P
KC = D // P
NG, HG = 4, 4
CH = 32
NCB = T // CH
ENDS = (0, 5000, 10000, 50000, 267735)
EW = (256, 64, 16, 4)
EO = (0, 256, 320, 336)
EC = sum(EW)
EB = EC - 2 * P
WB = DH + 1
V0 = H * WB
TM = V0 + D
E1, HF, HT, NHT = 9, 682, 114, 6
NE, TOPK = 8, 4


class Signal:

    def __init__(self, nc, ctx, name, per, first=1):
        self.sem = ctx.enter_context(nc.semaphore(name))
        self.per, self.first = per, first

    def at(self, it, k):
        return it * self.per + (k + self.first)

    def count(self, n):
        return n + self.first


def start(eng, signals):
    for signal in signals:
        eng.sem_inc(signal.sem, 1)


def wait(eng, it, signal, k):
    eng.wait_ge(signal.sem, signal.at(it, k))


def wait_apart(eng, it, signal, k, passed):
    eng.wait_ge(signal.sem, signal.at(it, k))
    eng.sem_inc(passed.sem, 1)


def sbufs(nc, ctx):
    return lambda name, shape, dt=F32: ctx.enter_context(nc.sbuf_tensor(name, shape, dt))


def psums(nc, ctx):
    return lambda name, shape, dt=F32: ctx.enter_context(nc.psum_tensor(name, shape, dt))


def embed_and_project(nc, sems, ids, emb, projT, wkq, wvbg, wA, wB, conv, gb, norms_w, h_d, F_d, tm_d):
    AHEAD = 3
    with ExitStack() as ctx:
        sb, ps = sbufs(nc, ctx), psums(nc, ctx)

        signals = []

        def sig(name, per=1):
            signals.append(Signal(nc, sems, "p1_" + name, per))
            return signals[-1]

        NX = NT + AHEAD * NA
        ids_i = sb("ids_i", [P, NX], I32)
        idx_all = sb("idx_all", [P, NX, 4], I32)
        msk_all = sb("msk_all", [P, NX, 4])
        idx = sb("idx", [P, NA, 4], I32)
        msk = sb("msk", [P, NA, 4])
        lt = sb("lt", [P, NX])
        ident = sb("ident", [P, P])
        upto = sb("upto", [P, P])
        ones = sb("ones", [P, P])
        projT_s = sb("projT_s", [P, 3, D])
        wkq_s = sb("wkq_s", [P, KC, 2 * D])
        wvbg_s = sb("wvbg_s", [P, KC, D + 2 * H])
        wA_s = sb("wA_s", [P, KC, 32])
        wB_s = sb("wB_s", [32, D])
        conv_s = sb("conv_s", [P, KC, 3])
        gb_s = sb("gb_s", [P, H])
        norms_s = sb("norms_s", [P, 2, DH])
        norms = sb("norms", [P, 2, DH])
        zero = sb("zero", [P, 1])
        step1, pstep = sb("step", [P, 1]), sb("pstep", [P, 1])
        E = sb("E", [P, NA, EC])
        Em = sb("Em", [P, NA, EC])
        ET = sb("ET", [P, NA, 3 * P])
        hs = sb("hs", [P, NA, D])
        st = sb("st", [P, NA, 6])
        mv = sb("mv", [P, NA, 2])
        ve = sb("ve", [P, NA])
        lnv = sb("lnv", [P, NA])
        rstd = sb("rstd", [P, NA])
        xn = sb("xn", [P, NA, D])
        xT = sb("xT", [P, KC, T])
        xAT = sb("xAT", [32, T])
        wpad = sb("wpad", [P, KC, 2 + T])
        cv = sb("cv", [P, 3, KC, T])
        ex = sb("ex", [P, KC, T])
        ex1 = sb("ex1", [P, KC, T])
        sg = sb("sg", [P, KC, T])
        ws = sb("ws", [P, KC, T])
        sq = sb("sq", [P, NA, 3 * D])
        ss = sb("ss", [P, NA, 3 * H])
        sse = sb("sse", [P, NA, 3 * H])
        lns = sb("lns", [P, NA, 3 * H])
        rs = sb("rs", [P, NA, 3 * H])
        qkt = sb("qkt", [P, NA, 2 * D])
        vs = sb("vs", [P, NA, D])
        z, zabs, zexp, gexp, gln, g = [sb(name, [P, NA, H]) for name in ("z_beta", "zabs_g", "zexp_beta", "zexp_g", "zln_g", "gate")]
        zg, b1, br = sb("z_g", [P, NA, H]), sb("beta_sum", [P, NA, H]), sb("beta_rec", [P, NA, H])
        Ft = sb("Ft", [P, NA, 3, H, HP])
        FT = sb("FT", [P, NG, NA, 3, P])
        tm = sb("tm", [P, NA, V0])
        tmw = tm[:].rearrange("p a (h e) -> p a h e", e=WB)

        pE = ps("pE", [P, NA, 512])
        pQ = ps("pQ", [P, NA, 512])
        pX = ps("pX", [P, KC, T])
        pA = ps("pA", [P, 512])
        pV = ps("pV", [P, NA, D])
        pF = ps("pF", [P, 512])
        Z0, G0 = T, T + NA * 2 * H
        zp = pA[:, Z0:G0].rearrange("p (a n) -> p a n", a=NA)
        G = pA[:, G0:G0 + NA * H].rearrange("p (a h) -> p a h", h=H)

        loaded, consts, ids_ready = sig("loaded"), sig("consts"), sig("ids_ready")
        idx_in, msk_in, carried, moved = sig("idx_in"), sig("msk_in"), sig("carried"), sig("moved")
        gathered = Signal(nc, sems, "p1_gathered", 16 * 4 * NA, first=0)
        masked, et_p, et, h_p, h_s = sig("masked", 4), sig("et_p"), sig("et", 2), sig("h_p"), sig("h_s")
        h_out, mean, root, normed = sig("h_out", 16), sig("mean", 5), sig("root", 2), sig("normed", 2)
        xt_p, xt, xa_p, xa, w_p, w_s = sig("xt_p"), sig("xt"), sig("xa_p"), sig("xa"), sig("w_p"), sig("w_s")
        z_p, z_s, zexps, v_p, v_s, v_out, qk_p = sig("z_p"), sig("z_s", 2), sig("zexps", 3), sig("v_p"), sig("v_s"), sig("v_out", 16), sig("qk_p")
        conved, wexp, silu, wt_p, squared = sig("conved", 6), sig("wexp"), sig("silu", 3), sig("wt_p"), sig("squared", 2)
        sums, logs, beta, soft, gate, gsum, running = sig("sums", 3), sig("logs", 2), sig("beta", 3), sig("soft"), sig("gate"), sig("gsum"), sig("running", 2)
        qk_scaled, w_scaled, heads = sig("qk_scaled", NA), sig("w_scaled", 2 * NA), sig("heads", 2 * NA)
        f_p, f_even, f_odd, f_out, tm_out = sig("f_p", 6), sig("f_even", 3), sig("f_odd", 3), sig("f_out", 16), sig("tm_out", 16)

        block = ctx.enter_context(nc.Block())

        def skewed(eng, step):
            step(0, None, None)
            step(1, 0, None)
            with eng.Fori(0, B) as it:
                step(it + 2, it + 1, it)

        def rows_of(x, n):
            return x[DS(n % B, 1)].rearrange("o (a p) n -> p (o a) n", p=P)

        @block.sync
        def _(sp):
            for dst, src in ((ids_i[:, 0:NT], ids), (ids_i[:, NT:NX], ids[:, 0:AHEAD * NA]),
                             (projT_s[:, 0:2, :], projT[0:2 * P, :].rearrange("(c p) n -> p c n", p=P)),
                             (projT_s[0:EB, 2, :], projT[2 * P:EC, :]),
                             (wkq_s[:], wkq.rearrange("(c p) n -> p c n", p=P)),
                             (wvbg_s[:], wvbg.rearrange("(c p) n -> p c n", p=P)),
                             (wA_s[:], wA.rearrange("(c p) n -> p c n", p=P)), (wB_s[:], wB),
                             (conv_s[:], conv.rearrange("(c p) n -> p c n", p=P)),
                             (gb_s[:], gb.partition_broadcast(P)), (norms_s[:], norms_w.partition_broadcast(P))):
                sp.dma_start(dst, src).then_inc(loaded.sem, 16)

            def step(first, second, third):
                if third is not None:
                    wait(sp, third, w_scaled, 2 * NA)
                    wait(sp, third, beta, 3)
                    sp.dma_start(rows_of(tm_d, third)[:, :, 0:V0], tm[:]).then_inc(tm_out.sem, 16)
                wait(sp, first, h_s, 1)
                sp.dma_start(rows_of(h_d, first), hs[:]).then_inc(h_out.sem, 16)
                if second is not None:
                    wait(sp, second, v_s, 1)
                    sp.dma_start(rows_of(tm_d, second)[:, :, V0:TM], vs[:]).then_inc(v_out.sem, 16)
                if third is not None:
                    wait(sp, third, f_even, 3)
                    wait(sp, third, f_odd, 3)
                    sp.dma_start(F_d[DS(third, 1)].rearrange("o p n -> p (o n)"), FT[:].rearrange("p g a m t -> p (g a m t)")).then_inc(f_out.sem, 16)

            skewed(sp, step)
            sp.wait_ge(h_out.sem, h_out.count(16 * (B + 2)))
            sp.wait_ge(v_out.sem, v_out.count(16 * (B + 1)))
            sp.wait_ge(tm_out.sem, tm_out.count(16 * B))
            sp.wait_ge(f_out.sem, f_out.count(16 * B))

        @block.gpsimd
        def _(pool):
            start(pool, signals)
            pool.memset(zero[:], 0.0).then_inc(consts.sem, 1)
            pool.memset(ident[:], 0.0).then_inc(consts.sem, 1)
            pool.memset(ones[:], 1.0).then_inc(consts.sem, 1)
            pool.memset(wpad[:], 0.0).then_inc(consts.sem, 1)
            pool.memset(Ft[:], 0.0).then_inc(consts.sem, 1)
            pool.wait_ge(consts.sem, consts.count(5))
            pool.memset(Ft[:, :, 1, :, DH + 1:DH + 2], 1.0).then_inc(consts.sem, 1)
            pool.memset(Ft[:, :, 0, :, DH:DH + 1], 1.0).then_inc(consts.sem, 1)
            pool.affine_select(out=ident[:], in_=ident[:], compare_op=ALU.not_equal, fill=1.0, base=0,
                               pattern=[[-1, P]], channel_multiplier=1).then_inc(consts.sem, 1)
            pool.affine_select(out=upto[:], in_=ones[:], compare_op=ALU.is_ge, fill=0.0, base=0,
                               pattern=[[1, P]], channel_multiplier=-1).then_inc(consts.sem, 1)
            pool.wait_ge(consts.sem, consts.count(9))

            def gather(n):
                wait(pool, n, idx_in, 1)
                wait(pool, n, masked, 0)
                wait(pool, n, carried, 0)
                pool.tensor_tensor(out=pstep[:], in0=zero[:], in1=zero[:], op=ALU.add).then_inc(carried.sem, 1)
                for a in range(NA):
                    for i in range(4):
                        pool.indirect_dma_start(
                            out=E[:, a, EO[i]:EO[i] + EW[i]], out_offset=None, in_=emb[i],
                            in_offset=bass.IndirectOffsetOnAxis(ap=idx[:, a, i:i + 1], axis=0),
                        ).then_inc(gathered.sem, 16)

            def step(first, second, third):
                if third is not None:
                    wait(pool, third, qk_scaled, NA)
                    wait(pool, third, f_p, 0)
                    for a in range(NA):
                        for m in range(2):
                            pool.tensor_tensor(
                                out=Ft[:, a, m, :, 0:DH],
                                in0=qkt[:, a, m * D:(m + 1) * D].rearrange("p (h d) -> p h d", d=DH),
                                in1=norms[:, m:m + 1, :].broadcast_to([P, H, DH]), op=ALU.mult).then_inc(heads.sem, 1)
                gather(first + 1)

            gather(0)
            skewed(pool, step)
            pool.wait_ge(gathered.sem, gathered.count(16 * 4 * NA * (B + 3)))

        @block.vector
        def _(dve):
            dve.wait_ge(loaded.sem, loaded.count(16 * 11))
            for i in range(4):
                lo, hi = ENDS[i], ENDS[i + 1]
                dve.tensor_scalar(lt[:], ids_i[:], float(-lo), 0.0, ALU.add, ALU.max).then_inc(ids_ready.sem, 1)
                dve.wait_ge(ids_ready.sem, ids_ready.count(4 * i + 1))
                dve.tensor_scalar(idx_all[:, :, i], lt[:], float(hi - lo - 1), None, ALU.min).then_inc(ids_ready.sem, 1)
                dve.wait_ge(ids_ready.sem, ids_ready.count(4 * i + 2))
                dve.tensor_scalar(lt[:], ids_i[:], float(lo), None, ALU.is_ge).then_inc(ids_ready.sem, 1)
                dve.wait_ge(ids_ready.sem, ids_ready.count(4 * i + 3))
                dve.scalar_tensor_tensor(out=msk_all[:, :, i], in0=ids_i[:], scalar=float(hi), in1=lt[:],
                                         op0=ALU.is_lt, op1=ALU.mult).then_inc(ids_ready.sem, 1)
                dve.wait_ge(ids_ready.sem, ids_ready.count(4 * i + 4))
            dve.tensor_scalar(norms[:, 1, :], norms_s[:, 1, :], DH ** -0.5, None, ALU.mult).then_inc(ids_ready.sem, 1)
            dve.tensor_copy(norms[:, 0, :], norms_s[:, 0, :]).then_inc(ids_ready.sem, 1)
            dve.wait_ge(ids_ready.sem, ids_ready.count(18))
            dve.wait_ge(consts.sem, consts.count(9))

            def rows_known(n):
                dve.tensor_copy(idx[:], idx_all[:, DS(n * NA, NA), :]).then_inc(idx_in.sem, 1)

            def betas(n):
                wait(dve, n, zexps, 3)
                dve.tensor_scalar(b1[:], zexp[:], 1.0, None, ALU.add).then_inc(beta.sem, 1)
                wait(dve, n, beta, 1)
                dve.reciprocal(br[:], b1[:]).then_inc(beta.sem, 1)
                wait(dve, n, beta, 2)
                wait(dve, n, tm_out, 0)
                dve.tensor_scalar(tmw[:, :, :, DH], br[:], 2.0, None, ALU.mult).then_inc(beta.sem, 1)

            def embeddings(n):
                dve.tensor_copy(msk[:], msk_all[:, DS(n * NA, NA), :]).then_inc(msk_in.sem, 1)
                wait(dve, n, msk_in, 1)
                wait(dve, n, gathered, 16 * 4 * NA)
                wait(dve, n, et_p, 0)
                for i in range(4):
                    dve.tensor_tensor(Em[:, :, EO[i]:EO[i] + EW[i]], E[:, :, EO[i]:EO[i] + EW[i]],
                                      msk[:, :, i:i + 1].broadcast_to([P, NA, EW[i]]), ALU.mult).then_inc(masked.sem, 1)

            def norm(n):
                wait(dve, n, root, 2)
                wait(dve, n, xt_p, 0)
                for a in range(NA):
                    dve.tensor_scalar(xn[:, a, :], hs[:, a, :], mv[:, a, 0:1], rstd[:, a:a + 1],
                                      ALU.subtract, ALU.mult).then_inc(normed.sem, 1)

            def scale_heads(n):
                wait(dve, n, logs, 2)
                wait(dve, n, heads, 0)
                for a in range(NA):
                    dve.tensor_tensor(qkt[:, a, :].rearrange("p (h d) -> p h d", d=DH),
                                      pQ[:, a, :].rearrange("p (h d) -> p h d", d=DH),
                                      rs[:, a, 0:2 * H].unsqueeze(2).broadcast_to([P, 2 * H, DH]), ALU.mult).then_inc(qk_scaled.sem, 1)
                wait(dve, n, f_p, 0)
                for a in range(NA):
                    wrow = pF[:, a * D:(a + 1) * D].rearrange("p (h d) -> p h d", d=DH)
                    wrs = rs[:, a, 2 * H:3 * H].unsqueeze(2).broadcast_to([P, H, DH])
                    dve.tensor_tensor(Ft[:, a, 2, :, 0:DH], wrow, wrs, ALU.mult).then_inc(w_scaled.sem, 1)
                    dve.tensor_tensor(tmw[:, a, :, 0:DH], wrow, wrs, ALU.mult).then_inc(w_scaled.sem, 1)

            def gate_of(n):
                wait(dve, n, soft, 1)
                wait(dve, n, gsum, 0)
                dve.scalar_tensor_tensor(out=g[:], in0=zg[:], scalar=0.0, in1=gln[:],
                                         op0=ALU.min, op1=ALU.subtract).then_inc(gate.sem, 1)

            def running_of(n):
                wait(dve, n, gsum, 1)
                dve.tensor_copy(Ft[:, :, 1, :, DH], G).then_inc(running.sem, 1)
                dve.tensor_scalar(Ft[:, :, 0, :, DH + 1], G, -1.0, None, ALU.mult).then_inc(running.sem, 1)

            def convolve(n):
                wait(dve, n, w_s, 1)
                wait(dve, n, wexp, 0)
                for c in range(KC):
                    dve.tensor_scalar(cv[:, 0, c, :], wpad[:, c, 0:T], conv_s[:, c, 0:1], None, ALU.mult).then_inc(conved.sem, 1)
                for k in (1, 2):
                    wait(dve, n, conved, 2 * k)
                    for c in range(KC):
                        dve.scalar_tensor_tensor(out=cv[:, k, c, :], in0=wpad[:, c, k:k + T], scalar=conv_s[:, c, k:k + 1],
                                                 in1=cv[:, k - 1, c, :], op0=ALU.mult, op1=ALU.add).then_inc(conved.sem, 1)

            def gate_logits(n):
                wait(dve, n, z_p, 1)
                wait(dve, n, zexps, 0)
                wait(dve, n, gate, 0)
                dve.tensor_copy(z[:], zp[:, :, 0:H]).then_inc(z_s.sem, 1)
                dve.tensor_tensor(zg[:], zp[:, :, H:2 * H], gb_s[:, None, :].broadcast_to([P, NA, H]), ALU.add).then_inc(z_s.sem, 1)

            def moments(n):
                wait(dve, n, h_s, 1)
                wait(dve, n, root, 0)
                for a in range(NA):
                    dve.bn_stats(st[:, a, :], hs[:, a, :]).then_inc(mean.sem, 1)
                wait(dve, n, mean, NA)
                wait(dve, n, moved, 0)
                dve.tensor_copy(step1[:], zero[:]).then_inc(moved.sem, 1)
                for a in range(NA):
                    dve.bn_aggr(mv[:, a, :], st[:, a, :]).then_inc(mean.sem, 1)
                wait(dve, n, mean, 2 * NA)
                dve.tensor_scalar(ve[:], mv[:, :, 1], 1e-5, None, ALU.add).then_inc(mean.sem, 1)

            def silu_of(n):
                wait(dve, n, wexp, 1)
                dve.tensor_scalar(ex1[:], ex[:], 1.0, None, ALU.add).then_inc(silu.sem, 1)
                wait(dve, n, silu, 1)
                dve.reciprocal(sg[:], ex1[:]).then_inc(silu.sem, 1)
                wait(dve, n, silu, 2)
                wait(dve, n, wt_p, 0)
                dve.tensor_tensor(ws[:], cv[:, 2, :, :], sg[:], ALU.mult).then_inc(silu.sem, 1)

            def even_heads(n, j):
                wait(dve, n, f_p, j + 1)
                wait(dve, n, f_out, 0)
                dve.tensor_copy(FT[:].rearrange("p g a m t -> p (g a m t)")[:, 512 * j:512 * (j + 1)], pF[:]).then_inc(f_even.sem, 1)

            def head_sums(n):
                wait(dve, n, squared, 2)
                wait(dve, n, logs, 0)
                dve.reduce_sum(ss[:].rearrange("p a h -> p (a h)"), sq[:].rearrange("p a (h d) -> p (a h) d", d=DH), X).then_inc(sums.sem, 1)
                wait(dve, n, sums, 1)
                dve.tensor_scalar(sse[:, :, 0:2 * H], ss[:, :, 0:2 * H], 1.0 / DH, 1e-5, ALU.mult, ALU.add).then_inc(sums.sem, 1)
                dve.tensor_scalar(sse[:, :, 2 * H:3 * H], ss[:, :, 2 * H:3 * H], 1e-12, None, ALU.add).then_inc(sums.sem, 1)

            def step(first, second, third):
                if third is not None:
                    betas(third)
                embeddings(first)
                rows_known(first + 1)
                if second is not None:
                    norm(second)
                if third is not None:
                    scale_heads(third)
                    gate_of(third)
                    running_of(third)
                if second is not None:
                    convolve(second)
                    gate_logits(second)
                if third is not None:
                    even_heads(third, 0)
                moments(first)
                if third is not None:
                    even_heads(third, 2)
                if second is not None:
                    silu_of(second)
                if third is not None:
                    even_heads(third, 4)
                if second is not None:
                    head_sums(second)

            rows_known(0)
            skewed(dve, step)

        @block.scalar
        def _(act):
            act.wait_ge(consts.sem, consts.count(9))

            def odd_heads(n, j):
                wait(act, n, f_p, j + 1)
                wait(act, n, f_out, 0)
                act.activation(FT[:].rearrange("p g a m t -> p (g a m t)")[:, 512 * j:512 * (j + 1)], pF[:], ACT.Copy).then_inc(f_odd.sem, 1)

            def step(first, second, third):
                if second is not None:
                    wait(act, second, mean, 5)
                    act.activation(lnv[:], ve[:], ACT.Ln).then_inc(root.sem, 1)
                if third is not None:
                    wait(act, third, sums, 3)
                    act.activation(lns[:], sse[:], ACT.Ln).then_inc(logs.sem, 1)
                    wait(act, third, zexps, 3)
                    wait(act, third, gate, 0)
                    act.activation(gln[:], gexp[:], ACT.Ln, bias=1.0).then_inc(soft.sem, 1)
                if second is not None:
                    wait(act, second, root, 1)
                    wait(act, second, normed, 0)
                    act.activation(rstd[:], lnv[:], ACT.Exp, scale=-0.5).then_inc(root.sem, 1)
                if third is not None:
                    wait(act, third, logs, 1)
                    wait(act, third, qk_scaled, 0)
                    wait(act, third, w_scaled, 0)
                    act.activation(rs[:], lns[:], ACT.Exp, scale=-0.5).then_inc(logs.sem, 1)
                wait(act, first, et_p, 1)
                wait(act, first, h_p, 0)
                act.activation(ET[:, :, 0:2 * P], pE[:, :, 0:2 * P], ACT.Copy).then_inc(et.sem, 1)
                act.activation(ET[0:EB, :, 2 * P:3 * P], pE[0:EB, :, 2 * P:3 * P], ACT.Copy).then_inc(et.sem, 1)
                if second is not None:
                    wait(act, second, xt_p, 1)
                    wait(act, second, v_p, 0)
                    wait(act, second, qk_p, 0)
                    act.activation(xT[:], pX[:], ACT.Copy).then_inc(xt.sem, 1)
                    wait(act, second, xa_p, 1)
                    act.activation(xAT[:], pA[0:32, 0:T], ACT.Copy).then_inc(xa.sem, 1)
                wait(act, first, h_p, 1)
                wait(act, first, h_out, 0)
                wait(act, first, normed, 0)
                act.activation(hs[:], pE[:, 0, :].rearrange("p (a n) -> p a n", a=NA), ACT.Copy, scale=float(D) ** 0.5).then_inc(h_s.sem, 1)
                if second is not None:
                    wait(act, second, w_p, 1)
                    wait(act, second, conved, 0)
                    act.activation(wpad[:, :, 2:2 + T], pX[:], ACT.Copy).then_inc(w_s.sem, 1)
                    wait(act, second, v_p, 1)
                    wait(act, second, v_out, 0)
                    act.activation(vs[:], pV[:], ACT.Copy).then_inc(v_s.sem, 1)
                    wait(act, second, conved, 6)
                    wait(act, second, silu, 0)
                    act.activation(ex[:], cv[:, 2, :, :], ACT.Exp, scale=-1.0).then_inc(wexp.sem, 1)
                    wait(act, second, z_s, 2)
                    wait(act, second, beta, 0)
                    act.activation(zabs[:], zg[:], ACT.Abs).then_inc(zexps.sem, 1)
                    act.activation(zexp[:], z[:], ACT.Exp, scale=-1.0).then_inc(zexps.sem, 1)
                    wait(act, second, zexps, 1)
                    wait(act, second, soft, 0)
                    act.activation(gexp[:], zabs[:], ACT.Exp, scale=-1.0).then_inc(zexps.sem, 1)
                if third is not None:
                    odd_heads(third, 1)
                if second is not None:
                    wait(act, second, qk_p, 1)
                    wait(act, second, sums, 0)
                    act.activation(sq[:, :, 0:2 * D], pQ[:], ACT.Square).then_inc(squared.sem, 1)
                if third is not None:
                    odd_heads(third, 3)
                    odd_heads(third, 5)
                if second is not None:
                    wait(act, second, wt_p, 1)
                    act.activation(sq[:, :, 2 * D:3 * D], pF[:].rearrange("p (a n) -> p a n", a=NA), ACT.Square).then_inc(squared.sem, 1)

            skewed(act, step)

        @block.tensor
        def _(pe):
            pe.wait_ge(consts.sem, consts.count(9))
            pe.wait_ge(loaded.sem, loaded.count(16 * 11))
            mm = nc.tensor.matmul

            def embeddings_T(n):
                wait(pe, n, masked, 4)
                wait(pe, n, h_s, 0)
                for a in range(NA):
                    for c in range(3):
                        w = P if c < 2 else EB
                        last = pe.transpose(pE[0:w, a, c * P:(c + 1) * P], Em[:, a, c * P:c * P + w], ident[:])
                last.then_inc(et_p.sem, 1)

            def project(n):
                wait(pe, n, et, 2)
                for a in range(NA):
                    for c in range(3):
                        w = P if c < 2 else EB
                        last = mm(pE[:, 0, a * D:(a + 1) * D], ET[0:w, a, c * P:(c + 1) * P], projT_s[0:w, c, :], start=(c == 0), stop=(c == 2))
                last.then_inc(h_p.sem, 1)

            def norm_T(n):
                wait(pe, n, normed, 2)
                wait(pe, n, w_s, 0)
                for c in range(KC):
                    for a in range(NA):
                        last = pe.transpose(pX[:, c, a * P:(a + 1) * P], xn[:, a, c * P:(c + 1) * P], ident[:])
                last.then_inc(xt_p.sem, 1)

            def xa_of(n):
                wait(pe, n, xt, 1)
                wait(pe, n, z_s, 0)
                if not isinstance(n, int):
                    wait(pe, n - 1, running, 0)
                for c in range(KC):
                    last = mm(pA[0:32, 0:T], wA_s[:, c, :], xT[:, c, :], start=(c == 0), stop=(c == KC - 1))
                last.then_inc(xa_p.sem, 1)

            def w_of(n):
                wait(pe, n, xa, 1)
                for c in range(KC):
                    last = mm(pX[:, c, :], wB_s[:, c * P:(c + 1) * P], xAT[:], start=True, stop=True)
                last.then_inc(w_p.sem, 1)

            def running_sums(n):
                wait(pe, n, gate, 1)
                wait(pe, n + 1, xa, 1)
                mm(pA[:, G0:G0 + H], upto[:], g[:, 0, :], start=True, stop=True)
                mm(pA[:, G0 + H:G0 + 2 * H], ones[:], g[:, 0, :], start=True, stop=False)
                mm(pA[:, G0 + H:G0 + 2 * H], upto[:], g[:, 1, :], start=False, stop=True).then_inc(gsum.sem, 1)

            def logits_of(n):
                wait(pe, n, running, 0)
                for a in range(NA):
                    for c in range(KC):
                        last = mm(pA[:, Z0 + 2 * H * a:Z0 + 2 * H * (a + 1)], xT[:, c, a * P:(a + 1) * P], wvbg_s[:, c, D:D + 2 * H], start=(c == 0), stop=(c == KC - 1))
                last.then_inc(z_p.sem, 1)

            def v_of(n):
                wait(pe, n, v_s, 0)
                for a in range(NA):
                    for c in range(KC):
                        last = mm(pV[:, a, :], xT[:, c, a * P:(a + 1) * P], wvbg_s[:, c, 0:D], start=(c == 0), stop=(c == KC - 1))
                last.then_inc(v_p.sem, 1)

            def qk_of(n):
                wait(pe, n, qk_scaled, 0)
                wait(pe, n, squared, 0)
                for a in range(NA):
                    for c in range(KC):
                        last = mm(pQ[:, a, :], xT[:, c, a * P:(a + 1) * P], wkq_s[:, c, :], start=(c == 0), stop=(c == KC - 1))
                last.then_inc(qk_p.sem, 1)

            def w_T(n):
                wait(pe, n, silu, 3)
                wait(pe, n, f_even, 0)
                wait(pe, n, f_odd, 0)
                for a in range(NA):
                    for c in range(KC):
                        last = pe.transpose(pF[:, a * D + c * P:a * D + (c + 1) * P], ws[:, c, a * P:(a + 1) * P], ident[:])
                last.then_inc(wt_p.sem, 1)

            def heads_T(n, j):
                if j == 0:
                    wait(pe, n, heads, 2 * NA)
                    wait(pe, n, w_scaled, 2 * NA)
                    wait(pe, n, running, 2)
                    wait(pe, n, squared, 2)
                else:
                    wait(pe, n, f_odd if j % 2 == 0 else f_even, (j + 1) // 2)
                for i in range(4):
                    r = 4 * j + i
                    gg, a, m = r // 6, r % 6 // 3, r % 3
                    last = pe.transpose(pF[:, i * P:(i + 1) * P],
                                        Ft[:, a, m, 4 * gg:4 * gg + 4, :].rearrange("p h d -> p (h d)"), ident[:])
                last.then_inc(f_p.sem, 1)

            def step(first, second, third):
                embeddings_T(first)
                if second is not None:
                    norm_T(second)
                project(first)
                if second is not None:
                    xa_of(second)
                    v_of(second)
                    w_of(second)
                if third is not None:
                    running_sums(third)
                if second is not None:
                    logits_of(second)
                    qk_of(second)
                if third is not None:
                    for j in range(6):
                        heads_T(third, j)
                if second is not None:
                    w_T(second)

            skewed(pe, step)


def attend(nc, sems, F_d, tm_d, xt_d, bx_d, h_d, wo, h2_d):
    NS = NG * NA
    HC = CH // 2
    DSTEP = HC * (CH + 1)
    GR = 4
    NGR = CH // GR
    NM = 4
    NL = NGR + (HC - 1) + 4
    W0, R0, Q0, G0, MW = 0, HP, HP + P, HP + 2 * P, HP + 3 * P
    HB = P // 2
    with ExitStack() as ctx:
        sb, ps = sbufs(nc, ctx), psums(nc, ctx)

        signals = []

        def sig(name, per=1):
            signals.append(Signal(nc, sems, "p3_" + name, per))
            return signals[-1]

        Fs = sb("Fs", [P, NG, NA, 3, P])
        XTs = sb("XTs", [P, NA, H, HB])
        BXs = sb("BXs", [P, NA, H, HB])
        tms = sb("tms", [P, NA, TM])
        tmw = tms[:, :, 0:V0].rearrange("p a (h e) -> p a h e", e=WB)
        wt = sb("wt", [P, NA, H, DH])
        va = sb("va", [P, NA, H, DH + 1])
        nbeta = sb("nbeta", [P, NA, H])
        hres = sb("hres", [P, NA, D])
        wo_s = sb("wo_s", [P, KC, D])
        lw = sb("lane_w", [P, CH, WB])
        lbeta = sb("lane_beta", [P, CH])
        lnbw = sb("lane_nbw", [P, CH, DH])
        Lf = sb("lane_L", [P, 2 * DSTEP])
        Xf = sb("lane_Xt", [P, 2 * DSTEP])
        L, Xt = [x[:, 0:CH * CH].rearrange("p (i j) -> p i j", j=CH) for x in (Lf, Xf)]
        Ld, Xd = [x[:].rearrange("p (b r) -> p b r", b=2)[:, :, 0:HC * CH].rearrange("p b (i j) -> p b i j", j=CH)[:, :, :, 0:HC]
                  for x in (Lf, Xf)]
        Yt = sb("lane_Yt", [P, HC, HC])
        bX = sb("lane_bX", [P, CH, CH])
        lprod = sb("lane_prod", [P, max(GR * CH * DH, HC * HC * HC // 2)])
        ident3 = sb("ident3", [P, P])
        identb = sb("identb", [P, P], BF16)
        future = sb("future", [P, 2, P], BF16)
        ones3 = sb("ones3", [P, 3, P])
        keep = sb("keep", [P, 3, P])
        Ms = sb("Ms", [P, NM, HG, MW])
        Ys = sb("Ys", [P, HG, HB])
        X64 = sb("X64", [P, HG, HB])
        nb = sb("nb", [P, NA, HG, HP + P])
        Qz = sb("Qz", [P, NG, NA, HG, P])
        Wz = sb("Wz", [P, NG, NA, HG, P])
        khat = sb("khat", [P, P])
        qhat = sb("qhat", [P, HG, P])
        nm = sb("nm", [P, HG])
        Ps = sb("Ps", [P, HG, 2 * P])
        PTs = sb("PTs", [P, HG, 2, P])
        rec = sb("rec", [P, HG])
        Os = sb("Os", [P, NA, D])
        OT = sb("OT", [P, KC, T])
        h2s = sb("h2s", [P, NA, D])

        pG = ps("pG", [P, 512])
        pY = ps("pY", [P, 512])
        pC = ps("pC", [P, 2, 512])
        pS = ps("pS", [P, 2, 512])
        pT = ps("pT", [P, 2, 512])

        loaded, cleared, consts = sig("loaded"), sig("cleared", 6), sig("consts")
        f_in, x_in, tm_in, h_in = [sig(f"f_in{i}", 9 * 16) for i in range(NG)], [sig(f"x_in{i}", 16 * 16) for i in range(NG)], sig("tm_in", 16), sig("h_in", 16)
        copied, w_in, gram, masked = sig("copied", 3), sig("w_in", NS), sig("gram", NS * HG), sig("masked", NS * HG)

        def two(name):
            return [sig(f"{name}{i}", NS) for i in range(2)]

        y_p, y_s, xy_p, x64 = sig("y_p", NS), sig("y_s", NS), sig("xy_p", NS), sig("x64", NS)
        top_p, top = two("top_p"), two("top")
        rhs_p, rhs, low_p, low = two("rhs_p"), two("rhs"), two("low_p"), two("low")
        hat_p, hat, score, peak, weight = two("hat_p"), two("hat"), two("score"), two("peak"), two("weight")
        wT_p, wT, out_p, inv, outs = two("wT_p"), two("wT"), two("out_p"), two("inv"), two("outs")
        oT_p, oT, y_out, h2, h2_out = sig("oT_p"), sig("oT"), sig("y_out"), sig("h2"), sig("h2_out", 16)
        pe_passed, pool_passed = sig("pe_passed"), sig("pool_passed")
        lane_in, lane_first, lane_prod, lane_sum = sig("lane_in", 16 * NCB), sig("lane_first", 4), sig("lane_prod", NL), sig("lane_sum", NL)
        lane_done, lane_out = sig("lane_done"), sig("lane_out", 32)

        block = ctx.enter_context(nc.Block())

        def load_group(sp, it, g):
            sp.dma_start(Fs[:, g].rearrange("p a m t -> p (a m t)"),
                         F_d[DS(it, 1), :, g * NA * 3 * P:(g + 1) * NA * 3 * P].rearrange("o p n -> p (o n)")).then_inc(f_in[g].sem, 16)
            heads = F_d[DS(it, 1)].rearrange("o p (g a m t) -> p (o g) a m t", g=NG, a=NA, m=3)
            for dst, m in ((Qz, 1), (Wz, 2)):
                for h in range(HG):
                    r = slice(HP * h, HP * (h + 1))
                    sp.dma_start(dst[r, g, :, h, :], heads[r, g, :, m, :]).then_inc(f_in[g].sem, 16)
            for dst, src in ((XTs, xt_d), (BXs, bx_d)):
                chunks = src[DS(it, 1)].rearrange("o c h s t -> (o c) s h t")
                for n in range(T // CH):
                    a, c = divmod(n, P // CH)
                    sp.dma_start(dst[CH * c:CH * (c + 1), a, HG * g:HG * (g + 1), CH * (c % 2):CH * (c % 2 + 1)],
                                 chunks[n, :, HG * g:HG * (g + 1), :]).then_inc(x_in[g].sem, 16)

        def rows_of(x, it):
            return x[DS(it, 1)].rearrange("o (a p) n -> p (o a) n", p=P)

        def load_lanes(sp, n):
            rows = tm_d[DS(n, 1), :, 0:V0].rearrange("o (c t) (h e) -> (o c) h t e", t=CH, e=WB)
            for c in range(NCB):
                sp.dma_start(lw[H * c:H * (c + 1)], rows[c]).then_inc(lane_in.sem, 16)

        def store_lanes(sp, n):
            for dst, src in ((xt_d, Xt), (bx_d, bX[:])):
                sp.dma_start(dst[DS(n, 1)].rearrange("o c h s t -> (o c h) (s t)"), src.rearrange("p s t -> p (s t)")).then_inc(lane_out.sem, 16)

        @block.sync
        def _(sp):
            load_lanes(sp, 0)
            for n in range(2):
                wait(sp, n, lane_sum, NGR)
                load_lanes(sp, n + 1)
                wait(sp, n, lane_done, 1)
                store_lanes(sp, n)
            wait(sp, 0, lane_out, 32)
            sp.dma_start(wo_s[:], wo.rearrange("(c p) n -> p c n", p=P)).then_inc(loaded.sem, 16)
            sp.dma_start(tms[:], rows_of(tm_d, 0)).then_inc(tm_in.sem, 16)
            sp.dma_start(hres[:], rows_of(h_d, 0)).then_inc(h_in.sem, 16)
            sp.wait_ge(cleared.sem, cleared.count(9))
            for g in range(NG):
                load_group(sp, 0, g)
            with sp.Fori(0, B) as it:
                wait(sp, it, copied, 3)
                sp.dma_start(tms[:], rows_of(tm_d, (it + 1) % B)).then_inc(tm_in.sem, 16)
                wait(sp, it + 1, lane_out, 32)
                for g in range(NG):
                    if g == NG - 1:
                        wait(sp, it + 2, lane_done, 1)
                        store_lanes(sp, (it + 2) % B)
                    wait(sp, it, score[0], NA * (g + 1))
                    wait(sp, it, score[1], NA * (g + 1))
                    wait(sp, it, hat[0], NA * (g + 1))
                    wait(sp, it, hat[1], NA * (g + 1))
                    load_group(sp, (it + 1) % B, g)
                    if g == 1:
                        wait(sp, it + 2, lane_sum, NGR)
                        load_lanes(sp, (it + 3) % B)
                wait(sp, it, h2, 1)
                sp.dma_start(rows_of(h2_d, it), h2s[:]).then_inc(h2_out.sem, 16)
                sp.dma_start(hres[:], rows_of(h_d, (it + 1) % B)).then_inc(h_in.sem, 16)
            sp.wait_ge(h2_out.sem, h2_out.count(16 * B))
            sp.wait_ge(h_in.sem, h_in.count(16 * (B + 1)))
            sp.wait_ge(lane_out.sem, lane_out.count(32 * (B + 2)))
            sp.wait_ge(lane_in.sem, lane_in.count(16 * NCB * (B + 3)))
            for g in range(NG):
                sp.wait_ge(f_in[g].sem, f_in[g].count(144 * (B + 1)))
                sp.wait_ge(x_in[g].sem, x_in[g].count(256 * (B + 1)))

        def read_before(k, early):
            return k + 1 - NM if early else max(0, k + 1 - NM)

        @block.gpsimd
        def _(pool):
            start(pool, signals)
            for x in (XTs, BXs, Ms, nb, ident3, Qz, Wz, qhat):
                pool.memset(x[:], 0.0).then_inc(cleared.sem, 1)
            pool.memset(va[:, :, :, DH:DH + 1], 1.0).then_inc(cleared.sem, 1)
            pool.memset(ones3[:], 1.0).then_inc(consts.sem, 1)
            pool.memset(future[:], 0.0).then_inc(consts.sem, 1)
            pool.wait_ge(cleared.sem, cleared.count(9))
            pool.wait_ge(consts.sem, consts.count(2))
            pool.affine_select(out=ident3[:], in_=ident3[:], compare_op=ALU.not_equal, fill=1.0, base=0,
                               pattern=[[-1, P]], channel_multiplier=1).then_inc(consts.sem, 1)
            pool.affine_select(out=keep[:, 0, :], in_=ones3[:, 0, :], compare_op=ALU.is_gt, fill=0.0, base=0,
                               pattern=[[-1, P]], channel_multiplier=1).then_inc(consts.sem, 1)
            pool.affine_select(out=keep[:, 1, :], in_=ones3[:, 1, :], compare_op=ALU.is_ge, fill=0.0, base=0,
                               pattern=[[1, P]], channel_multiplier=-1).then_inc(consts.sem, 1)
            pool.affine_select(out=keep[:, 2, :].rearrange("p (c t) -> p c t", t=CH), in_=ones3[:, 2, :].rearrange("p (c t) -> p c t", t=CH),
                               compare_op=ALU.is_gt, fill=0.0, base=0, pattern=[[CH, P // CH], [0, CH]], channel_multiplier=-1).then_inc(consts.sem, 1)
            pool.affine_select(out=future[:], in_=future[:], compare_op=ALU.is_ge, fill=-1e30, base=0,
                               pattern=[[0, 2], [-1, P]], channel_multiplier=1).then_inc(consts.sem, 1)
            pool.wait_ge(consts.sem, consts.count(7))
            pool.tensor_copy(identb[:], ident3[:]).then_inc(consts.sem, 1)
            pool.wait_ge(consts.sem, consts.count(8))

            def rows_in(n, before):
                pool.wait_ge(tm_in.sem, tm_in.count(n * 16 + 16))
                wait(pool, n, low[0], 0)
                wait_apart(pool, n, low[1], 0, pool_passed)
                pool.tensor_scalar(nbeta[:], tmw[:, :, :, DH], -1.0, None, ALU.mult).then_inc(copied.sem, 1)
                wait_apart(pool, n, w_in, 0, pool_passed)
                pool.tensor_copy(wt[:], tmw[:, :, :, 0:DH]).then_inc(copied.sem, 1)
                before()
                wait(pool, n, out_p[0], 0)
                wait_apart(pool, n, out_p[1], 0, pool_passed)
                pool.tensor_copy(va[:, :, :, 0:DH], tms[:, :, V0:TM].rearrange("p a (h d) -> p a h d", d=DH)).then_inc(copied.sem, 1)

            def w_into(n, k):
                g, a = divmod(k, NA)
                if k == 0:
                    wait(pool, n, copied, 2)
                if k >= NA or not isinstance(n, int):
                    wait(pool, n, score[0], read_before(k, k == 0))
                    wait(pool, n, score[1], read_before(k, k == 0))
                pool.tensor_tensor(out=Ms[:, k % NM, :, W0:W0 + DH], in0=wt[:, a, HG * g:HG * (g + 1), :],
                                   in1=ones3[:, 0, 0:1].unsqueeze(2).broadcast_to([P, HG, DH]), op=ALU.mult).then_inc(w_in.sem, 1)

            rows_in(0, lambda: w_into(0, 0))
            with pool.Fori(0, B) as it:
                for k in range(1, NS):
                    w_into(it, k)
                rows_in(it + 1, lambda: w_into(it + 1, 0))

        def steps(it, step):
            for k in range(1, NS + 1):
                front = (it, k + 1) if k + 1 < NS else (it + 1, k + 1 - NS)
                middle = (it, k) if k < NS else (it + 1, 0)
                step(front, middle, (it, k - 1))

        def first_steps(step):
            step((0, 0), None, None)
            step((0, 1), (0, 0), None)

        def each(f):
            f(0)
            f(1)

        def c0(k):
            return R0 if k % NA == 0 else W0

        @block.tensor
        def _(pe):
            mm = nc.tensor.matmul
            pe.wait_ge(consts.sem, consts.count(8))
            pe.wait_ge(loaded.sem, loaded.count(16))
            if True:
                def gram_of(it, k, h):
                    g, a = divmod(k, NA)
                    if a == 0 and h == 0:
                        pe.wait_ge(f_in[g].sem, f_in[g].count(it * 144 + 144))
                        pe.wait_ge(x_in[g].sem, x_in[g].count(it * 256 + 256))
                    wait(pe, it, masked, HG * k + h)
                    mm(pG[:, 0:3 * P], Wz[:, g, a, h, :], Fs[:, g, a, :, :].rearrange("p m t -> p (m t)"),
                       start=True, stop=True).then_inc(gram.sem, 1)

                def blocks(f):
                    for h in range(HG):
                        for r in (slice(0, HB), slice(HB, P)):
                            last = f(h, r)
                    return last

                def y_of(it, k):
                    g, a = divmod(k, NA)
                    wait(pe, it, masked, HG * (k + 1))
                    wait_apart(pe, it, x64, k, pe_passed)
                    blocks(lambda h, r: mm(pY[r, h * HB:(h + 1) * HB], Ms[r, k % NM, h, G0 + r.start:G0 + r.stop],
                                           BXs[r, a, HG * g + h, :], start=True, stop=True)).then_inc(y_p.sem, 1)

                def xy_of(it, k):
                    g, a = divmod(k, NA)
                    wait_apart(pe, it, y_s, k + 1, pe_passed)
                    blocks(lambda h, r: mm(pY[r, h * HB:(h + 1) * HB], Ys[r, h, :],
                                           XTs[r, a, HG * g + h, :], start=True, stop=True)).then_inc(xy_p.sem, 1)

                def top_of(it, k, pr):
                    a = k % NA
                    wait(pe, it, x64, k + 1)
                    wait(pe, it, hat[pr], k)
                    wait_apart(pe, it, w_in, k + 1, pe_passed)
                    for hh in range(2):
                        last = mm(pC[0:HB, pr, 160 * hh + c0(k):160 * hh + R0 + HB], X64[0:HB, 2 * pr + hh, :],
                                  Ms[0:HB, k % NM, 2 * pr + hh, c0(k):R0 + HB], start=True, stop=True)
                    last.then_inc(top_p[pr].sem, 1)

                def rhs_of(it, k, pr):
                    wait_apart(pe, it, top[pr], k + 1, pe_passed)
                    for hh in range(2):
                        last = mm(pC[HB:P, pr, 160 * hh + c0(k):160 * hh + R0 + HB], Ms[0:HB, k % NM, 2 * pr + hh, G0 + HB:G0 + P],
                                  nb[0:HB, k % NA, 2 * pr + hh, c0(k):R0 + HB], start=True, stop=True)
                    last.then_inc(rhs_p[pr].sem, 1)

                def low_of(it, k, pr):
                    wait_apart(pe, it, rhs[pr], k + 1, pe_passed)
                    for hh in range(2):
                        last = mm(pC[HB:P, pr, 160 * hh + c0(k):160 * hh + R0 + P], X64[HB:P, 2 * pr + hh, :],
                                  Ms[HB:P, k % NM, 2 * pr + hh, c0(k):R0 + P], start=True, stop=True)
                    last.then_inc(low_p[pr].sem, 1)

                def hat_of(it, k, pr):
                    wait(pe, it, low[pr], k + 1)
                    for h in (2 * pr, 2 * pr + 1):
                        if k % NA == 0:
                            l, r = Ms[:, k % NM, h, W0:W0 + HP], nb[:, k % NA, h, R0:R0 + P]
                        else:
                            l, r = nb[:, k % NA, h, W0:W0 + HP], Ms[:, k % NM, h, Q0:Q0 + P]
                        last = mm(pC[HP * h:HP * (h + 1), pr, 0:P], l, r, start=True, stop=True, tile_position=(0, HP * h))
                    last.then_inc(hat_p[pr].sem, 1)

                def score_of(it, k, pr):
                    g, a = divmod(k, NA)
                    wait(pe, it, weight[pr], k)
                    sc = pS[:, pr, :].rearrange("p (h j) -> p h j", h=2)
                    mm(sc[:, :, P:2 * P], identb[:], future[:], start=True, stop=False)
                    for hh in range(2):
                        h = 2 * pr + hh
                        mm(sc[:, hh, P:2 * P], Qz[:, g, a, h, :], Fs[:, g, a, 0, :], start=False, stop=False)
                        last = mm(sc[:, hh, P:2 * P], Ms[:, k % NM, h, Q0:Q0 + P], nb[:, k % NA, h, R0:R0 + P], start=False, stop=(hh == 1 and a == 0))
                    if a == 1:
                        wait(pe, it, hat[0], k + 1)
                        wait(pe, it, hat[1], k + 1)
                        for hh in range(2):
                            last = mm(sc[:, hh, 0:P], qhat[:, 2 * pr + hh, :], khat[:], start=False, stop=(hh == 1))
                    last.then_inc(score[pr].sem, 1)

                def weights_T(it, k, pr):
                    a = k % NA
                    wait(pe, it, weight[pr], k + 1)
                    if k == 0:
                        wait(pe, it, oT, 0)
                        wait(pe, it, h2, 0)
                    wait(pe, it, outs[pr], k)
                    for hh in range(2):
                        for j in range(1 - a, 2):
                            last = pe.transpose(pT[:, pr, (2 * hh + j) * P:(2 * hh + j + 1) * P], Ps[:, 2 * pr + hh, j * P:(j + 1) * P], ident3[:])
                    last.then_inc(wT_p[pr].sem, 1)

                def out_of(it, k, pr):
                    g, a = divmod(k, NA)
                    wait(pe, it, wT[pr], k + 1)
                    if k == 0:
                        wait(pe, it, copied, 3)
                    for hh in range(2):
                        for j in range(1 - a, 2):
                            jt = j - 1 + a
                            last = mm(pT[:, pr, hh * HP:hh * HP + DH + 1], PTs[:, 2 * pr + hh, j, :], va[:, jt, HG * g + 2 * pr + hh, :],
                                      start=(j == 1 - a), stop=(j == 1))
                    last.then_inc(out_p[pr].sem, 1)

                def outs_T(it):
                    wait(pe, it, outs[0], NS)
                    wait(pe, it, outs[1], NS)
                    for c in range(KC):
                        for a in range(NA):
                            last = pe.transpose(pT[:, 0, c * T + a * P:c * T + (a + 1) * P], Os[:, a, c * P:(c + 1) * P], ident3[:])
                    last.then_inc(oT_p.sem, 1)

                def through_wo(it):
                    wait(pe, it, oT, 1)
                    for a in range(NA):
                        for c in range(KC):
                            last = mm(pT[:, 1, a * D:(a + 1) * D], OT[:, c, a * P:(a + 1) * P], wo_s[:, c, :], start=(c == 0), stop=(c == KC - 1))
                    last.then_inc(y_out.sem, 1)

                def step(front, middle, soft):
                    gram_of(*front, 0)
                    if soft:
                        score_of(*soft, 0)
                    if middle:
                        each(lambda pr: top_of(*middle, pr))
                    gram_of(*front, 1)
                    if soft:
                        score_of(*soft, 1)
                    if middle:
                        each(lambda pr: rhs_of(*middle, pr))
                    gram_of(*front, 2)
                    if soft:
                        weights_T(*soft, 0)
                    if middle:
                        each(lambda pr: low_of(*middle, pr))
                    gram_of(*front, 3)
                    if soft:
                        weights_T(*soft, 1)
                    if middle:
                        each(lambda pr: hat_of(*middle, pr))
                    y_of(*front)
                    if soft:
                        out_of(*soft, 0)
                    xy_of(*front)
                    if soft:
                        out_of(*soft, 1)

                first_steps(step)
                with pe.Fori(0, B) as it:
                    steps(it, step)
                    outs_T(it)
                    through_wo(it)

        PRODUCTS = ([("gram", b, GR * GR * (b + 1) * DH) for b in range(NGR)] + [("solve", t, 2 * t * t) for t in range(1, HC)]
                    + [(kind, half, HC * HC * (HC // 2) // (1 + small)) for kind, half, small in
                       (("left", 0, 0), ("left", 1, 1), ("right", 0, 1), ("right", 1, 0))])
        LANES = ([("first", 0, None, 0, 1200)] + [(what, n, kind, t, size + 100) for n, (kind, t, size) in enumerate(PRODUCTS) for what in ("product", "sums")]
                 + [("last", 0, None, 0, 1100)])
        LANE_COST = sum(step[-1] for step in LANES)

        @block.vector
        def _(dve):
            def lane_operands(kind, t):
                q = HC // 2
                if kind == "gram":
                    n = GR * (t + 1)
                    sizes = [P, GR, n, DH]
                    one, other = lnbw[:, None, 0:n, :], lw[:, GR * t:n, 0:DH].unsqueeze(2)
                    to = L[:, GR * t:n, 0:n]
                elif kind == "solve":
                    sizes = [P, 2, t, t]
                    one, other = Xd[:, :, 0:t, 0:t], Ld[:, :, t:t + 1, 0:t]
                    to = Xd[:, :, 0:t, t]
                elif kind == "left":
                    js, ss = slice(q * t, q * (t + 1)), slice(q * t, HC)
                    sizes = [P, q, HC, HC - q * t]
                    one, other = Xt[:, js, ss].unsqueeze(2), L[:, None, HC:CH, ss]
                    to = Yt[:, js, :]
                else:
                    sizes = [P, HC, q, q * (t + 1)]
                    one = Yt[:, :, 0:q * (t + 1)].unsqueeze(2)
                    i = slice(HC + q * t, HC + q * (t + 1))
                    other = Xt[:, HC:HC + q * (t + 1), i].rearrange("p r i -> p i r").unsqueeze(1)
                    to = Xt[:, 0:HC, i]
                a, b, c = sizes[1:]
                place = lprod[:, 0:a * b * c].rearrange("p (a b c) -> p a b c", b=b, c=c)
                return one.broadcast_to(sizes), other.broadcast_to(sizes), place, to

            def lane_step(n, what, i, kind, t):
                if what == "first":
                    wait(dve, n, lane_in, 16 * NCB)
                    wait(dve, n, lane_out, 0)
                    dve.scalar_tensor_tensor(out=lnbw[:], in0=lw[:, :, 0:DH], scalar=-1.0, in1=lw[:, :, DH:WB].broadcast_to([P, CH, DH]),
                                             op0=ALU.mult, op1=ALU.mult).then_inc(lane_first.sem, 1)
                    dve.tensor_copy(lbeta[:], lw[:, :, DH]).then_inc(lane_first.sem, 1)
                    dve.memset(Xf[:], 0.0).then_inc(lane_first.sem, 1)
                    wait(dve, n, lane_first, 3)
                    dve.memset(Xf[:, 0:CH * CH:CH + 1], 1.0).then_inc(lane_first.sem, 1)
                elif what == "product":
                    one, other, place, _ = lane_operands(kind, t)
                    if i == 0:
                        wait(dve, n, lane_first, 4)
                    wait(dve, n, lane_sum, i)
                    dve.tensor_tensor(place, one, other, ALU.mult).then_inc(lane_prod.sem, 1)
                elif what == "sums":
                    _, _, place, to = lane_operands(kind, t)
                    wait(dve, n, lane_prod, i + 1)
                    dve.reduce_sum(to, place, X).then_inc(lane_sum.sem, 1)
                else:
                    wait(dve, n, lane_sum, NL)
                    dve.tensor_tensor(bX[:], Xt.rearrange("p s t -> p t s"), lbeta[:].unsqueeze(2).broadcast_to([P, CH, CH]),
                                      ALU.mult).then_inc(lane_done.sem, 1)

            def lane_steps(n, lo, hi):
                at = 0
                for what, i, kind, t, cost in LANES:
                    if lo * LANE_COST <= at < hi * LANE_COST:
                        lane_step(n, what, i, kind, t)
                    at += cost

            with dve.Fori(0, 2) as n:
                lane_steps(n, 0, 1)
            dve.wait_ge(consts.sem, consts.count(8))
            if True:

                def peak_of(it, k, pr):
                    a = k % NA
                    wait(dve, it, score[pr], k + 1)
                    sc = pS[:, pr, :].rearrange("p (h j) -> p h j", h=2)
                    dve.tensor_reduce(out=nm[:, 2 * pr:2 * pr + 2], in_=sc[:, :, (1 - a) * P:2 * P], axis=X, op=ALU.max, negate=True).then_inc(peak[pr].sem, 1)

                def mask(it, k, h):
                    wait(dve, it, gram, HG * k + h + 1)
                    if k >= NA or not isinstance(it, int):
                        wait(dve, it, score[h // 2], read_before(k, k < NA))
                    dve.tensor_tensor(Ms[:, k % NM, h, R0:MW], pG[:, 0:3 * P], keep[:].rearrange("p m t -> p (m t)"), ALU.mult).then_inc(masked.sem, 1)

                def x64_of(it, k):
                    g, a = divmod(k, NA)
                    wait(dve, it, xy_p, k + 1)
                    dve.tensor_tensor(X64[:], XTs[:, a, HG * g:HG * (g + 1), :],
                                      pY[:, 0:HG * HB].rearrange("p (h t) -> p h t", h=HG), ALU.subtract).then_inc(x64.sem, 1)

                def rhs_of(it, k, pr):
                    wait(dve, it, rhs_p[pr], k + 1)
                    m = Ms[HB:P, k % NM, 2 * pr:2 * pr + 2, c0(k):R0 + HB]
                    dve.tensor_tensor(m, pC[HB:P, pr, 0:320].rearrange("p (h n) -> p h n", h=2)[:, :, c0(k):R0 + HB], m, ALU.add).then_inc(rhs[pr].sem, 1)

                def hat_of(it, k, pr):
                    g, a = divmod(k, NA)
                    r = slice(2 * HP * pr, 2 * HP * (pr + 1))
                    wait(dve, it, hat_p[pr], k + 1)
                    if a == 0:
                        wait(dve, it, score[0], k)
                        wait(dve, it, score[1], k)
                        last = dve.tensor_tensor(khat[r, :], pC[r, pr, 0:P], Fs[r, g, 0, 0, :], ALU.add)
                    else:
                        for h in (2 * pr, 2 * pr + 1):
                            r = slice(HP * h, HP * (h + 1))
                            last = dve.tensor_tensor(qhat[r, h, :], pC[r, pr, 0:P], Fs[r, g, 1, 1, :], ALU.add)
                    last.then_inc(hat[pr].sem, 1)

                def outs_of(it, k, pr):
                    g, a = divmod(k, NA)
                    o = pT[:, pr, 0:2 * HP].rearrange("p (h n) -> p h n", h=2)
                    wait(dve, it, out_p[pr], k + 1)
                    dve.reciprocal(rec[:, 2 * pr:2 * pr + 2], o[:, :, DH]).then_inc(inv[pr].sem, 1)
                    wait(dve, it, inv[pr], k + 1)
                    at = DH * (HG * g + 2 * pr)
                    dve.tensor_tensor(Os[:, a, at:at + 2 * DH].rearrange("p (h d) -> p h d", d=DH), o[:, :, 0:DH],
                                      rec[:, 2 * pr:2 * pr + 2].unsqueeze(2).broadcast_to([P, 2, DH]), ALU.mult).then_inc(outs[pr].sem, 1)

                def h2_of(it):
                    wait(dve, it, y_out, 1)
                    wait(dve, it, h2_out, 0)
                    dve.wait_ge(h_in.sem, h_in.count(it * 16 + 16))
                    dve.tensor_tensor(h2s[:], pT[:, 1, :].rearrange("p (a n) -> p a n", a=NA), hres[:], ALU.add).then_inc(h2.sem, 1)

                def step(front, middle, soft):
                    if soft:
                        it, k = soft

                        def lanes(lo, hi):
                            if k > 0:
                                lane_steps(it + 2, (k - 1 + lo) / (NS - 1), (k - 1 + hi) / (NS - 1))
                    else:
                        def lanes(lo, hi):
                            pass
                    mask(*front, 0)
                    lanes(0.0,0.3)
                    mask(*front, 1)
                    if soft:
                        peak_of(*soft, 0)
                        peak_of(*soft, 1)
                    if middle:
                        rhs_of(*middle, 0)
                        rhs_of(*middle, 1)
                    mask(*front, 2)
                    lanes(0.3,0.4)
                    mask(*front, 3)
                    lanes(0.4,0.65)
                    if middle:
                        hat_of(*middle, 0)
                        hat_of(*middle, 1)
                    if soft:
                        outs_of(*soft, 0)
                    lanes(0.65,0.75)
                    if soft:
                        outs_of(*soft, 1)
                    x64_of(*front)
                    lanes(0.75,1.0)

                first_steps(step)
                with dve.Fori(0, B) as it:
                    steps(it, step)
                    h2_of(it)

        @block.scalar
        def _(act):
            act.wait_ge(consts.sem, consts.count(8))
            if True:
                def weight_of(it, k, pr):
                    a = k % NA
                    wait(act, it, peak[pr], k + 1)
                    for hh in range(2):
                        h = 2 * pr + hh
                        last = act.activation(Ps[:, h, (1 - a) * P:2 * P], pS[:, pr, (2 * hh + 1 - a) * P:(2 * hh + 2) * P], ACT.Exp, bias=nm[:, h:h + 1])
                    last.then_inc(weight[pr].sem, 1)

                def y_of(it, k):
                    wait(act, it, y_p, k + 1)
                    act.activation(Ys[:].rearrange("p h t -> p (h t)"), pY[:, 0:HG * HB], ACT.Copy).then_inc(y_s.sem, 1)

                def wT_of(it, k, pr):
                    a = k % NA
                    wait(act, it, wT_p[pr], k + 1)
                    act.activation(PTs[:, 2 * pr:2 * pr + 2, 1 - a:2, :], pT[:, pr, :].rearrange("p (h j t) -> p h j t", h=2, j=2)[:, :, 1 - a:2, :],
                                   ACT.Copy).then_inc(wT[pr].sem, 1)

                def scaled_of(it, k, pr, rows, cols, before, after):
                    g, a = divmod(k, NA)
                    wait(act, it, before[pr], k + 1)
                    if k == 0:
                        wait(act, it, copied, 1)
                    for hh in range(2):
                        h = 2 * pr + hh
                        last = act.activation(nb[rows, a, h, cols], pC[rows, pr, 160 * hh + cols.start:160 * hh + cols.stop], ACT.Copy,
                                              scale=nbeta[rows, a, HG * g + h:HG * g + h + 1])
                    last.then_inc(after[pr].sem, 1)

                def top_of(it, k, pr):
                    scaled_of(it, k, pr, slice(0, HB), slice(c0(k), R0 + HB), top_p, top)

                def low_of(it, k, pr):
                    scaled_of(it, k, pr, slice(HB, P), slice(c0(k), R0 + P), low_p, low)

                def step(front, middle, soft):
                    if middle:
                        top_of(*middle, 0)
                        top_of(*middle, 1)
                    if soft:
                        weight_of(*soft, 0)
                        weight_of(*soft, 1)
                        wT_of(*soft, 0)
                    if middle:
                        low_of(*middle, 0)
                        low_of(*middle, 1)
                    y_of(*front)
                    if soft:
                        wT_of(*soft, 1)

                first_steps(step)
                with act.Fori(0, B) as it:
                    steps(it, step)
                    wait(act, it, oT_p, 1)
                    act.activation(OT[:].rearrange("p c t -> p (c t)"), pT[:, 0, :], ACT.Copy).then_inc(oT.sem, 1)


def experts(nc, sems, h2_d, w12, w3, wg, bias, out):
    NU = E1 * NHT
    MID = 4
    with ExitStack() as ctx:
        sb, ps = sbufs(nc, ctx), psums(nc, ctx)

        signals = []

        def sig(name, per=1):
            signals.append(Signal(nc, sems, "p4_" + name, per))
            return signals[-1]

        W12 = sb("W12", [P, E1, KC, 2, NHT * HT])
        W3 = sb("W3", [HT, E1, NHT, D])
        wg_s = sb("wg_s", [P, KC, NE])
        bias_s = sb("bias_s", [P, NE])
        ident4 = sb("ident4", [P, P])
        lower = sb("lower", [P, NE, NE])
        h2s = sb("h2in", [P, NA, D])
        st = sb("st4", [P, NA, 6])
        mv = sb("mv4", [P, NA, 2])
        ve = sb("ve4", [P, NA])
        lnv = sb("lnv4", [P, NA])
        rstd = sb("rstd4", [P, NA])
        xn = sb("xn4", [P, NA, D])
        xT = sb("xT4", [P, KC, T])
        gl = sb("gl", [P, NA, NE])
        cmp = sb("cmp", [P, 3, NA, NE, NE])
        rank = sb("rank", [P, NA, NE])
        top = sb("topmask", [P, NA, NE])
        mx = sb("mx", [P, NA])
        ge = sb("ge", [P, NA, NE])
        gx = sb("gx", [P, NA, NE])
        gm = sb("gmask", [P, NA, NE])
        gs = sb("gs", [P, NA])
        gr = sb("gr", [P, NA])
        route = sb("route", [P, NA, NE])
        sl = sb("sl", [HT, 3, T])
        gT = sb("gT", [HT, 3, NHT, T])
        acc = sb("acc", [P, 2, NA, D])
        zero4, step4 = sb("zero4", [P, 1]), sb("step4", [P, 1])

        pU = ps("pU", [P, 3, 2, T])
        pD = ps("pD", [P, 3, NA, D])
        pX = ps("pX4", [P, KC, T])
        pR = ps("pR", [P, NA, NE])

        loaded, consts = sig("loaded"), sig("consts")
        w_in = [sig(f"w_in{e}") for e in range(E1)]
        h2_in, mean, ln_r, normed, xt_p, xt = sig("h2_in", 16), sig("mean", 5), sig("ln_r", 2), sig("normed", NA), sig("xt_p"), sig("xt")
        gate, router, gexp = sig("gate"), sig("router", 12), sig("gexp")
        up, silu, hidden = sig("up", NU), sig("silu", NU), sig("hidden", NU)
        down, summed, stored = sig("down", E1), sig("summed", NA * E1), sig("stored", 16)
        block = ctx.enter_context(nc.Block())

        def rows_of(x, it):
            return x[DS(it, 1)].rearrange("o (a p) n -> p (o a) n", p=P)

        @block.sync
        def _(sp):
            sp.dma_start(wg_s[:], wg.rearrange("(c p) n -> p c n", p=P)).then_inc(loaded.sem, 16)
            sp.dma_start(bias_s[:], bias.partition_broadcast(P)).then_inc(loaded.sem, 16)
            sp.dma_start(h2s[:], rows_of(h2_d, 0)).then_inc(h2_in.sem, 16)
            for e in range(E1):
                sp.dma_start(W12[:, e].rearrange("p c m n -> p (c m n)"), w12[:, e, :]).then_inc(w_in[e].sem, 16)
                sp.dma_start(W3[:, e].rearrange("p t n -> p (t n)"), w3[:, e, :]).then_inc(w_in[e].sem, 16)
            with sp.Fori(0, B) as it:
                wait(sp, it, summed, NA)
                sp.dma_start(h2s[:], rows_of(h2_d, (it + 1) % B)).then_inc(h2_in.sem, 16)
                wait(sp, it, summed, NA * E1)
                sp.dma_start(rows_of(out, it), acc[:, 0]).then_inc(stored.sem, 16)
            sp.wait_ge(stored.sem, stored.count(16 * B))

        @block.gpsimd
        def _(pool):
            start(pool, signals)
            pool.memset(zero4[:], 0.0).then_inc(consts.sem, 1)
            pool.memset(ident4[:], 0.0).then_inc(consts.sem, 1)
            pool.memset(lower[:], 1.0).then_inc(consts.sem, 1)
            pool.wait_ge(consts.sem, consts.count(3))
            pool.affine_select(out=ident4[:], in_=ident4[:], compare_op=ALU.not_equal, fill=1.0, base=0,
                               pattern=[[-1, P]], channel_multiplier=1).then_inc(consts.sem, 1)
            pool.affine_select(out=lower[:], in_=lower[:], compare_op=ALU.is_gt, fill=0.0, base=0,
                               pattern=[[1, NE], [-1, NE]], channel_multiplier=0).then_inc(consts.sem, 1)

        @block.tensor
        def _(pe):
            mm = nc.tensor.matmul

            def transposes():
                for c in range(KC):
                    for a in range(NA):
                        last = pe.transpose(pX[:, c, a * P:(a + 1) * P], xn[:, a, c * P:(c + 1) * P], ident4[:])
                return last

            pe.wait_ge(consts.sem, consts.count(5))
            pe.wait_ge(loaded.sem, loaded.count(32))
            pe.wait_ge(normed.sem, normed.count(NA))
            transposes().then_inc(xt_p.sem, 1)
            with pe.Fori(0, B) as it:
                def up_of(e):
                    pe.wait_ge(w_in[e].sem, w_in[e].count(32))
                    for t in range(NHT):
                        n = NHT * e + t
                        wait(pe, it, hidden, max(0, n - 2))
                        for m in range(2):
                            for c in range(KC):
                                last = mm(pU[0:HT, n % 3, m, :], W12[:, e, c, m, t * HT:(t + 1) * HT], xT[:, c, :],
                                          start=(c == 0), stop=(c == KC - 1))
                        last.then_inc(up.sem, 1)

                def down_of(e):
                    wait(pe, it, hidden, NHT * (e + 1))
                    wait(pe, it, summed, max(0, NA * (e - 2)))
                    for a in range(NA):
                        for t in range(NHT):
                            last = mm(pD[:, e % 3, a, :], gT[:, e % 3, t, a * P:(a + 1) * P], W3[:, e, t, :],
                                      start=(t == 0), stop=(t == NHT - 1))
                    last.then_inc(down.sem, 1)

                wait(pe, it, xt, 1)
                wait(pe, it, router, 0)
                for a in range(NA):
                    for c in range(KC):
                        last = mm(pR[:, a, :], xT[:, c, a * P:(a + 1) * P], wg_s[:, c, :], start=(c == 0), stop=(c == KC - 1))
                last.then_inc(gate.sem, 1)
                for e in range(E1):
                    up_of(e)
                    if e:
                        down_of(e - 1)
                    if e == MID + 1:
                        pe.wait_ge(normed.sem, normed.count((it + 2) * NA))
                        transposes().then_inc(xt_p.sem, 1)
                down_of(E1 - 1)

        @block.vector
        def _(dve):
            def stats(it):
                dve.wait_ge(h2_in.sem, h2_in.count(it * 16 + 16))
                for a in range(NA):
                    dve.bn_stats(st[:, a, :], h2s[:, a, :]).then_inc(mean.sem, 1)
                wait(dve, it, mean, NA)
                dve.tensor_copy(step4[:], zero4[:])
                for a in range(NA):
                    dve.bn_aggr(mv[:, a, :], st[:, a, :]).then_inc(mean.sem, 1)
                wait(dve, it, mean, 2 * NA)
                dve.tensor_scalar(ve[:], mv[:, :, 1], 1e-5, None, ALU.add).then_inc(mean.sem, 1)

            def norm(it):
                wait(dve, it, ln_r, 2)
                wait(dve, it, xt_p, 0)
                for a in range(NA):
                    dve.tensor_scalar(xn[:, a, :], h2s[:, a, :], mv[:, a, 0:1], rstd[:, a:a + 1],
                                      ALU.subtract, ALU.mult).then_inc(normed.sem, 1)

            dve.wait_ge(consts.sem, consts.count(5))
            dve.wait_ge(loaded.sem, loaded.count(32))
            stats(0)
            norm(0)
            with dve.Fori(0, B) as it:
                def hidden_of(e):
                    for t in range(NHT):
                        n = NHT * e + t
                        wait(dve, it, silu, n + 1)
                        wait(dve, it, down, max(0, e - 2))
                        dve.tensor_tensor(gT[:, e % 3, t, :], sl[:, n % 3, :], pU[0:HT, n % 3, 1, :], ALU.mult).then_inc(hidden.sem, 1)

                def sum_of(e):
                    wait(dve, it, down, e + 1)
                    if e == 0:
                        wait(dve, it, stored, 0)
                    else:
                        wait(dve, it, summed, NA * e)
                    for a in range(NA):
                        dst = acc[:, e % 2, a, :]
                        if e == 0:
                            dve.tensor_tensor(dst, pD[:, 0, a, :], h2s[:, a, :], ALU.add).then_inc(summed.sem, 1)
                        else:
                            dve.scalar_tensor_tensor(out=dst, in0=pD[:, e % 3, a, :], scalar=route[:, a, e - 1:e],
                                                     in1=acc[:, (e - 1) % 2, a, :], op0=ALU.mult, op1=ALU.add).then_inc(summed.sem, 1)

                def chained(n):
                    wait(dve, it, router, n)

                wait(dve, it, gate, 1)
                dve.tensor_tensor(gl[:], pR[:], bias_s[:, None, :].broadcast_to([P, NA, NE]), ALU.add).then_inc(router.sem, 1)
                chained(1)
                mine = gl[:].unsqueeze(3).broadcast_to([P, NA, NE, NE])
                other = gl[:].unsqueeze(2).broadcast_to([P, NA, NE, NE])
                dve.tensor_tensor(cmp[:, 0], other, mine, ALU.is_gt).then_inc(router.sem, 1)
                dve.tensor_tensor(cmp[:, 1], other, mine, ALU.is_equal).then_inc(router.sem, 1)
                dve.reduce_max(mx[:], gl[:], X).then_inc(router.sem, 1)
                chained(4)
                dve.tensor_tensor(cmp[:, 2], cmp[:, 1], lower[:, None, :, :].broadcast_to([P, NA, NE, NE]), ALU.mult).then_inc(router.sem, 1)
                dve.tensor_tensor(ge[:], gl[:], mx[:].unsqueeze(2).broadcast_to([P, NA, NE]), ALU.subtract).then_inc(router.sem, 1)
                chained(6)
                dve.tensor_tensor(cmp[:, 1], cmp[:, 0], cmp[:, 2], ALU.add).then_inc(router.sem, 1)
                chained(7)
                dve.reduce_sum(rank[:], cmp[:, 1], X).then_inc(router.sem, 1)
                chained(8)
                wait(dve, it, gexp, 1)
                dve.scalar_tensor_tensor(out=gm[:], in0=rank[:], scalar=float(TOPK), in1=gx[:], op0=ALU.is_lt, op1=ALU.mult).then_inc(router.sem, 1)
                chained(9)
                dve.reduce_sum(gs[:], gm[:], X).then_inc(router.sem, 1)
                chained(10)
                dve.reciprocal(gr[:], gs[:]).then_inc(router.sem, 1)
                chained(11)
                wait(dve, it, summed, 0)
                dve.tensor_tensor(route[:], gm[:], gr[:].unsqueeze(2).broadcast_to([P, NA, NE]), ALU.mult).then_inc(router.sem, 1)
                chained(12)
                for e in range(E1):
                    hidden_of(e)
                    if e:
                        sum_of(e - 1)
                    if e == MID - 1:
                        stats(it + 1)
                    if e == MID:
                        norm(it + 1)
                sum_of(E1 - 1)

        @block.scalar
        def _(act):
            def root(it):
                wait(act, it, mean, 5)
                act.activation(lnv[:], ve[:], ACT.Ln).then_inc(ln_r.sem, 1)
                wait(act, it, ln_r, 1)
                act.activation(rstd[:], lnv[:], ACT.Exp, scale=-0.5).then_inc(ln_r.sem, 1)

            root(0)
            act.wait_ge(xt_p.sem, xt_p.count(1))
            act.activation(xT[:], pX[:], ACT.Copy).then_inc(xt.sem, 1)
            with act.Fori(0, B) as it:
                wait(act, it, router, 6)
                act.activation(gx[:], ge[:], ACT.Exp).then_inc(gexp.sem, 1)
                for e in range(E1):
                    for t in range(NHT):
                        n = NHT * e + t
                        wait(act, it, up, n + 1)
                        wait(act, it, hidden, max(0, n - 2))
                        act.activation(sl[:, n % 3, :], pU[0:HT, n % 3, 0, :], ACT.Silu).then_inc(silu.sem, 1)
                    if e == MID - 1:
                        root(it + 1)
                act.wait_ge(xt_p.sem, xt_p.count(it + 2))
                act.activation(xT[:], pX[:], ACT.Copy).then_inc(xt.sem, 1)


def kernel(**inputs):
    import numpy as np
    import concourse.bacc as bacc
    from concourse.bass_utils import run_bass_kernel_spmd

    a = {k.replace("L0_", ""): np.asarray(v) for k, v in inputs.items()}
    def stacked(shared, routed):
        return np.concatenate([a[shared][None], a[routed]], 0)

    def padded(x):
        return np.pad(x, [(0, 0), (0, NHT * HT - HF), (0, 0)])

    w12 = np.stack([padded(stacked(f"ffn_Ws{m}", f"ffn_W{m}")) for m in (1, 2)])
    w12 = w12.reshape(2, E1, NHT * HT, KC, P).transpose(4, 1, 3, 0, 2).reshape(P, E1, -1)
    w3 = padded(stacked("ffn_Ws3", "ffn_W3").transpose(0, 2, 1))
    w3 = w3.reshape(E1, NHT, HT, D).transpose(2, 0, 1, 3).reshape(HT, E1, -1)
    arrays = {
        "w12": w12, "w3": w3, "wg": a["ffn_Wg"].T, "bias": a["ffn_routing_bias"],
        "ids": np.ascontiguousarray(a["x"].reshape(NT, P).T),
        "emb0": a["tok_emb0"], "emb1": a["tok_emb1"], "emb2": a["tok_emb2"], "emb3": a["tok_emb3"],
        "projT": np.ascontiguousarray(np.concatenate([a[f"tok_proj{i}"].T for i in range(4)], 0)),
        "wkq": np.concatenate([a["attn_Wk"], a["attn_Wq"]], 1),
        "wvbg": np.concatenate([a["attn_Wv"], a["attn_beta_w"], a["attn_g_w"]], 1),
        "wA": a["attn_wA"], "wB": a["attn_wB"], "conv": a["attn_conv_w"], "gb": a["attn_g_b"],
        "wo": a["attn_Wo"],
        "norms_w": np.stack([a["attn_knorm_w"], a["attn_qnorm_w"]]),
    }
    nc = bacc.Bacc("TRN2", target_bir_lowering=False, num_devices=1)
    t = {}
    arrays = {f"in_{n}": np.ascontiguousarray(v) for n, v in arrays.items()}
    for n, v in arrays.items():
        t[n[3:]] = nc.dram_tensor(n, v.shape, mybir.dt.from_np(v.dtype), kind="ExternalInput").ap()
    out = nc.dram_tensor("out", (B, T, D), F32, kind="ExternalOutput").ap()
    build(nc, t, out)
    r = run_bass_kernel_spmd(nc, [arrays], core_ids=[0])
    return r.results[0]["out"]


def build(nc, t, out):
    h_d = nc.dram_tensor("h_scratch", (B, T, D), F32).ap()
    F_d = nc.dram_tensor("heads_scratch", (B, P, NG * NA * 3 * P), F32).ap()
    tm_d = nc.dram_tensor("token_scratch", (B, T, TM), F32).ap()
    with ExitStack() as sems:
        embed_and_project(nc, sems, t["ids"], [t[f"emb{i}"] for i in range(4)], t["projT"], t["wkq"], t["wvbg"],
                          t["wA"], t["wB"], t["conv"], t["gb"], t["norms_w"], h_d, F_d, tm_d)
        xt_d = nc.dram_tensor("xt_scratch", (B, NCB, H, CH, CH), F32).ap()
        bx_d = nc.dram_tensor("bx_scratch", (B, NCB, H, CH, CH), F32).ap()
        h2_d = nc.dram_tensor("h2_scratch", (B, T, D), F32).ap()
        attend(nc, sems, F_d, tm_d, xt_d, bx_d, h_d, t["wo"], h2_d)
        experts(nc, sems, h2_d, t["w12"], t["w3"], t["wg"], t["bias"], out)
```

```python
from contextlib import ExitStack

import concourse.bass as bass
from concourse import mybir

P = 128
F32 = mybir.dt.float32
BF16 = mybir.dt.bfloat16
I32 = mybir.dt.int32
ALU = mybir.AluOpType
ACT = mybir.ActivationFunctionType
X = mybir.AxisListType.X
DS = bass.ds

B, T, D = 16, 256, 256
H, DH = 16, 16
HP = 32
NT = B * T // P
NA = T // P
KC = D // P
NG, HG = 4, 4
CH = 32
NCB = T // CH
ENDS = (0, 5000, 10000, 50000, 267735)
EW = (256, 64, 16, 4)
EO = (0, 256, 320, 336)
EC = sum(EW)
EB = EC - 2 * P
WB = DH + 1
V0 = H * WB
TM = V0 + D
E1, HF, HT, NHT = 9, 682, 114, 6
NE, TOPK = 8, 4
NTE = NT
NTILES = TOPK * NT + NE - 1
NLIST = NTILES + 2


class Signal:

    def __init__(self, nc, ctx, name, per, first=1):
        self.sem = ctx.enter_context(nc.semaphore(name)) if name else None
        self.per, self.first = per, first

    def onward(self, rises, per=1):
        later = Signal(None, None, None, per, self.first + rises)
        later.sem = self.sem
        return later

    def at(self, it, k):
        return it * self.per + (k + self.first)

    def count(self, n):
        return n + self.first


def start(eng, signals):
    for signal in signals:
        eng.sem_inc(signal.sem, 1)


def wait(eng, it, signal, k):
    eng.wait_ge(signal.sem, signal.at(it, k))


def wait_apart(eng, it, signal, k, passed):
    eng.wait_ge(signal.sem, signal.at(it, k))
    eng.sem_inc(passed.sem, 1)


def sbufs(nc, ctx):
    return lambda name, shape, dt=F32: ctx.enter_context(nc.sbuf_tensor(name, shape, dt))


def psums(nc, ctx):
    return lambda name, shape, dt=F32: ctx.enter_context(nc.psum_tensor(name, shape, dt))


def embed_and_project(nc, sems, loaded, consts, ids, emb, projT, wkq, wvbg, wA, wB, conv, gb, norms_w, h_d, F_d, tm_d):
    AHEAD = 3
    with ExitStack() as ctx:
        sb, ps = sbufs(nc, ctx), psums(nc, ctx)

        signals = []

        def sig(name, per=1):
            signals.append(Signal(nc, sems, "p1_" + name, per))
            return signals[-1]

        NX = NT + AHEAD * NA
        ids_i = sb("ids_i", [P, NX], I32)
        idx_all = sb("idx_all", [P, NX, 4], I32)
        msk_all = sb("msk_all", [P, NX, 4])
        idx = sb("idx", [P, NA, 4], I32)
        msk = sb("msk", [P, NA, 4])
        lt = sb("lt", [P, NX])
        ident = sb("ident", [P, P])
        upto = sb("upto", [P, P])
        ones = sb("ones", [P, P])
        projT_s = sb("projT_s", [P, 3, D])
        wkq_s = sb("wkq_s", [P, KC, 2 * D])
        wvbg_s = sb("wvbg_s", [P, KC, D + 2 * H])
        wA_s = sb("wA_s", [P, KC, 32])
        wB_s = sb("wB_s", [32, D])
        conv_s = sb("conv_s", [P, KC, 3])
        gb_s = sb("gb_s", [P, H])
        norms_s = sb("norms_s", [P, 2, DH])
        norms = sb("norms", [P, 2, DH])
        zero = sb("zero", [P, 1])
        step1, pstep = sb("step", [P, 1]), sb("pstep", [P, 1])
        E = sb("E", [P, NA, EC])
        Em = sb("Em", [P, NA, EC])
        ET = sb("ET", [P, NA, 3 * P])
        hs = sb("hs", [P, NA, D])
        st = sb("st", [P, NA, 6])
        mv = sb("mv", [P, NA, 2])
        ve = sb("ve", [P, NA])
        lnv = sb("lnv", [P, NA])
        rstd = sb("rstd", [P, NA])
        xn = sb("xn", [P, NA, D])
        xT = sb("xT", [P, KC, T])
        xAT = sb("xAT", [32, T])
        wpad = sb("wpad", [P, KC, 2 + T])
        cv = sb("cv", [P, 3, KC, T])
        ws = sb("ws", [P, KC, T])
        sq = sb("sq", [P, NA, 3 * D])
        ss = sb("ss", [P, NA, 3 * H])
        sse = sb("sse", [P, NA, 3 * H])
        lns = sb("lns", [P, NA, 3 * H])
        rs = sb("rs", [P, NA, 3 * H])
        qkt = sb("qkt", [P, NA, 2 * D])
        vs = sb("vs", [P, NA, D])
        z, zabs, zexp, gexp, gln, g = [sb(name, [P, NA, H]) for name in ("z_beta", "zabs_g", "zexp_beta", "zexp_g", "zln_g", "gate")]
        zg, b1, br = sb("z_g", [P, NA, H]), sb("beta_sum", [P, NA, H]), sb("beta_rec", [P, NA, H])
        Ft = sb("Ft", [P, NA, 3, H, HP])
        FT = sb("FT", [P, NG, NA, 3, P])
        tm = sb("tm", [P, NA, V0])
        tmw = tm[:].rearrange("p a (h e) -> p a h e", e=WB)

        pE = ps("pE", [P, NA, 512])
        pQ = ps("pQ", [P, NA, 512])
        pX = ps("pX", [P, KC, T])
        pA = ps("pA", [P, 512])
        pV = ps("pV", [P, NA, D])
        pF = ps("pF", [P, 512])
        Z0, G0 = T, T + NA * 2 * H
        zp = pA[:, Z0:G0].rearrange("p (a n) -> p a n", a=NA)
        G = pA[:, G0:G0 + NA * H].rearrange("p (a h) -> p a h", h=H)

        ids_in, ids_ready = sig("ids_in"), sig("ids_ready")
        idx_in, msk_in, carried, moved = sig("idx_in"), sig("msk_in"), sig("carried"), sig("moved")
        gathered = Signal(nc, sems, "p1_gathered", 16 * 4 * NA, first=0)
        masked, et_p, et, h_p, h_s = sig("masked", 4), sig("et_p"), sig("et", 2), sig("h_p"), sig("h_s")
        h_out, mean, root, normed = sig("h_out", 16), sig("mean", 5), sig("root", 2), sig("normed", 2)
        xt_p, xt, xa_p, xa, w_p, w_s = sig("xt_p"), sig("xt"), sig("xa_p"), sig("xa"), sig("w_p"), sig("w_s")
        z_p, z_s, zexps, v_p, v_s, v_out, qk_p = sig("z_p"), sig("z_s", 2), sig("zexps", 3), sig("v_p"), sig("v_s"), sig("v_out", 16), sig("qk_p")
        conved, silu, wt_p, squared = sig("conved", 6), sig("silu"), sig("wt_p"), sig("squared", 2)
        sums, logs, beta, soft, gate, gsum, running = sig("sums", 3), sig("logs", 2), sig("beta", 3), sig("soft"), sig("gate"), sig("gsum"), sig("running", 2)
        qk_scaled, w_scaled, heads = sig("qk_scaled", NA), sig("w_scaled", 2 * NA), sig("heads", 2 * NA)
        f_p, f_even, f_odd, f_out, tm_out = sig("f_p", 6), sig("f_even", 3), sig("f_odd", 3), sig("f_out", 16), sig("tm_out", 16)

        block = ctx.enter_context(nc.Block())

        def skewed(eng, step):
            step(0, None, None)
            step(1, 0, None)
            with eng.Fori(0, B) as it:
                step(it + 2, it + 1, it)

        def rows_of(x, n):
            return x[DS(n % B, 1)].rearrange("o (a p) n -> p (o a) n", p=P)

        @block.sync
        def _(sp):
            sp.dma_start(ids_i[:, 0:NT], ids).then_inc(ids_in.sem, 16)
            sp.dma_start(ids_i[:, NT:NX], ids[:, 0:AHEAD * NA]).then_inc(ids_in.sem, 16)
            for dst, src in ((projT_s[:, 0:2, :], projT[0:2 * P, :].rearrange("(c p) n -> p c n", p=P)),
                             (projT_s[0:EB, 2, :], projT[2 * P:EC, :]),
                             (wkq_s[:], wkq.rearrange("(c p) n -> p c n", p=P)),
                             (wvbg_s[:], wvbg.rearrange("(c p) n -> p c n", p=P)),
                             (wA_s[:], wA.rearrange("(c p) n -> p c n", p=P)), (wB_s[:], wB),
                             (conv_s[:], conv.rearrange("(c p) n -> p c n", p=P)),
                             (gb_s[:], gb.partition_broadcast(P)), (norms_s[:], norms_w.partition_broadcast(P))):
                sp.dma_start(dst, src).then_inc(loaded.sem, 16)

            def step(first, second, third):
                if third is not None:
                    wait(sp, third, w_scaled, 2 * NA)
                    wait(sp, third, beta, 3)
                    sp.dma_start(rows_of(tm_d, third)[:, :, 0:V0], tm[:]).then_inc(tm_out.sem, 16)
                wait(sp, first, h_s, 1)
                sp.dma_start(rows_of(h_d, first), hs[:]).then_inc(h_out.sem, 16)
                if second is not None:
                    wait(sp, second, v_s, 1)
                    sp.dma_start(rows_of(tm_d, second)[:, :, V0:TM], vs[:]).then_inc(v_out.sem, 16)
                if third is not None:
                    wait(sp, third, f_even, 3)
                    wait(sp, third, f_odd, 3)
                    sp.dma_start(F_d[DS(third, 1)].rearrange("o p n -> p (o n)"), FT[:].rearrange("p g a m t -> p (g a m t)")).then_inc(f_out.sem, 16)

            skewed(sp, step)
            sp.wait_ge(h_out.sem, h_out.count(16 * (B + 2)))
            sp.wait_ge(v_out.sem, v_out.count(16 * (B + 1)))
            sp.wait_ge(tm_out.sem, tm_out.count(16 * B))
            sp.wait_ge(f_out.sem, f_out.count(16 * B))

        @block.gpsimd
        def _(pool):
            start(pool, signals + [loaded, consts])
            pool.memset(zero[:], 0.0).then_inc(consts.sem, 1)
            pool.memset(ident[:], 0.0).then_inc(consts.sem, 1)
            pool.memset(ones[:], 1.0).then_inc(consts.sem, 1)
            pool.memset(wpad[:], 0.0).then_inc(consts.sem, 1)
            pool.memset(Ft[:], 0.0).then_inc(consts.sem, 1)
            pool.wait_ge(consts.sem, consts.count(5))
            pool.memset(Ft[:, :, 1, :, DH + 1:DH + 2], 1.0).then_inc(consts.sem, 1)
            pool.memset(Ft[:, :, 0, :, DH:DH + 1], 1.0).then_inc(consts.sem, 1)
            pool.affine_select(out=ident[:], in_=ident[:], compare_op=ALU.not_equal, fill=1.0, base=0,
                               pattern=[[-1, P]], channel_multiplier=1).then_inc(consts.sem, 1)
            pool.affine_select(out=upto[:], in_=ones[:], compare_op=ALU.is_ge, fill=0.0, base=0,
                               pattern=[[1, P]], channel_multiplier=-1).then_inc(consts.sem, 1)
            pool.wait_ge(consts.sem, consts.count(9))

            def gather(n):
                wait(pool, n, idx_in, 1)
                wait(pool, n, masked, 0)
                wait(pool, n, carried, 0)
                pool.tensor_tensor(out=pstep[:], in0=zero[:], in1=zero[:], op=ALU.add).then_inc(carried.sem, 1)
                for a in range(NA):
                    for i in range(4):
                        pool.indirect_dma_start(
                            out=E[:, a, EO[i]:EO[i] + EW[i]], out_offset=None, in_=emb[i],
                            in_offset=bass.IndirectOffsetOnAxis(ap=idx[:, a, i:i + 1], axis=0),
                        ).then_inc(gathered.sem, 16)

            def step(first, second, third):
                if third is not None:
                    wait(pool, third, qk_scaled, NA)
                    wait(pool, third, f_p, 0)
                    for a in range(NA):
                        for m in range(2):
                            pool.tensor_tensor(
                                out=Ft[:, a, m, :, 0:DH],
                                in0=qkt[:, a, m * D:(m + 1) * D].rearrange("p (h d) -> p h d", d=DH),
                                in1=norms[:, m:m + 1, :].broadcast_to([P, H, DH]), op=ALU.mult).then_inc(heads.sem, 1)
                gather(first + 1)

            gather(0)
            skewed(pool, step)
            pool.wait_ge(gathered.sem, gathered.count(16 * 4 * NA * (B + 3)))

        @block.vector
        def _(dve):
            dve.wait_ge(ids_in.sem, ids_in.count(16 * 2))
            for i in range(4):
                lo, hi = ENDS[i], ENDS[i + 1]
                dve.tensor_scalar(lt[:], ids_i[:], float(-lo), 0.0, ALU.add, ALU.max).then_inc(ids_ready.sem, 1)
                dve.wait_ge(ids_ready.sem, ids_ready.count(4 * i + 1))
                dve.tensor_scalar(idx_all[:, :, i], lt[:], float(hi - lo - 1), None, ALU.min).then_inc(ids_ready.sem, 1)
                dve.wait_ge(ids_ready.sem, ids_ready.count(4 * i + 2))
                dve.tensor_scalar(lt[:], ids_i[:], float(lo), None, ALU.is_ge).then_inc(ids_ready.sem, 1)
                dve.wait_ge(ids_ready.sem, ids_ready.count(4 * i + 3))
                dve.scalar_tensor_tensor(out=msk_all[:, :, i], in0=ids_i[:], scalar=float(hi), in1=lt[:],
                                         op0=ALU.is_lt, op1=ALU.mult).then_inc(ids_ready.sem, 1)
                dve.wait_ge(ids_ready.sem, ids_ready.count(4 * i + 4))

            def rows_known(n):
                dve.tensor_copy(idx[:], idx_all[:, DS(n * NA, NA), :]).then_inc(idx_in.sem, 1)

            rows_known(0)
            dve.wait_ge(loaded.sem, loaded.count(16 * 9))
            dve.tensor_scalar(norms[:, 1, :], norms_s[:, 1, :], DH ** -0.5, None, ALU.mult).then_inc(ids_ready.sem, 1)
            dve.tensor_copy(norms[:, 0, :], norms_s[:, 0, :]).then_inc(ids_ready.sem, 1)
            dve.wait_ge(ids_ready.sem, ids_ready.count(18))
            dve.wait_ge(consts.sem, consts.count(9))

            def betas(n):
                wait(dve, n, zexps, 3)
                dve.tensor_scalar(b1[:], zexp[:], 1.0, None, ALU.add).then_inc(beta.sem, 1)
                wait(dve, n, beta, 1)
                dve.reciprocal(br[:], b1[:]).then_inc(beta.sem, 1)
                wait(dve, n, beta, 2)
                wait(dve, n, tm_out, 0)
                dve.tensor_scalar(tmw[:, :, :, DH], br[:], 2.0, None, ALU.mult).then_inc(beta.sem, 1)

            def embeddings(n):
                dve.tensor_copy(msk[:], msk_all[:, DS(n * NA, NA), :]).then_inc(msk_in.sem, 1)
                wait(dve, n, msk_in, 1)
                wait(dve, n, gathered, 16 * 4 * NA)
                wait(dve, n, et_p, 0)
                for i in range(4):
                    dve.tensor_tensor(Em[:, :, EO[i]:EO[i] + EW[i]], E[:, :, EO[i]:EO[i] + EW[i]],
                                      msk[:, :, i:i + 1].broadcast_to([P, NA, EW[i]]), ALU.mult).then_inc(masked.sem, 1)

            def norm(n):
                wait(dve, n, root, 2)
                wait(dve, n, xt_p, 0)
                for a in range(NA):
                    dve.tensor_scalar(xn[:, a, :], hs[:, a, :], mv[:, a, 0:1], rstd[:, a:a + 1],
                                      ALU.subtract, ALU.mult).then_inc(normed.sem, 1)

            def scale_qk(n):
                wait(dve, n, logs, 2)
                wait(dve, n, heads, 0)
                for a in range(NA):
                    dve.tensor_tensor(qkt[:, a, :].rearrange("p (h d) -> p h d", d=DH),
                                      pQ[:, a, :].rearrange("p (h d) -> p h d", d=DH),
                                      rs[:, a, 0:2 * H].unsqueeze(2).broadcast_to([P, 2 * H, DH]), ALU.mult).then_inc(qk_scaled.sem, 1)

            def scale_w(n):
                wait(dve, n, logs, 2)
                wait(dve, n, f_p, 0)
                wait(dve, n, tm_out, 0)
                for a in range(NA):
                    wrow = pF[:, a * D:(a + 1) * D].rearrange("p (h d) -> p h d", d=DH)
                    wrs = rs[:, a, 2 * H:3 * H].unsqueeze(2).broadcast_to([P, H, DH])
                    dve.tensor_tensor(Ft[:, a, 2, :, 0:DH], wrow, wrs, ALU.mult).then_inc(w_scaled.sem, 1)
                    dve.tensor_tensor(tmw[:, a, :, 0:DH], wrow, wrs, ALU.mult).then_inc(w_scaled.sem, 1)

            def gate_of(n):
                wait(dve, n, soft, 1)
                wait(dve, n, gsum, 0)
                dve.scalar_tensor_tensor(out=g[:], in0=zg[:], scalar=0.0, in1=gln[:],
                                         op0=ALU.min, op1=ALU.subtract).then_inc(gate.sem, 1)

            def running_of(n):
                wait(dve, n, gsum, 1)
                dve.tensor_copy(Ft[:, :, 1, :, DH], G).then_inc(running.sem, 1)
                dve.tensor_scalar(Ft[:, :, 0, :, DH + 1], G, -1.0, None, ALU.mult).then_inc(running.sem, 1)

            def convolve(n):
                wait(dve, n, w_s, 1)
                wait(dve, n, silu, 0)
                for c in range(KC):
                    dve.tensor_scalar(cv[:, 0, c, :], wpad[:, c, 0:T], conv_s[:, c, 0:1], None, ALU.mult).then_inc(conved.sem, 1)
                for k in (1, 2):
                    wait(dve, n, conved, 2 * k)
                    for c in range(KC):
                        dve.scalar_tensor_tensor(out=cv[:, k, c, :], in0=wpad[:, c, k:k + T], scalar=conv_s[:, c, k:k + 1],
                                                 in1=cv[:, k - 1, c, :], op0=ALU.mult, op1=ALU.add).then_inc(conved.sem, 1)

            def gate_logits(n):
                wait(dve, n, z_p, 1)
                wait(dve, n, zexps, 0)
                wait(dve, n, gate, 0)
                dve.tensor_copy(z[:], zp[:, :, 0:H]).then_inc(z_s.sem, 1)
                dve.tensor_tensor(zg[:], zp[:, :, H:2 * H], gb_s[:, None, :].broadcast_to([P, NA, H]), ALU.add).then_inc(z_s.sem, 1)

            def moments(n):
                wait(dve, n, h_s, 1)
                wait(dve, n, root, 0)
                for a in range(NA):
                    dve.bn_stats(st[:, a, :], hs[:, a, :]).then_inc(mean.sem, 1)
                wait(dve, n, mean, NA)
                wait(dve, n, moved, 0)
                dve.tensor_copy(step1[:], zero[:]).then_inc(moved.sem, 1)
                for a in range(NA):
                    dve.bn_aggr(mv[:, a, :], st[:, a, :]).then_inc(mean.sem, 1)
                wait(dve, n, mean, 2 * NA)
                dve.tensor_scalar(ve[:], mv[:, :, 1], 1e-5, None, ALU.add).then_inc(mean.sem, 1)

            def even_heads(n, j):
                wait(dve, n, f_p, j + 1)
                wait(dve, n, f_out, 0)
                dve.tensor_copy(FT[:].rearrange("p g a m t -> p (g a m t)")[:, 512 * j:512 * (j + 1)], pF[:]).then_inc(f_even.sem, 1)

            def head_sums(n):
                wait(dve, n, squared, 2)
                wait(dve, n, logs, 0)
                dve.reduce_sum(ss[:].rearrange("p a h -> p (a h)"), sq[:].rearrange("p a (h d) -> p (a h) d", d=DH), X).then_inc(sums.sem, 1)
                wait(dve, n, sums, 1)
                dve.tensor_scalar(sse[:, :, 0:2 * H], ss[:, :, 0:2 * H], 1.0 / DH, 1e-5, ALU.mult, ALU.add).then_inc(sums.sem, 1)
                dve.tensor_scalar(sse[:, :, 2 * H:3 * H], ss[:, :, 2 * H:3 * H], 1e-12, None, ALU.add).then_inc(sums.sem, 1)

            def step(first, second, third):
                embeddings(first)
                if third is not None:
                    gate_of(third)
                    scale_w(third)
                    scale_qk(third)
                    betas(third)
                if second is not None:
                    convolve(second)
                rows_known(first + 1)
                if third is not None:
                    running_of(third)
                if second is not None:
                    gate_logits(second)
                if third is not None:
                    even_heads(third, 0)
                moments(first)
                if third is not None:
                    even_heads(third, 2)
                norm(first)
                if third is not None:
                    even_heads(third, 4)
                if second is not None:
                    head_sums(second)

            skewed(dve, step)

        @block.scalar
        def _(act):
            act.wait_ge(consts.sem, consts.count(9))

            def odd_heads(n, j):
                wait(act, n, f_p, j + 1)
                wait(act, n, f_out, 0)
                act.activation(FT[:].rearrange("p g a m t -> p (g a m t)")[:, 512 * j:512 * (j + 1)], pV[:].rearrange("p a n -> p (a n)"), ACT.Copy).then_inc(f_odd.sem, 1)

            def log_of_variance(n):
                wait(act, n, mean, 5)
                wait(act, n, root, 0)
                act.activation(lnv[:], ve[:], ACT.Ln).then_inc(root.sem, 1)

            def log_of_sums(n):
                wait(act, n, sums, 3)
                act.activation(lns[:], sse[:], ACT.Ln).then_inc(logs.sem, 1)

            def softplus(n):
                wait(act, n, zexps, 3)
                wait(act, n, gate, 0)
                act.activation(gln[:], gexp[:], ACT.Ln, bias=1.0).then_inc(soft.sem, 1)

            def root_of_variance(n):
                wait(act, n, root, 1)
                wait(act, n, normed, 0)
                act.activation(rstd[:], lnv[:], ACT.Exp, scale=-0.5).then_inc(root.sem, 1)

            def root_of_sums(n):
                wait(act, n, logs, 1)
                wait(act, n, qk_scaled, 0)
                wait(act, n, w_scaled, 0)
                act.activation(rs[:], lns[:], ACT.Exp, scale=-0.5).then_inc(logs.sem, 1)

            def embeddings_T(n):
                wait(act, n, et_p, 1)
                wait(act, n, h_p, 0)
                act.activation(ET[:, :, 0:2 * P], pE[:, :, 0:2 * P], ACT.Copy).then_inc(et.sem, 1)
                act.activation(ET[0:EB, :, 2 * P:3 * P], pE[0:EB, :, 2 * P:3 * P], ACT.Copy).then_inc(et.sem, 1)

            def norm_T(n):
                wait(act, n, xt_p, 1)
                wait(act, n, v_p, 0)
                wait(act, n, qk_p, 0)
                act.activation(xT[:], pX[:], ACT.Copy).then_inc(xt.sem, 1)

            def xa_of(n):
                wait(act, n, xa_p, 1)
                act.activation(xAT[:], pA[0:32, 0:T], ACT.Copy).then_inc(xa.sem, 1)

            def embedded(n):
                wait(act, n, h_p, 1)
                wait(act, n, h_out, 0)
                wait(act, n, normed, 0)
                act.activation(hs[:], pE[:, 0, :].rearrange("p (a n) -> p a n", a=NA), ACT.Copy, scale=float(D) ** 0.5).then_inc(h_s.sem, 1)

            def w_of(n):
                wait(act, n, w_p, 1)
                wait(act, n, conved, 0)
                act.activation(wpad[:, :, 2:2 + T], pX[:], ACT.Copy).then_inc(w_s.sem, 1)

            def v_of(n):
                wait(act, n, v_p, 1)
                wait(act, n, v_out, 0)
                act.activation(vs[:], pV[:], ACT.Copy).then_inc(v_s.sem, 1)

            def silu_of(n):
                wait(act, n, conved, 6)
                wait(act, n, wt_p, 0)
                act.activation(ws[:], cv[:, 2, :, :], ACT.Silu).then_inc(silu.sem, 1)

            def exp_of_gates(n):
                wait(act, n, z_s, 2)
                wait(act, n, beta, 0)
                act.activation(zabs[:], zg[:], ACT.Abs).then_inc(zexps.sem, 1)
                act.activation(zexp[:], z[:], ACT.Exp, scale=-1.0).then_inc(zexps.sem, 1)
                wait(act, n, zexps, 1)
                wait(act, n, soft, 0)
                act.activation(gexp[:], zabs[:], ACT.Exp, scale=-1.0).then_inc(zexps.sem, 1)

            def square_qk(n):
                wait(act, n, qk_p, 1)
                wait(act, n, sums, 0)
                act.activation(sq[:, :, 0:2 * D], pQ[:], ACT.Square).then_inc(squared.sem, 1)

            def square_w(n):
                wait(act, n, wt_p, 1)
                wait(act, n, sums, 0)
                act.activation(sq[:, :, 2 * D:3 * D], pF[:].rearrange("p (a n) -> p a n", a=NA), ACT.Square).then_inc(squared.sem, 1)

            def step(first, second, third):
                if third is not None:
                    log_of_sums(third)
                if second is not None:
                    xa_of(second)
                if third is not None:
                    softplus(third)
                    root_of_sums(third)
                embeddings_T(first)
                if second is not None:
                    w_of(second)
                embedded(first)
                if second is not None:
                    exp_of_gates(second)
                log_of_variance(first)
                if second is not None:
                    v_of(second)
                root_of_variance(first)
                if second is not None:
                    silu_of(second)
                if third is not None:
                    odd_heads(third, 1)
                norm_T(first)
                if second is not None:
                    square_qk(second)
                if third is not None:
                    odd_heads(third, 3)
                if second is not None:
                    square_w(second)
                if third is not None:
                    odd_heads(third, 5)

            skewed(act, step)

        @block.tensor
        def _(pe):
            pe.wait_ge(consts.sem, consts.count(9))
            pe.wait_ge(loaded.sem, loaded.count(16 * 9))
            mm = nc.tensor.matmul

            def embeddings_T(n):
                wait(pe, n, masked, 4)
                wait(pe, n, h_s, 0)
                for a in range(NA):
                    for c in range(3):
                        w = P if c < 2 else EB
                        last = pe.transpose(pE[0:w, a, c * P:(c + 1) * P], Em[:, a, c * P:c * P + w], ident[:])
                last.then_inc(et_p.sem, 1)

            def project(n):
                wait(pe, n, et, 2)
                for a in range(NA):
                    for c in range(3):
                        w = P if c < 2 else EB
                        last = mm(pE[:, 0, a * D:(a + 1) * D], ET[0:w, a, c * P:(c + 1) * P], projT_s[0:w, c, :], start=(c == 0), stop=(c == 2))
                last.then_inc(h_p.sem, 1)

            def norm_T(n):
                wait(pe, n, normed, 2)
                wait(pe, n, w_s, 0)
                for c in range(KC):
                    for a in range(NA):
                        last = pe.transpose(pX[:, c, a * P:(a + 1) * P], xn[:, a, c * P:(c + 1) * P], ident[:])
                last.then_inc(xt_p.sem, 1)

            def xa_of(n):
                wait(pe, n, xt, 1)
                wait(pe, n, z_s, 0)
                if not isinstance(n, int):
                    wait(pe, n - 1, running, 0)
                for c in range(KC):
                    last = mm(pA[0:32, 0:T], wA_s[:, c, :], xT[:, c, :], start=(c == 0), stop=(c == KC - 1))
                last.then_inc(xa_p.sem, 1)

            def w_of(n):
                wait(pe, n, xa, 1)
                for c in range(KC):
                    last = mm(pX[:, c, :], wB_s[:, c * P:(c + 1) * P], xAT[:], start=True, stop=True)
                last.then_inc(w_p.sem, 1)

            def running_sums(n):
                wait(pe, n, gate, 1)
                wait(pe, n + 1, xa, 1)
                mm(pA[:, G0:G0 + H], upto[:], g[:, 0, :], start=True, stop=True)
                mm(pA[:, G0 + H:G0 + 2 * H], ones[:], g[:, 0, :], start=True, stop=False)
                mm(pA[:, G0 + H:G0 + 2 * H], upto[:], g[:, 1, :], start=False, stop=True).then_inc(gsum.sem, 1)

            def logits_of(n):
                wait(pe, n, running, 0)
                for a in range(NA):
                    for c in range(KC):
                        last = mm(pA[:, Z0 + 2 * H * a:Z0 + 2 * H * (a + 1)], xT[:, c, a * P:(a + 1) * P], wvbg_s[:, c, D:D + 2 * H], start=(c == 0), stop=(c == KC - 1))
                last.then_inc(z_p.sem, 1)

            def v_of(n):
                wait(pe, n, v_s, 0)
                if not isinstance(n, int):
                    wait(pe, n - 1, f_odd, 0)
                for a in range(NA):
                    for c in range(KC):
                        last = mm(pV[:, a, :], xT[:, c, a * P:(a + 1) * P], wvbg_s[:, c, 0:D], start=(c == 0), stop=(c == KC - 1))
                last.then_inc(v_p.sem, 1)

            def qk_of(n):
                wait(pe, n, qk_scaled, 0)
                wait(pe, n, squared, 0)
                for a in range(NA):
                    for c in range(KC):
                        last = mm(pQ[:, a, :], xT[:, c, a * P:(a + 1) * P], wkq_s[:, c, :], start=(c == 0), stop=(c == KC - 1))
                last.then_inc(qk_p.sem, 1)

            def w_T(n):
                wait(pe, n, silu, 1)
                wait(pe, n, f_even, 0)
                for a in range(NA):
                    for c in range(KC):
                        last = pe.transpose(pF[:, a * D + c * P:a * D + (c + 1) * P], ws[:, c, a * P:(a + 1) * P], ident[:])
                last.then_inc(wt_p.sem, 1)

            def heads_T(n, j):
                dst = pV[:].rearrange("p a n -> p (a n)") if j % 2 else pF[:]
                if j == 0:
                    wait(pe, n, heads, 2 * NA)
                    wait(pe, n, w_scaled, 2 * NA)
                    wait(pe, n, running, 2)
                    wait(pe, n, squared, 2)
                elif j == 1:
                    wait(pe, n + 1, v_s, 1)
                else:
                    wait(pe, n, f_odd if j % 2 else f_even, j // 2)
                for i in range(4):
                    r = 4 * j + i
                    gg, a, m = r // 6, r % 6 // 3, r % 3
                    last = pe.transpose(dst[:, i * P:(i + 1) * P],
                                        Ft[:, a, m, 4 * gg:4 * gg + 4, :].rearrange("p h d -> p (h d)"), ident[:])
                last.then_inc(f_p.sem, 1)

            def step(first, second, third):
                if second is not None:
                    xa_of(second)
                    v_of(second)
                embeddings_T(first)
                if second is not None:
                    w_of(second)
                project(first)
                if third is not None:
                    running_sums(third)
                if second is not None:
                    logits_of(second)
                if third is not None:
                    heads_T(third, 0)
                if second is not None:
                    qk_of(second)
                if third is not None:
                    heads_T(third, 1)
                    heads_T(third, 2)
                norm_T(first)
                if third is not None:
                    heads_T(third, 3)
                    heads_T(third, 4)
                if second is not None:
                    w_T(second)
                if third is not None:
                    heads_T(third, 5)

            skewed(pe, step)


def attend(nc, sems, loaded, consts, F_d, tm_d, xt_d, bx_d, h_d, wo, h2_d):
    NS = NG * NA
    HC = CH // 2
    DSTEP = HC * (CH + 1)
    GR = 4
    NGR = CH // GR
    NM = 4
    NL = NGR + (HC - 1) + 4
    W0, R0, Q0, G0, MW = 0, HP, HP + P, HP + 2 * P, HP + 3 * P
    HB = P // 2
    with ExitStack() as ctx:
        sb, ps = sbufs(nc, ctx), psums(nc, ctx)

        signals = []

        def sig(name, per=1):
            signals.append(Signal(nc, sems, "p3_" + name, per))
            return signals[-1]

        Fs = sb("Fs", [P, NG, NA, 3, P])
        XTs = sb("XTs", [P, NA, H, HB])
        BXs = sb("BXs", [P, NA, H, HB])
        tms = sb("tms", [P, NA, TM])
        tmw = tms[:, :, 0:V0].rearrange("p a (h e) -> p a h e", e=WB)
        wt = sb("wt", [P, NA, H, DH])
        va = sb("va", [P, NA, H, DH + 1])
        nbeta = sb("nbeta", [P, NA, H])
        hres = sb("hres", [P, NA, D])
        wo_s = sb("wo_s", [P, KC, D])
        lw = sb("lane_w", [P, CH, WB])
        lbeta = sb("lane_beta", [P, CH])
        lnbw = sb("lane_nbw", [P, CH, DH])
        Lf = sb("lane_L", [P, 2 * DSTEP])
        Xf = sb("lane_Xt", [P, 2 * DSTEP])
        L, Xt = [x[:, 0:CH * CH].rearrange("p (i j) -> p i j", j=CH) for x in (Lf, Xf)]
        Ld, Xd = [x[:].rearrange("p (b r) -> p b r", b=2)[:, :, 0:HC * CH].rearrange("p b (i j) -> p b i j", j=CH)[:, :, :, 0:HC]
                  for x in (Lf, Xf)]
        Yt = sb("lane_Yt", [P, HC, HC])
        bX = sb("lane_bX", [P, CH, CH])
        lprod = sb("lane_prod", [P, HC * HC * HC // 2])
        lgram = sb("lane_gram", [P, 2, GR * CH * DH])
        ident3 = sb("ident3", [P, P])
        identb = sb("identb", [P, P], BF16)
        future = sb("future", [P, 2, P], BF16)
        ones3 = sb("ones3", [P, 3, P])
        keep = sb("keep", [P, 3, P])
        Ms = sb("Ms", [P, NM, HG, MW])
        Ys = sb("Ys", [P, HG, HB])
        X64 = sb("X64", [P, HG, HB])
        nb = sb("nb", [P, NA, HG, HP + P])
        Qz = sb("Qz", [P, NG, NA, HG, P])
        Wz = sb("Wz", [P, NG, NA, HG, P])
        khat = sb("khat", [P, P])
        qhat = sb("qhat", [P, HG, P])
        nm = sb("nm", [P, HG])
        Ps = sb("Ps", [P, HG, 2 * P])
        PTs = sb("PTs", [P, HG, 2, P])
        rec = sb("rec", [P, HG])
        Os = sb("Os", [P, NA, D])
        OT = sb("OT", [P, KC, T])
        h2s = sb("h2s", [P, NA, D])

        pG = ps("pG", [P, 512])
        pY = ps("pY", [P, 512])
        pC = ps("pC", [P, 2, 512])
        pS = ps("pS", [P, 2, 512])
        pT = ps("pT", [P, 2, 512])

        cleared = sig("cleared", 9)
        f_in, x_in, tm_in, h_in = [sig(f"f_in{i}", 9 * 16) for i in range(NG)], [sig(f"x_in{i}", 16 * 16) for i in range(NG)], sig("tm_in", 16), sig("h_in", 16)
        copied, w_in, gram, masked = sig("copied", 3), sig("w_in", NS), sig("gram", NS * HG), sig("masked", NS * HG)

        def two(name):
            return [sig(f"{name}{i}", NS) for i in range(2)]

        y_p, y_s, xy_p, x64 = sig("y_p", NS), sig("y_s", NS), sig("xy_p", NS), sig("x64", NS)
        top_p, top = two("top_p"), two("top")
        rhs_p, rhs, low_p, low = two("rhs_p"), two("rhs"), two("low_p"), two("low")
        hat_p, hat, score, peak, weight = two("hat_p"), two("hat"), two("score"), two("peak"), two("weight")
        wT_p, wT, out_p, inv, outs = two("wT_p"), two("wT"), two("out_p"), two("inv"), two("outs")
        oT_p, oT, y_out, h2, h2_out = sig("oT_p"), sig("oT"), sig("y_out"), sig("h2"), sig("h2_out", 16)
        pe_passed, pool_passed = sig("pe_passed"), sig("pool_passed")
        lane_in, lane_first, lane_prod, lane_sum = sig("lane_in", 16 * NCB), sig("lane_first", 2), sig("lane_prod", NL - NGR), sig("lane_sum", NL)
        lane_gram, lane_cleared = sig("lane_gram", NGR), sig("lane_cleared", 2)
        lane_done, lane_out = sig("lane_done"), sig("lane_out", 32)

        block = ctx.enter_context(nc.Block())

        def load_group(sp, it, g):
            sp.dma_start(Fs[:, g].rearrange("p a m t -> p (a m t)"),
                         F_d[DS(it, 1), :, g * NA * 3 * P:(g + 1) * NA * 3 * P].rearrange("o p n -> p (o n)")).then_inc(f_in[g].sem, 16)
            heads = F_d[DS(it, 1)].rearrange("o p (g a m t) -> p (o g) a m t", g=NG, a=NA, m=3)
            for dst, m in ((Qz, 1), (Wz, 2)):
                for h in range(HG):
                    r = slice(HP * h, HP * (h + 1))
                    sp.dma_start(dst[r, g, :, h, :], heads[r, g, :, m, :]).then_inc(f_in[g].sem, 16)
            for dst, src in ((XTs, xt_d), (BXs, bx_d)):
                chunks = src[DS(it, 1)].rearrange("o c h s t -> (o c) s h t")
                for n in range(T // CH):
                    a, c = divmod(n, P // CH)
                    sp.dma_start(dst[CH * c:CH * (c + 1), a, HG * g:HG * (g + 1), CH * (c % 2):CH * (c % 2 + 1)],
                                 chunks[n, :, HG * g:HG * (g + 1), :]).then_inc(x_in[g].sem, 16)

        def rows_of(x, it):
            return x[DS(it, 1)].rearrange("o (a p) n -> p (o a) n", p=P)

        def load_lanes(sp, n):
            rows = tm_d[DS(n, 1), :, 0:V0].rearrange("o (c t) (h e) -> (o c) h t e", t=CH, e=WB)
            for c in range(NCB):
                sp.dma_start(lw[H * c:H * (c + 1)], rows[c]).then_inc(lane_in.sem, 16)

        def store_lanes(sp, n):
            for dst, src in ((xt_d, Xt), (bx_d, bX[:])):
                sp.dma_start(dst[DS(n, 1)].rearrange("o c h s t -> (o c h) (s t)"), src.rearrange("p s t -> p (s t)")).then_inc(lane_out.sem, 16)

        @block.sync
        def _(sp):
            load_lanes(sp, 0)
            wait(sp, 0, lane_sum, NGR)
            load_lanes(sp, 1)
            wait(sp, 0, lane_done, 1)
            store_lanes(sp, 0)
            sp.dma_start(wo_s[:], wo.rearrange("(c p) n -> p c n", p=P)).then_inc(loaded.sem, 16)
            sp.dma_start(tms[:], rows_of(tm_d, 0)).then_inc(tm_in.sem, 16)
            sp.dma_start(hres[:], rows_of(h_d, 0)).then_inc(h_in.sem, 16)
            sp.wait_ge(cleared.sem, cleared.count(9))
            wait(sp, 0, lane_out, 32)
            for g in range(NG):
                load_group(sp, 0, g)
            wait(sp, 1, lane_sum, NGR)
            load_lanes(sp, 2)
            wait(sp, 1, lane_done, 1)
            store_lanes(sp, 1)
            with sp.Fori(0, B) as it:
                wait(sp, it, copied, 3)
                sp.dma_start(tms[:], rows_of(tm_d, (it + 1) % B)).then_inc(tm_in.sem, 16)
                wait(sp, it + 1, lane_out, 32)
                for g in range(NG):
                    if g == NG - 1:
                        wait(sp, it + 2, lane_done, 1)
                        store_lanes(sp, (it + 2) % B)
                    wait(sp, it, score[0], NA * (g + 1))
                    wait(sp, it, score[1], NA * (g + 1))
                    wait(sp, it, hat[0], NA * (g + 1))
                    wait(sp, it, hat[1], NA * (g + 1))
                    load_group(sp, (it + 1) % B, g)
                    if g == 1:
                        wait(sp, it + 2, lane_sum, NGR)
                        load_lanes(sp, (it + 3) % B)
                wait(sp, it, h2, 1)
                sp.dma_start(rows_of(h2_d, it), h2s[:]).then_inc(h2_out.sem, 16)
                sp.dma_start(hres[:], rows_of(h_d, (it + 1) % B)).then_inc(h_in.sem, 16)
            sp.wait_ge(h2_out.sem, h2_out.count(16 * B))
            sp.wait_ge(h_in.sem, h_in.count(16 * (B + 1)))
            sp.wait_ge(lane_out.sem, lane_out.count(32 * (B + 2)))
            sp.wait_ge(lane_in.sem, lane_in.count(16 * NCB * (B + 3)))
            for g in range(NG):
                sp.wait_ge(f_in[g].sem, f_in[g].count(144 * (B + 1)))
                sp.wait_ge(x_in[g].sem, x_in[g].count(256 * (B + 1)))

        def lane_operands(kind, t):
            q = HC // 2
            if kind == "gram":
                n = GR * (t + 1)
                sizes = [P, GR, n, DH]
                one, other = lnbw[:, None, 0:n, :], lw[:, GR * t:n, 0:DH].unsqueeze(2)
                to = L[:, GR * t:n, 0:n]
            elif kind == "solve":
                sizes = [P, 2, t, t]
                one, other = Xd[:, :, 0:t, 0:t], Ld[:, :, t:t + 1, 0:t]
                to = Xd[:, :, 0:t, t]
            elif kind == "left":
                js, ss = slice(q * t, q * (t + 1)), slice(q * t, HC)
                sizes = [P, q, HC, HC - q * t]
                one, other = Xt[:, js, ss].unsqueeze(2), L[:, None, HC:CH, ss]
                to = Yt[:, js, :]
            else:
                sizes = [P, HC, q, q * (t + 1)]
                one = Yt[:, :, 0:q * (t + 1)].unsqueeze(2)
                i = slice(HC + q * t, HC + q * (t + 1))
                other = Xt[:, HC:HC + q * (t + 1), i].rearrange("p r i -> p i r").unsqueeze(1)
                to = Xt[:, 0:HC, i]
            a, b, c = sizes[1:]
            place = (lgram[:, t % 2] if kind == "gram" else lprod)[:, 0:a * b * c].rearrange("p (a b c) -> p a b c", b=b, c=c)
            return one.broadcast_to(sizes), other.broadcast_to(sizes), place, to

        def read_before(k, early):
            return k + 1 - NM if early else max(0, k + 1 - NM)

        @block.gpsimd
        def _(pool):
            start(pool, signals)

            def gram_products(n, b):
                one, other, place, _ = lane_operands("gram", b)
                if b == 0:
                    wait(pool, n, lane_first, 2)
                wait(pool, n, lane_sum, max(0, b - 1))
                pool.tensor_tensor(out=place, in0=one, in1=other, op=ALU.mult).then_inc(lane_gram.sem, 1)

            for x in (XTs, BXs, Ms, nb, ident3, Qz, Wz, qhat):
                pool.memset(x[:], 0.0).then_inc(cleared.sem, 1)
            pool.memset(va[:, :, :, DH:DH + 1], 1.0).then_inc(cleared.sem, 1)
            pool.memset(ones3[:], 1.0).then_inc(consts.sem, 1)
            pool.memset(future[:], 0.0).then_inc(consts.sem, 1)
            pool.wait_ge(cleared.sem, cleared.count(9))
            pool.wait_ge(consts.sem, consts.count(2))
            pool.affine_select(out=ident3[:], in_=ident3[:], compare_op=ALU.not_equal, fill=1.0, base=0,
                               pattern=[[-1, P]], channel_multiplier=1).then_inc(consts.sem, 1)
            pool.affine_select(out=keep[:, 0, :], in_=ones3[:, 0, :], compare_op=ALU.is_gt, fill=0.0, base=0,
                               pattern=[[-1, P]], channel_multiplier=1).then_inc(consts.sem, 1)
            pool.affine_select(out=keep[:, 1, :], in_=ones3[:, 1, :], compare_op=ALU.is_ge, fill=0.0, base=0,
                               pattern=[[1, P]], channel_multiplier=-1).then_inc(consts.sem, 1)
            pool.affine_select(out=keep[:, 2, :].rearrange("p (c t) -> p c t", t=CH), in_=ones3[:, 2, :].rearrange("p (c t) -> p c t", t=CH),
                               compare_op=ALU.is_gt, fill=0.0, base=0, pattern=[[CH, P // CH], [0, CH]], channel_multiplier=-1).then_inc(consts.sem, 1)
            pool.affine_select(out=future[:], in_=future[:], compare_op=ALU.is_ge, fill=-1e30, base=0,
                               pattern=[[0, 2], [-1, P]], channel_multiplier=1).then_inc(consts.sem, 1)
            pool.wait_ge(consts.sem, consts.count(7))
            pool.tensor_copy(identb[:], ident3[:]).then_inc(consts.sem, 1)
            pool.wait_ge(consts.sem, consts.count(8))

            def rows_in(n, before):
                pool.wait_ge(tm_in.sem, tm_in.count(n * 16 + 16))
                wait(pool, n, low[0], 0)
                wait_apart(pool, n, low[1], 0, pool_passed)
                pool.tensor_scalar(nbeta[:], tmw[:, :, :, DH], -1.0, None, ALU.mult).then_inc(copied.sem, 1)
                wait_apart(pool, n, w_in, 0, pool_passed)
                pool.tensor_copy(wt[:], tmw[:, :, :, 0:DH]).then_inc(copied.sem, 1)
                before()
                wait(pool, n, out_p[0], 0)
                wait_apart(pool, n, out_p[1], 0, pool_passed)
                pool.tensor_copy(va[:, :, :, 0:DH], tms[:, :, V0:TM].rearrange("p a (h d) -> p a h d", d=DH)).then_inc(copied.sem, 1)

            def w_into(n, k):
                g, a = divmod(k, NA)
                if k == 0:
                    wait(pool, n, copied, 2)
                if k >= NA or not isinstance(n, int):
                    wait(pool, n, score[0], read_before(k, k == 0))
                    wait(pool, n, score[1], read_before(k, k == 0))
                pool.tensor_tensor(out=Ms[:, k % NM, :, W0:W0 + DH], in0=wt[:, a, HG * g:HG * (g + 1), :],
                                   in1=ones3[:, 0, 0:1].unsqueeze(2).broadcast_to([P, HG, DH]), op=ALU.mult).then_inc(w_in.sem, 1)

            grams_behind = {1: (0, 1), 2: (2, 3), 3: (4, 5), 4: (6, 7)}

            rows_in(0, lambda: w_into(0, 0))
            with pool.Fori(0, B) as it:
                for k in range(1, NS):
                    w_into(it, k)
                    for b in grams_behind.get(k, ()):
                        gram_products(it + 2, b)
                rows_in(it + 1, lambda: w_into(it + 1, 0))

        def steps(it, step):
            for k in range(1, NS + 1):
                front = (it, k + 1) if k + 1 < NS else (it + 1, k + 1 - NS)
                middle = (it, k) if k < NS else (it + 1, 0)
                step(front, middle, (it, k - 1))

        def first_steps(step):
            step((0, 0), None, None)
            step((0, 1), (0, 0), None)

        def each(f):
            f(0)
            f(1)

        def c0(k):
            return R0 if k % NA == 0 else W0

        @block.tensor
        def _(pe):
            mm = nc.tensor.matmul
            pe.wait_ge(consts.sem, consts.count(8))
            pe.wait_ge(loaded.sem, loaded.count(16))
            def gram_of(it, k, h):
                g, a = divmod(k, NA)
                if a == 0 and h == 0:
                    pe.wait_ge(f_in[g].sem, f_in[g].count(it * 144 + 144))
                    pe.wait_ge(x_in[g].sem, x_in[g].count(it * 256 + 256))
                wait(pe, it, masked, HG * k + h)
                mm(pG[:, 0:3 * P], Wz[:, g, a, h, :], Fs[:, g, a, :, :].rearrange("p m t -> p (m t)"),
                   start=True, stop=True).then_inc(gram.sem, 1)

            def blocks(f):
                for h in range(HG):
                    for r in (slice(0, HB), slice(HB, P)):
                        last = f(h, r)
                return last

            def y_of(it, k):
                g, a = divmod(k, NA)
                wait(pe, it, masked, HG * (k + 1))
                wait_apart(pe, it, x64, k, pe_passed)
                blocks(lambda h, r: mm(pY[r, h * HB:(h + 1) * HB], Ms[r, k % NM, h, G0 + r.start:G0 + r.stop],
                                       BXs[r, a, HG * g + h, :], start=True, stop=True)).then_inc(y_p.sem, 1)

            def xy_of(it, k):
                g, a = divmod(k, NA)
                wait_apart(pe, it, y_s, k + 1, pe_passed)
                blocks(lambda h, r: mm(pY[r, h * HB:(h + 1) * HB], Ys[r, h, :],
                                       XTs[r, a, HG * g + h, :], start=True, stop=True)).then_inc(xy_p.sem, 1)

            def top_of(it, k, pr):
                a = k % NA
                wait(pe, it, x64, k + 1)
                wait(pe, it, hat[pr], k)
                wait_apart(pe, it, w_in, k + 1, pe_passed)
                for hh in range(2):
                    last = mm(pC[0:HB, pr, 160 * hh + c0(k):160 * hh + R0 + HB], X64[0:HB, 2 * pr + hh, :],
                              Ms[0:HB, k % NM, 2 * pr + hh, c0(k):R0 + HB], start=True, stop=True)
                last.then_inc(top_p[pr].sem, 1)

            def rhs_of(it, k, pr):
                wait_apart(pe, it, top[pr], k + 1, pe_passed)
                for hh in range(2):
                    last = mm(pC[HB:P, pr, 160 * hh + c0(k):160 * hh + R0 + HB], Ms[0:HB, k % NM, 2 * pr + hh, G0 + HB:G0 + P],
                              nb[0:HB, k % NA, 2 * pr + hh, c0(k):R0 + HB], start=True, stop=True)
                last.then_inc(rhs_p[pr].sem, 1)

            def low_of(it, k, pr):
                wait_apart(pe, it, rhs[pr], k + 1, pe_passed)
                for hh in range(2):
                    last = mm(pC[HB:P, pr, 160 * hh + c0(k):160 * hh + R0 + P], X64[HB:P, 2 * pr + hh, :],
                              Ms[HB:P, k % NM, 2 * pr + hh, c0(k):R0 + P], start=True, stop=True)
                last.then_inc(low_p[pr].sem, 1)

            def hat_of(it, k, pr):
                wait(pe, it, low[pr], k + 1)
                for h in (2 * pr, 2 * pr + 1):
                    if k % NA == 0:
                        l, r = Ms[:, k % NM, h, W0:W0 + HP], nb[:, k % NA, h, R0:R0 + P]
                    else:
                        l, r = nb[:, k % NA, h, W0:W0 + HP], Ms[:, k % NM, h, Q0:Q0 + P]
                    last = mm(pC[HP * h:HP * (h + 1), pr, 0:P], l, r, start=True, stop=True, tile_position=(0, HP * h))
                last.then_inc(hat_p[pr].sem, 1)

            def score_of(it, k, pr):
                g, a = divmod(k, NA)
                wait(pe, it, weight[pr], k)
                sc = pS[:, pr, :].rearrange("p (h j) -> p h j", h=2)
                mm(sc[:, :, P:2 * P], identb[:], future[:], start=True, stop=False)
                for hh in range(2):
                    h = 2 * pr + hh
                    mm(sc[:, hh, P:2 * P], Qz[:, g, a, h, :], Fs[:, g, a, 0, :], start=False, stop=False)
                    last = mm(sc[:, hh, P:2 * P], Ms[:, k % NM, h, Q0:Q0 + P], nb[:, k % NA, h, R0:R0 + P], start=False, stop=(hh == 1 and a == 0))
                if a == 0:
                    last.then_inc(score[pr].sem, 1)

            def far_score_of(it, k, pr):
                if k % NA == 0:
                    return
                wait(pe, it, hat[0], k + 1)
                wait(pe, it, hat[1], k + 1)
                for hh in range(2):
                    last = mm(pS[:, pr, 2 * hh * P:(2 * hh + 1) * P], qhat[:, 2 * pr + hh, :], khat[:], start=False, stop=(hh == 1))
                last.then_inc(score[pr].sem, 1)

            def weights_T(it, k, pr):
                a = k % NA
                wait(pe, it, weight[pr], k + 1)
                if k == 0:
                    wait(pe, it, oT, 0)
                    wait(pe, it, h2, 0)
                wait(pe, it, outs[pr], k)
                for hh in range(2):
                    for j in range(1 - a, 2):
                        last = pe.transpose(pT[:, pr, (2 * hh + j) * P:(2 * hh + j + 1) * P], Ps[:, 2 * pr + hh, j * P:(j + 1) * P], ident3[:])
                last.then_inc(wT_p[pr].sem, 1)

            def out_of(it, k, pr):
                g, a = divmod(k, NA)
                wait(pe, it, wT[pr], k + 1)
                if k == 0:
                    wait(pe, it, copied, 3)
                for hh in range(2):
                    for j in range(1 - a, 2):
                        jt = j - 1 + a
                        last = mm(pT[:, pr, hh * HP:hh * HP + DH + 1], PTs[:, 2 * pr + hh, j, :], va[:, jt, HG * g + 2 * pr + hh, :],
                                  start=(j == 1 - a), stop=(j == 1))
                last.then_inc(out_p[pr].sem, 1)

            def outs_T(it):
                wait(pe, it, outs[0], NS)
                wait(pe, it, outs[1], NS)
                for c in range(KC):
                    for a in range(NA):
                        last = pe.transpose(pT[:, 0, c * T + a * P:c * T + (a + 1) * P], Os[:, a, c * P:(c + 1) * P], ident3[:])
                last.then_inc(oT_p.sem, 1)

            def through_wo(it):
                wait(pe, it, oT, 1)
                for a in range(NA):
                    for c in range(KC):
                        last = mm(pT[:, 1, a * D:(a + 1) * D], OT[:, c, a * P:(a + 1) * P], wo_s[:, c, :], start=(c == 0), stop=(c == KC - 1))
                last.then_inc(y_out.sem, 1)

            def step(front, middle, soft):
                gram_of(*front, 0)
                if soft:
                    score_of(*soft, 0)
                    far_score_of(*soft, 0)
                gram_of(*front, 1)
                if middle:
                    each(lambda pr: top_of(*middle, pr))
                if soft:
                    score_of(*soft, 1)
                    far_score_of(*soft, 1)
                if middle:
                    each(lambda pr: rhs_of(*middle, pr))
                gram_of(*front, 2)
                if soft:
                    weights_T(*soft, 0)
                if middle:
                    each(lambda pr: low_of(*middle, pr))
                gram_of(*front, 3)
                if soft:
                    weights_T(*soft, 1)
                if middle:
                    each(lambda pr: hat_of(*middle, pr))
                y_of(*front)
                if soft:
                    out_of(*soft, 0)
                    out_of(*soft, 1)
                xy_of(*front)

            first_steps(step)
            with pe.Fori(0, B) as it:
                steps(it, step)
                outs_T(it)
                through_wo(it)

        GRAMS = [("gram", b, GR * GR * (b + 1) * DH) for b in range(NGR)]
        SOLVES = ([("solve", t, 2 * t * t) for t in range(1, HC)]
                  + [(kind, half, HC * HC * (HC // 2) // (1 + small)) for kind, half, small in
                     (("left", 0, 0), ("left", 1, 1), ("right", 0, 1), ("right", 1, 0))])
        LANE_FIRST = [("first", 0, None, 0, 600)]
        LANE_SUMS = [("sums", n, kind, t, size + 100) for n, (kind, t, size) in enumerate(GRAMS)]
        LANE_SOLVE = ([("clear", 0, None, 0, 700)]
                      + [(what, NGR + n, kind, t, size + 100) for n, (kind, t, size) in enumerate(SOLVES) for what in ("product", "sums")]
                      + [("last", 0, None, 0, 1100)])
        LANE_GRAM = [(what, n, kind, t, size) for _, n, kind, t, size in LANE_SUMS for what in ("product", "sums")]

        @block.vector
        def _(dve):
            def lane_step(n, what, i, kind, t):
                if what == "first":
                    wait(dve, n, lane_in, 16 * NCB)
                    wait(dve, n, lane_gram, 0)
                    wait(dve, n, lane_done, 0)
                    dve.scalar_tensor_tensor(out=lnbw[:], in0=lw[:, :, 0:DH], scalar=-1.0, in1=lw[:, :, DH:WB].broadcast_to([P, CH, DH]),
                                             op0=ALU.mult, op1=ALU.mult).then_inc(lane_first.sem, 1)
                    dve.tensor_copy(lbeta[:], lw[:, :, DH]).then_inc(lane_first.sem, 1)
                elif what == "clear":
                    wait(dve, n, lane_out, 0)
                    dve.memset(Xf[:], 0.0).then_inc(lane_cleared.sem, 1)
                    wait(dve, n, lane_cleared, 1)
                    dve.memset(Xf[:, 0:CH * CH:CH + 1], 1.0).then_inc(lane_cleared.sem, 1)
                    wait(dve, n, lane_cleared, 2)
                elif what == "product":
                    one, other, place, _ = lane_operands(kind, t)
                    wait(dve, n, lane_sum, i)
                    if i == 0:
                        wait(dve, n, lane_first, 2)
                    dve.tensor_tensor(place, one, other, ALU.mult).then_inc(lane_gram.sem if kind == "gram" else lane_prod.sem, 1)
                elif what == "sums":
                    _, _, place, to = lane_operands(kind, t)
                    if kind == "gram":
                        wait(dve, n, lane_gram, i + 1)
                    else:
                        wait(dve, n, lane_prod, i + 1 - NGR)
                    dve.reduce_sum(to, place, X).then_inc(lane_sum.sem, 1)
                else:
                    wait(dve, n, lane_sum, NL)
                    dve.tensor_tensor(bX[:], Xt.rearrange("p s t -> p t s"), lbeta[:].unsqueeze(2).broadcast_to([P, CH, CH]),
                                      ALU.mult).then_inc(lane_done.sem, 1)

            def lane_steps(n, steps, lo, hi):
                whole, at = sum(step[-1] for step in steps), 0
                for what, i, kind, t, cost in steps:
                    if lo * whole <= at < hi * whole:
                        lane_step(n, what, i, kind, t)
                    at += cost

            lane_steps(0, LANE_FIRST + LANE_GRAM + LANE_SOLVE, 0, 1)
            lane_steps(1, LANE_FIRST, 0, 1)
            dve.wait_ge(consts.sem, consts.count(8))

            def peak_of(it, k, pr):
                a = k % NA
                wait(dve, it, score[pr], k + 1)
                sc = pS[:, pr, :].rearrange("p (h j) -> p h j", h=2)
                dve.tensor_reduce(out=nm[:, 2 * pr:2 * pr + 2], in_=sc[:, :, (1 - a) * P:2 * P], axis=X, op=ALU.max, negate=True).then_inc(peak[pr].sem, 1)

            def mask(it, k, h):
                wait(dve, it, gram, HG * k + h + 1)
                if k >= NA or not isinstance(it, int):
                    wait(dve, it, score[h // 2], read_before(k, k < NA))
                dve.tensor_tensor(Ms[:, k % NM, h, R0:MW], pG[:, 0:3 * P], keep[:].rearrange("p m t -> p (m t)"), ALU.mult).then_inc(masked.sem, 1)

            def x64_of(it, k):
                g, a = divmod(k, NA)
                wait(dve, it, xy_p, k + 1)
                dve.tensor_tensor(X64[:], XTs[:, a, HG * g:HG * (g + 1), :],
                                  pY[:, 0:HG * HB].rearrange("p (h t) -> p h t", h=HG), ALU.subtract).then_inc(x64.sem, 1)

            def rhs_of(it, k, pr):
                wait(dve, it, rhs_p[pr], k + 1)
                m = Ms[HB:P, k % NM, 2 * pr:2 * pr + 2, c0(k):R0 + HB]
                dve.tensor_tensor(m, pC[HB:P, pr, 0:320].rearrange("p (h n) -> p h n", h=2)[:, :, c0(k):R0 + HB], m, ALU.add).then_inc(rhs[pr].sem, 1)

            def hat_of(it, k, pr):
                g, a = divmod(k, NA)
                r = slice(2 * HP * pr, 2 * HP * (pr + 1))
                wait(dve, it, hat_p[pr], k + 1)
                if a == 0:
                    wait(dve, it, score[0], k)
                    wait(dve, it, score[1], k)
                    last = dve.tensor_tensor(khat[r, :], pC[r, pr, 0:P], Fs[r, g, 0, 0, :], ALU.add)
                else:
                    for h in (2 * pr, 2 * pr + 1):
                        r = slice(HP * h, HP * (h + 1))
                        last = dve.tensor_tensor(qhat[r, h, :], pC[r, pr, 0:P], Fs[r, g, 1, 1, :], ALU.add)
                last.then_inc(hat[pr].sem, 1)

            def outs_of(it, k, pr):
                g, a = divmod(k, NA)
                o = pT[:, pr, 0:2 * HP].rearrange("p (h n) -> p h n", h=2)
                wait(dve, it, out_p[pr], k + 1)
                dve.reciprocal(rec[:, 2 * pr:2 * pr + 2], o[:, :, DH]).then_inc(inv[pr].sem, 1)
                wait(dve, it, inv[pr], k + 1)
                at = DH * (HG * g + 2 * pr)
                dve.tensor_tensor(Os[:, a, at:at + 2 * DH].rearrange("p (h d) -> p h d", d=DH), o[:, :, 0:DH],
                                  rec[:, 2 * pr:2 * pr + 2].unsqueeze(2).broadcast_to([P, 2, DH]), ALU.mult).then_inc(outs[pr].sem, 1)

            def h2_of(it):
                wait(dve, it, y_out, 1)
                wait(dve, it, h2_out, 0)
                dve.wait_ge(h_in.sem, h_in.count(it * 16 + 16))
                dve.tensor_tensor(h2s[:], pT[:, 1, :].rearrange("p (a n) -> p a n", a=NA), hres[:], ALU.add).then_inc(h2.sem, 1)

            def step(front, middle, soft):
                if soft:
                    it, k = soft

                    def lanes(lo, hi):
                        if k < 3:
                            lane_steps(it + 2, LANE_SUMS[3 * k:3 * k + 3], lo, hi)
                        else:
                            parts = NS - 3
                            lane_steps(it + 2, LANE_SOLVE, (k - 3 + lo) / parts, (k - 3 + hi) / parts)
                            if k == NS - 1 and hi == 1:
                                lane_steps(it + 3, LANE_FIRST, 0, 1)
                else:
                    def lanes(lo, hi):
                        k = front[1]
                        lane_steps(1, LANE_GRAM + LANE_SOLVE, (k + lo) / 2, (k + hi) / 2)
                        if k == 1 and hi == 1:
                            lane_steps(2, LANE_FIRST, 0, 1)
                mask(*front, 0)
                lanes(0.0,0.3)
                mask(*front, 1)
                if soft:
                    peak_of(*soft, 0)
                    peak_of(*soft, 1)
                if middle:
                    rhs_of(*middle, 0)
                    rhs_of(*middle, 1)
                mask(*front, 2)
                lanes(0.3,0.45)
                mask(*front, 3)
                lanes(0.45,0.7)
                if middle:
                    hat_of(*middle, 0)
                    hat_of(*middle, 1)
                if soft:
                    outs_of(*soft, 0)
                lanes(0.7,1.0)
                if soft:
                    outs_of(*soft, 1)
                x64_of(*front)

            first_steps(step)
            with dve.Fori(0, B) as it:
                steps(it, step)
                h2_of(it)

        @block.scalar
        def _(act):
            act.wait_ge(consts.sem, consts.count(8))
            def weight_of(it, k, pr):
                a = k % NA
                wait(act, it, peak[pr], k + 1)
                for hh in range(2):
                    h = 2 * pr + hh
                    last = act.activation(Ps[:, h, (1 - a) * P:2 * P], pS[:, pr, (2 * hh + 1 - a) * P:(2 * hh + 2) * P], ACT.Exp, bias=nm[:, h:h + 1])
                last.then_inc(weight[pr].sem, 1)

            def y_of(it, k):
                wait(act, it, y_p, k + 1)
                act.activation(Ys[:].rearrange("p h t -> p (h t)"), pY[:, 0:HG * HB], ACT.Copy).then_inc(y_s.sem, 1)

            def wT_of(it, k, pr):
                a = k % NA
                wait(act, it, wT_p[pr], k + 1)
                act.activation(PTs[:, 2 * pr:2 * pr + 2, 1 - a:2, :], pT[:, pr, :].rearrange("p (h j t) -> p h j t", h=2, j=2)[:, :, 1 - a:2, :],
                               ACT.Copy).then_inc(wT[pr].sem, 1)

            def scaled_of(it, k, pr, rows, cols, before, after):
                g, a = divmod(k, NA)
                wait(act, it, before[pr], k + 1)
                if k == 0:
                    wait(act, it, copied, 1)
                for hh in range(2):
                    h = 2 * pr + hh
                    last = act.activation(nb[rows, a, h, cols], pC[rows, pr, 160 * hh + cols.start:160 * hh + cols.stop], ACT.Copy,
                                          scale=nbeta[rows, a, HG * g + h:HG * g + h + 1])
                last.then_inc(after[pr].sem, 1)

            def top_of(it, k, pr):
                scaled_of(it, k, pr, slice(0, HB), slice(c0(k), R0 + HB), top_p, top)

            def low_of(it, k, pr):
                scaled_of(it, k, pr, slice(HB, P), slice(c0(k), R0 + P), low_p, low)

            def step(front, middle, soft):
                if middle:
                    top_of(*middle, 0)
                    top_of(*middle, 1)
                if soft:
                    weight_of(*soft, 0)
                    weight_of(*soft, 1)
                if middle:
                    low_of(*middle, 0)
                    low_of(*middle, 1)
                if soft:
                    wT_of(*soft, 0)
                    wT_of(*soft, 1)
                y_of(*front)

            first_steps(step)
            with act.Fori(0, B) as it:
                steps(it, step)
                wait(act, it, oT_p, 1)
                act.activation(OT[:].rearrange("p c t -> p (c t)"), pT[:, 0, :], ACT.Copy).then_inc(oT.sem, 1)


def route_and_share(nc, sems, loaded, consts, h2_d, w12, w3, wg, bias, token_ids, firsts, pads, lists, W12, W3, w_in, carry, tile, expert, xn_d, acc_d, slot_d):
    with ExitStack() as ctx:
        sb, ps = sbufs(nc, ctx), psums(nc, ctx)

        signals = []

        def sig(name, per=1):
            signals.append(Signal(nc, sems, "p4_" + name, per))
            return signals[-1]

        W12s = sb("W12s", [P, KC, 2, NHT * HT])
        W3s = sb("W3s", [HT, NHT, D])
        wg_s = sb("wg_s", [P, KC, NE])
        bias_s = sb("bias_s", [P, NE])
        toks = sb("toks", [P, NT])
        ident4 = sb("ident4", [P, P])
        ones4 = sb("ones4", [P, P])
        before = sb("before", [P, P])
        lower = sb("lower", [P, NE, NE])
        h2s = sb("h2in", [P, NA, D])
        hres = sb("hres4", [P, NA, D])
        st = sb("st4", [P, NA, 6])
        mv = sb("mv4", [P, NA, 2])
        ve = sb("ve4", [P, NA])
        lnv = sb("lnv4", [P, NA])
        rstd = sb("rstd4", [P, NA])
        xn = sb("xn4", [P, NA, D])
        xT = sb("xT4", [P, KC, T])
        gl = sb("gl", [P, NA, NE])
        cmp = sb("cmp", [P, 3, NA, NE, NE])
        rank = sb("rank", [P, NA, NE])
        top = sb("topmask", [P, NA, NE])
        mx = sb("mx", [P, NA])
        ge = sb("ge", [P, NA, NE])
        gx = sb("gx", [P, NA, NE])
        gm = sb("gmask", [P, NA, NE])
        gs = sb("gs", [P, NA])
        gr = sb("gr", [P, NA])
        route = sb("route", [P, NA, NE])
        selT = sb("selT", [P, NA, NE, NE])
        order = sb("order", [P, NA, NE])
        hot = sb("hot", [P, NA, TOPK, NE])
        slot = sb("slot", [P, NA, NE])
        hs, hr = sb("hot_slot", [P, NA, TOPK, NE]), sb("hot_route", [P, NA, TOPK, NE])
        slotf = sb("slotf", [P, NA, TOPK])
        sloti, hi, lo, addr = [sb(name, [P, NA, TOPK], I32) for name in ("sloti", "slot_hi", "slot_lo", "addr")]
        pair = sb("pair", [P, NA, TOPK, 2])
        pad = sb("pad", [P, 2 * NE * NTE])
        zeros = sb("zeros", [P, D])
        sl = sb("sl", [HT, 3, T])
        gT = sb("gT", [HT, NHT, T])
        acc = sb("acc", [P, NA, D])
        zero4, step4, step_s = sb("zero4", [P, 1]), sb("step4", [P, 1]), sb("step_s", [P, 1])

        tiles = sb("tiles", [1, NTE])
        nth = sb("nth", [1, NLIST])
        upto5 = sb("upto5", [1, NE, NE])
        first = sb("first", [1, NE])
        count = sb("count", [1, NE])
        more = sb("more", [1, NE, NTE])
        nt = sb("ntiles", [1, NE])
        cum = sb("cum", [1, NE, NE])
        end = sb("end", [1, NE])
        past = sb("past", [1, NLIST, NE])
        pastn = sb("pastn", [1, NLIST, NE])
        ef, sf, tf, tin = [sb(name, [1, NLIST]) for name in ("ef", "sf", "tf", "tin")]

        pU = ps("pU", [P, 4, 2, T])
        pD = ps("pD", [P, NA, D])
        pX = ps("pX4", [P, KC, T])
        pR = ps("pR", [P, NA, NE])
        pP = ps("pP", [P, NA + 1, NE])

        table = sig("table")
        cleared, moved, carried, shared_in = sig("cleared"), sig("moved"), sig("carried"), sig("shared_in")
        h2_in, res_in, mean, root, normed = sig("h2_in", 16), sig("res_in", 16), sig("mean", 5), sig("root", 2), sig("normed", NA)
        xn_out, xt_p, xt, gate, gexp = sig("xn_out", 16), sig("xt_p"), sig("xt"), sig("gate"), sig("gexp")
        router, chosen, place_p, placed, pairs = sig("router", 12), sig("chosen"), sig("place_p"), sig("placed", 14), sig("pairs", 3)
        told = sig("told")
        scattered = Signal(nc, sems, "p4_scattered", 16 * NA * TOPK, first=0)
        up, silu, hidden, down, summed, stored = sig("up", NHT), sig("silu", NHT), sig("hidden", NHT), sig("down"), sig("summed"), sig("stored", 16)
        block = ctx.enter_context(nc.Block())

        def rows_of(x, n):
            return x[DS(n * T, T), :].rearrange("(a p) n -> p a n", p=P)

        @block.sync
        def _(sp):
            sp.dma_start(h2s[:], rows_of(h2_d, 0)).then_inc(h2_in.sem, 16)
            for dst, src in ((wg_s[:], wg.rearrange("(c p) n -> p c n", p=P)), (bias_s[:], bias.partition_broadcast(P)),
                             (toks[:], token_ids), (carry[:], firsts.partition_broadcast(P)), (pad[:], pads), *zip((tiles[:], nth[:], upto5[:].rearrange("p i j -> p (i j)"), first[:]), lists)):
                sp.dma_start(dst, src).then_inc(loaded.sem, 16)
            for c in range(KC):
                sp.dma_start(W12s[:, c].rearrange("p m n -> p (m n)"), w12[:, 0, c * 2 * NHT * HT:(c + 1) * 2 * NHT * HT]).then_inc(shared_in.sem, 16)
            sp.dma_start(W3s[:].rearrange("p t n -> p (t n)"), w3[:, 0, :]).then_inc(shared_in.sem, 16)
            sp.dma_start(hres[:], rows_of(h2_d, 0)).then_inc(res_in.sem, 16)
            sp.wait_ge(loaded.sem, loaded.count(16 * 9))
            sp.dma_start(slot_d.rearrange("(p n) m -> p (n m)", p=P), pad[:]).then_inc(cleared.sem, 16)
            sp.wait_ge(consts.sem, consts.count(7))
            sp.dma_start(xn_d[NT * P:(NT + 1) * P, :], zeros[:]).then_inc(cleared.sem, 16)
            sp.dma_start(acc_d[NT * P:(NT + 1) * P, :], zeros[:]).then_inc(cleared.sem, 16)
            up_share, down_share = NE * KC // B, NE * NHT // B
            w12_parts, w3_parts = w12.rearrange("p e (c n) -> p (e c) n", c=KC), w3.rearrange("p e (t n) -> p (e t) n", t=NHT)
            W12_parts, W3_parts = W12[:].rearrange("p e c m n -> p (e c) (m n)"), W3[:].rearrange("p e t n -> p (e t) n")
            with sp.Fori(0, B) as it:
                wait(sp, it, normed, NA)
                sp.dma_start(rows_of(xn_d, it), xn[:]).then_inc(xn_out.sem, 16)
                sp.dma_start(h2s[:], rows_of(h2_d, (it + 1) % B)).then_inc(h2_in.sem, 16)
                sp.dma_start(W12_parts[:, DS(it * up_share, up_share)], w12_parts[:, DS(it * up_share + KC, up_share)]).then_inc(w_in.sem, 16)
                sp.dma_start(W3_parts[:, DS(it * down_share, down_share)], w3_parts[:, DS(it * down_share + NHT, down_share)]).then_inc(w_in.sem, 16)
                wait(sp, it, summed, 1)
                sp.dma_start(hres[:], rows_of(h2_d, (it + 1) % B)).then_inc(res_in.sem, 16)
                sp.dma_start(rows_of(acc_d, it), acc[:]).then_inc(stored.sem, 16)
            sp.wait_ge(cleared.sem, cleared.count(48))
            sp.wait_ge(xn_out.sem, xn_out.count(16 * B))
            sp.wait_ge(stored.sem, stored.count(16 * B))
            sp.wait_ge(res_in.sem, res_in.count(16 * (B + 1)))

        @block.gpsimd
        def _(pool):
            start(pool, signals + [w_in])
            pool.memset(zero4[:], 0.0).then_inc(consts.sem, 1)
            pool.memset(ident4[:], 0.0).then_inc(consts.sem, 1)
            pool.memset(lower[:], 1.0).then_inc(consts.sem, 1)
            pool.memset(ones4[:], 1.0).then_inc(consts.sem, 1)
            pool.memset(zeros[:], 0.0).then_inc(consts.sem, 1)
            pool.wait_ge(consts.sem, consts.count(5))
            pool.affine_select(out=ident4[:], in_=ident4[:], compare_op=ALU.not_equal, fill=1.0, base=0,
                               pattern=[[-1, P]], channel_multiplier=1).then_inc(consts.sem, 1)
            pool.affine_select(out=lower[:], in_=lower[:], compare_op=ALU.is_gt, fill=0.0, base=0,
                               pattern=[[1, NE], [-1, NE]], channel_multiplier=0).then_inc(consts.sem, 1)
            pool.affine_select(out=before[:], in_=ones4[:], compare_op=ALU.is_gt, fill=0.0, base=0,
                               pattern=[[1, P]], channel_multiplier=-1).then_inc(consts.sem, 1)
            pool.wait_ge(cleared.sem, cleared.count(48))
            with pool.Fori(0, B) as it:
                wait(pool, it, placed, 14)
                wait(pool, it, pairs, 3)
                wait(pool, it, moved, 0)
                pool.tensor_tensor(out=step4[:], in0=zero4[:], in1=zero4[:], op=ALU.add).then_inc(moved.sem, 1)
                for a in range(NA):
                    for k in range(TOPK):
                        pool.indirect_dma_start(
                            out=slot_d, out_offset=bass.IndirectOffsetOnAxis(ap=addr[:, a, k:k + 1], axis=0),
                            in_=pair[:, a, k, :], in_offset=None).then_inc(scattered.sem, 16)
                pool.wait_ge(scattered.sem, scattered.at(it, scattered.per))
                pool.sem_inc(told.sem, 1)

        @block.tensor
        def _(pe):
            mm = nc.tensor.matmul

            def transposes():
                for c in range(KC):
                    for a in range(NA):
                        last = pe.transpose(pX[:, c, a * P:(a + 1) * P], xn[:, a, c * P:(c + 1) * P], ident4[:])
                last.then_inc(xt_p.sem, 1)

            pe.wait_ge(consts.sem, consts.count(8))
            pe.wait_ge(loaded.sem, loaded.count(16 * 9))
            pe.wait_ge(normed.sem, normed.count(NA))
            transposes()
            pe.wait_ge(shared_in.sem, shared_in.count(16 * 3))
            with pe.Fori(0, B) as it:
                wait(pe, it, xt, 1)
                wait(pe, it, router, 0)
                for a in range(NA):
                    for c in range(KC):
                        last = mm(pR[:, a, :], xT[:, c, a * P:(a + 1) * P], wg_s[:, c, :], start=(c == 0), stop=(c == KC - 1))
                last.then_inc(gate.sem, 1)
                for t in range(NHT):
                    wait(pe, it, hidden, max(0, t - 3))
                    for m in range(2):
                        for c in range(KC):
                            last = mm(pU[0:HT, t % 4, m, :], W12s[:, c, m, t * HT:(t + 1) * HT], xT[:, c, :],
                                      start=(c == 0), stop=(c == KC - 1))
                    last.then_inc(up.sem, 1)
                wait(pe, it + 1, normed, NA)
                transposes()
                wait(pe, it, chosen, 1)
                wait(pe, it, placed, 0)
                mm(pP[:, 0, :], before[:], top[:, 0, :], start=True, stop=True)
                mm(pP[:, 1, :], ones4[:], top[:, 0, :], start=True, stop=False)
                mm(pP[:, 1, :], before[:], top[:, 1, :], start=False, stop=True)
                mm(pP[:, 2, :], ones4[:], top[:, 0, :], start=True, stop=False)
                mm(pP[:, 2, :], ones4[:], top[:, 1, :], start=False, stop=True).then_inc(place_p.sem, 1)
                wait(pe, it, hidden, NHT)
                wait(pe, it, summed, 0)
                for a in range(NA):
                    for t in range(NHT):
                        last = mm(pD[:, a, :], gT[:, t, a * P:(a + 1) * P], W3s[:, t, :], start=(t == 0), stop=(t == NHT - 1))
                last.then_inc(down.sem, 1)

        @block.vector
        def _(dve):
            def stats(n):
                dve.wait_ge(h2_in.sem, h2_in.count(n * 16 + 16))
                wait(dve, n, root, 0)
                wait(dve, n, normed, 0)
                for a in range(NA):
                    dve.bn_stats(st[:, a, :], h2s[:, a, :]).then_inc(mean.sem, 1)
                wait(dve, n, mean, NA)
                wait(dve, n, carried, 0)
                dve.tensor_copy(step_s[:], zero4[:]).then_inc(carried.sem, 1)
                for a in range(NA):
                    dve.bn_aggr(mv[:, a, :], st[:, a, :]).then_inc(mean.sem, 1)
                wait(dve, n, mean, 2 * NA)
                dve.tensor_scalar(ve[:], mv[:, :, 1], 1e-5, None, ALU.add).then_inc(mean.sem, 1)

            def norm(n):
                wait(dve, n, root, 2)
                wait(dve, n, xt_p, 0)
                wait(dve, n, xn_out, 0)
                for a in range(NA):
                    dve.tensor_scalar(xn[:, a, :], h2s[:, a, :], mv[:, a, 0:1], rstd[:, a:a + 1],
                                      ALU.subtract, ALU.mult).then_inc(normed.sem, 1)

            dve.wait_ge(consts.sem, consts.count(8))
            stats(0)
            norm(0)
            dve.wait_ge(loaded.sem, loaded.count(16 * 9))
            with dve.Fori(0, B) as it:
                def hidden_of(t):
                    wait(dve, it, silu, t + 1)
                    wait(dve, it, down, 0)
                    dve.tensor_tensor(gT[:, t, :], sl[:, t % 3, :], pU[0:HT, t % 4, 1, :], ALU.mult).then_inc(hidden.sem, 1)

                def chained(n):
                    wait(dve, it, router, n)

                def choose():
                    wait(dve, it, gate, 1)
                    dve.tensor_tensor(gl[:], pR[:], bias_s[:, None, :].broadcast_to([P, NA, NE]), ALU.add).then_inc(router.sem, 1)
                    chained(1)
                    mine = gl[:].unsqueeze(3).broadcast_to([P, NA, NE, NE])
                    other = gl[:].unsqueeze(2).broadcast_to([P, NA, NE, NE])
                    dve.tensor_tensor(cmp[:, 0], other, mine, ALU.is_gt).then_inc(router.sem, 1)
                    dve.tensor_tensor(cmp[:, 1], other, mine, ALU.is_equal).then_inc(router.sem, 1)
                    dve.reduce_max(mx[:], gl[:], X).then_inc(router.sem, 1)
                    chained(4)
                    dve.tensor_tensor(cmp[:, 2], cmp[:, 1], lower[:, None, :, :].broadcast_to([P, NA, NE, NE]), ALU.mult).then_inc(router.sem, 1)
                    dve.tensor_tensor(ge[:], gl[:], mx[:].unsqueeze(2).broadcast_to([P, NA, NE]), ALU.subtract).then_inc(router.sem, 1)
                    chained(6)
                    dve.tensor_tensor(cmp[:, 1], cmp[:, 0], cmp[:, 2], ALU.add).then_inc(router.sem, 1)
                    chained(7)
                    dve.reduce_sum(rank[:], cmp[:, 1], X).then_inc(router.sem, 1)
                    chained(8)
                    wait(dve, it, place_p, 0)
                    dve.tensor_scalar(top[:], rank[:], float(TOPK), None, ALU.is_lt).then_inc(chosen.sem, 1)

                def weigh():
                    wait(dve, it, gexp, 1)
                    wait(dve, it, chosen, 1)
                    dve.tensor_tensor(gm[:], top[:], gx[:], ALU.mult).then_inc(router.sem, 1)
                    chained(9)
                    dve.reduce_sum(gs[:], gm[:], X).then_inc(router.sem, 1)
                    chained(10)
                    dve.reciprocal(gr[:], gs[:]).then_inc(router.sem, 1)
                    chained(11)
                    dve.tensor_tensor(route[:], gm[:], gr[:].unsqueeze(2).broadcast_to([P, NA, NE]), ALU.mult).then_inc(router.sem, 1)

                def step(n):
                    wait(dve, it, placed, n)

                def order_of():
                    wait(dve, it, chosen, 1)
                    dve.tensor_tensor(selT[:], top[:].unsqueeze(2).broadcast_to([P, NA, NE, NE]),
                                      lower[:, None, :, :].broadcast_to([P, NA, NE, NE]), ALU.mult).then_inc(placed.sem, 1)
                    step(1)
                    dve.reduce_sum(order[:], selT[:], X).then_inc(placed.sem, 1)
                    step(2)
                    for k in range(TOPK):
                        dve.scalar_tensor_tensor(out=hot[:, :, k, :], in0=order[:], scalar=float(k), in1=top[:],
                                                 op0=ALU.is_equal, op1=ALU.mult).then_inc(placed.sem, 1)

                def place():
                    wait(dve, it, place_p, 1)
                    dve.tensor_tensor(slot[:], pP[:, 0:NA, :], carry[:, None, :].broadcast_to([P, NA, NE]), ALU.add).then_inc(placed.sem, 1)
                    step(7)
                    dve.tensor_tensor(carry[:], pP[:, NA, :], carry[:], ALU.add).then_inc(placed.sem, 1)
                    dve.tensor_tensor(hs[:], hot[:], slot[:].unsqueeze(2).broadcast_to([P, NA, TOPK, NE]), ALU.mult).then_inc(placed.sem, 1)
                    step(9)
                    dve.reduce_sum(slotf[:], hs[:], X).then_inc(placed.sem, 1)
                    step(10)
                    dve.tensor_copy(sloti[:], slotf[:]).then_inc(placed.sem, 1)
                    step(11)
                    wait(dve, it, told, 0)
                    dve.tensor_scalar(hi[:], sloti[:], P - 1, (NE * NTE).bit_length() - 1, ALU.bitwise_and, ALU.logical_shift_left).then_inc(placed.sem, 1)
                    dve.tensor_scalar(lo[:], sloti[:], P.bit_length() - 1, None, ALU.logical_shift_right).then_inc(placed.sem, 1)
                    step(13)
                    dve.tensor_tensor(addr[:], hi[:], lo[:], ALU.bitwise_or).then_inc(placed.sem, 1)
                    dve.tensor_copy(pair[:, :, :, 0], toks[:, DS(it * NA, NA)].unsqueeze(2).broadcast_to([P, NA, TOPK])).then_inc(pairs.sem, 1)
                    wait(dve, it, router, 12)
                    dve.tensor_tensor(hr[:], hot[:], route[:].unsqueeze(2).broadcast_to([P, NA, TOPK, NE]), ALU.mult).then_inc(pairs.sem, 1)
                    wait(dve, it, pairs, 2)
                    dve.reduce_sum(pair[:, :, :, 1], hr[:], X).then_inc(pairs.sem, 1)

                choose()
                hidden_of(0)
                stats(it + 1)
                hidden_of(1)
                order_of()
                hidden_of(2)
                norm(it + 1)
                hidden_of(3)
                weigh()
                hidden_of(4)
                hidden_of(5)
                place()
                wait(dve, it, down, 1)
                wait(dve, it, stored, 0)
                dve.wait_ge(res_in.sem, res_in.count(it * 16 + 16))
                dve.tensor_tensor(acc[:], pD[:], hres[:], ALU.add).then_inc(summed.sem, 1)

            wait(dve, B, placed, 0)
            n = 0

            def chained(op):
                nonlocal n
                n += 1
                op.then_inc(table.sem, 1)
                dve.wait_ge(table.sem, table.count(n))

            chained(dve.tensor_tensor(count[:], carry[0:1, :], first[:], ALU.subtract))
            chained(dve.tensor_tensor(more[:], count[:].unsqueeze(2).broadcast_to([1, NE, NTE]), tiles[:, None, :].broadcast_to([1, NE, NTE]), ALU.is_gt))
            chained(dve.reduce_sum(nt[:], more[:], X))
            chained(dve.tensor_tensor(cum[:], nt[:, None, :].broadcast_to([1, NE, NE]), upto5[:], ALU.mult))
            chained(dve.reduce_sum(end[:], cum[:], X))
            chained(dve.tensor_tensor(past[:], nth[:].unsqueeze(2).broadcast_to([1, NLIST, NE]), end[:, None, :].broadcast_to([1, NLIST, NE]), ALU.is_ge))
            chained(dve.reduce_sum(ef[:], past[:], X))
            chained(dve.tensor_tensor(pastn[:], past[:], nt[:, None, :].broadcast_to([1, NLIST, NE]), ALU.mult))
            chained(dve.reduce_sum(sf[:], pastn[:], X))
            chained(dve.tensor_tensor(tf[:], nth[:], sf[:], ALU.subtract))
            chained(dve.scalar_tensor_tensor(out=tin[:], in0=ef[:], scalar=float(NE), in1=tf[:], op0=ALU.is_lt, op1=ALU.mult))
            chained(dve.scalar_tensor_tensor(out=tile[:], in0=ef[:], scalar=float(NTE), in1=tin[:], op0=ALU.mult, op1=ALU.add))
            chained(dve.tensor_scalar(expert[:], ef[:], float(NE - 1), None, ALU.min))

        @block.scalar
        def _(act):
            def root_of(n):
                wait(act, n, mean, 5)
                act.activation(lnv[:], ve[:], ACT.Ln).then_inc(root.sem, 1)
                wait(act, n, root, 1)
                wait(act, n, normed, 0)
                act.activation(rstd[:], lnv[:], ACT.Exp, scale=-0.5).then_inc(root.sem, 1)

            def rows_T(n):
                wait(act, n, xt_p, 1)
                wait(act, n, up, 0)
                act.activation(xT[:], pX[:], ACT.Copy).then_inc(xt.sem, 1)

            root_of(0)
            rows_T(0)
            with act.Fori(0, B) as it:
                for t in range(NHT):
                    wait(act, it, up, t + 1)
                    wait(act, it, hidden, max(0, t - 2))
                    act.activation(sl[:, t % 3, :], pU[0:HT, t % 4, 0, :], ACT.Silu).then_inc(silu.sem, 1)
                    if t == 1:
                        root_of(it + 1)
                        wait(act, it, router, 6)
                        act.activation(gx[:], ge[:], ACT.Exp).then_inc(gexp.sem, 1)
                rows_T(it + 1)

    return [(moved, B), (carried, B + 1), (xt_p, B + 1), (xt, B + 1), (silu, NHT * B), (hidden, NHT * B), (up, NHT * B), (down, B)]


def experts(nc, sems, loaded, consts, before, empty, W12, W3, w_in, tile, expert, xn_d, acc_d, slot_d, out):
    HH = HF // 2
    with ExitStack() as ctx:
        sb, ps = sbufs(nc, ctx), psums(nc, ctx)

        signals = []

        def sig(name, per=1):
            signals.append(Signal(nc, sems, "p5_" + name, per))
            return signals[-1]

        slots = sb("slots", [P, NE * NTE + 1, 2])
        ident5 = sb("ident5", [P, P])
        gidx = sb("gidx", [P, 1], I32)
        sidx = sb("sidx", [P, 1], I32)
        wcol = sb("wcol", [P, 1])
        zero5, step5, step6 = sb("zero5", [P, 1]), sb("step5", [P, 1]), sb("step6", [P, 1])
        xs = sb("xs", [P, D])
        xT = sb("xT5", [P, KC, P])
        sl = sb("sl5", [P, 2, HH])
        g = sb("g5", [P, NHT * HT])
        hT = sb("hT5", [HT, NHT, P])
        y = sb("y5", [P, D])

        pH = ps("pH5", [P, 2, 512])
        pV = ps("pV5", [P, 2, 512])
        pT = ps("pT5", [P, 2, 512])
        pX = ps("pX5", [P, 512])
        pD = ps("pD5", [P, 512])

        g_in, s_in, w_col = sig("g_in"), sig("s_in"), sig("w_col")
        gathered = Signal(nc, sems, "p5_gathered", 16, first=0)
        adding = Signal(nc, sems, "p5_adding", 16, first=0)
        added = sig("added")
        moved, carried, xt_p, xt, silu, hidden, up_h, down = [signal.onward(rises) for signal, rises in before]
        up_v, ht_p, ht_a, ht_v, scaled = sig("up_v"), sig("ht_p"), sig("ht_a"), sig("ht_v"), sig("scaled")
        done = sig("done")
        block = ctx.enter_context(nc.Block())

        @block.sync
        def _(sp):
            sp.dma_start(slots[:, 0:NE * NTE, :].rearrange("p n m -> p (n m)"), slot_d.rearrange("(p n) m -> p (n m)", p=P)).then_inc(loaded.sem, 16)
            sp.dma_start(slots[:, NE * NTE, :], empty).then_inc(loaded.sem, 16)
            sp.wait_ge(done.sem, done.count(1))
            rows = NT * P // 4
            for i in range(4):
                sp.dma_start(out.rearrange("b t n -> (b t) n")[i * rows:(i + 1) * rows, :], acc_d[i * rows:(i + 1) * rows, :]).then_inc(done.sem, 16)
            sp.wait_ge(done.sem, done.count(1 + 64))

        @block.gpsimd
        def _(pool):
            start(pool, signals)
            pool.memset(zero5[:], 0.0).then_inc(consts.sem, 1)
            pool.memset(ident5[:], 0.0).then_inc(consts.sem, 1)
            pool.memset(g[:], 0.0).then_inc(consts.sem, 1)
            pool.wait_ge(consts.sem, consts.count(3))
            pool.affine_select(out=ident5[:], in_=ident5[:], compare_op=ALU.not_equal, fill=1.0, base=0,
                               pattern=[[-1, P]], channel_multiplier=1).then_inc(consts.sem, 1)
            pool.wait_ge(consts.sem, consts.count(4))

            def gather(n):
                wait(pool, n, g_in, 1)
                wait(pool, n, xt_p, 0)
                wait(pool, n, moved, 0)
                pool.tensor_tensor(out=step5[:], in0=zero5[:], in1=zero5[:], op=ALU.add).then_inc(moved.sem, 1)
                pool.indirect_dma_start(out=xs[:], out_offset=None, in_=xn_d, in_offset=bass.IndirectOffsetOnAxis(ap=gidx[:], axis=0)).then_inc(gathered.sem, 16)

            def add(n):
                wait(pool, n, s_in, 1)
                wait(pool, n, scaled, 1)
                wait(pool, n, added, 0)
                wait(pool, n, carried, 0)
                pool.tensor_tensor(out=step6[:], in0=zero5[:], in1=zero5[:], op=ALU.add).then_inc(carried.sem, 1)
                pool.indirect_dma_start(out=acc_d, out_offset=bass.IndirectOffsetOnAxis(ap=sidx[:], axis=0), in_=y[:], in_offset=None,
                                        compute_op=ALU.add).then_inc(adding.sem, 16)
                pool.wait_ge(adding.sem, n * 16 + 16)
                pool.sem_inc(added.sem, 1)

            gather(0)
            gather(1)
            gather(2)
            with pool.Fori(0, NTILES - 1) as it:
                gather(it + 3)
                add(it)
            add(NTILES - 1)
            pool.wait_ge(gathered.sem, 16 * (NTILES + 2))
            pool.sem_inc(done.sem, 1)

        @block.tensor
        def _(pe):
            mm = nc.tensor.matmul
            pe.wait_ge(consts.sem, consts.count(4))
            pe.wait_ge(w_in.sem, w_in.count(16 * 2 * B))

            def rows_T(n):
                pe.wait_ge(gathered.sem, n * 16 + 16)
                wait(pe, n, xt, 0)
                for c in range(KC):
                    last = pe.transpose(pX[:, c * P:(c + 1) * P], xs[:, c * P:(c + 1) * P], ident5[:])
                last.then_inc(xt_p.sem, 1)

            def up(n, e, m, bank, signal):
                for i in range(2):
                    for c in range(KC):
                        last = mm(bank[:, i, 0:HH], xT[:, c, :], W12[:, DS(e, 1), c, m, i * HH:(i + 1) * HH].rearrange("p o n -> p (o n)"),
                                  start=(c == 0), stop=(c == KC - 1))
                last.then_inc(signal.sem, 1)

            def hidden_T(n):
                wait(pe, n, hidden, 1)
                wait(pe, n, ht_a, 0)
                wait(pe, n, ht_v, 0)
                for t in range(NHT):
                    last = pe.transpose(pT[0:HT, t // 4, t % 4 * P:(t % 4 + 1) * P], g[:, t * HT:(t + 1) * HT], ident5[:])
                last.then_inc(ht_p.sem, 1)

            def down_of(n, e):
                wait(pe, n, ht_a, 1)
                wait(pe, n, ht_v, 1)
                wait(pe, n, scaled, 0)
                for t in range(NHT):
                    last = mm(pD[:, 0:D], hT[:, t, :], W3[:, DS(e, 1), t, :].rearrange("p o n -> p (o n)"), start=(t == 0), stop=(t == NHT - 1))
                last.then_inc(down.sem, 1)

            def expert_of(n):
                return pe.value_load(expert[0:1, DS(n, 1)], min_val=0, max_val=NE - 1)

            def step(n, last):
                e = expert_of(n)
                wait(pe, n, xt, 1)
                wait(pe, n, silu, 0)
                up(n, e, 0, pH, up_h)
                if last is not None:
                    e_last = expert_of(last)
                    hidden_T(last)
                rows_T(n + 1)
                up(n, e, 1, pV, up_v)
                if last is not None:
                    down_of(last, e_last)

            rows_T(0)
            step(0, None)
            with pe.Fori(0, NTILES - 1) as it:
                step(it + 1, it)
            hidden_T(NTILES - 1)
            down_of(NTILES - 1, expert_of(NTILES - 1))

        @block.vector
        def _(dve):
            dve.wait_ge(loaded.sem, loaded.count(16 * 2))
            dve.wait_ge(consts.sem, consts.count(4))
            def tile_of(n):
                return dve.value_load(tile[0:1, DS(n, 1)], min_val=0, max_val=NE * NTE)

            def tokens_in(n):
                if not isinstance(n, int) or n > 0:
                    dve.wait_ge(gathered.sem, n * 16)
                dve.tensor_copy(gidx[:], slots[:, DS(tile_of(n), 1), 0]).then_inc(g_in.sem, 1)

            def tokens_out(n):
                wait(dve, n, added, 0)
                t = tile_of(n)
                dve.tensor_copy(sidx[:], slots[:, DS(t, 1), 0]).then_inc(s_in.sem, 1)
                wait(dve, n, scaled, 0)
                dve.tensor_copy(wcol[:], slots[:, DS(t, 1), 1]).then_inc(w_col.sem, 1)

            def hidden_of(n):
                wait(dve, n, up_v, 1)
                wait(dve, n, silu, 1)
                wait(dve, n, ht_p, 0)
                dve.tensor_tensor(g[:, 0:HF].rearrange("p (i n) -> p i n", i=2), sl[:], pV[:, :, 0:HH], ALU.mult).then_inc(hidden.sem, 1)

            def features(n):
                wait(dve, n, ht_p, 1)
                wait(dve, n, down, 0)
                dve.tensor_copy(hT[:, 4:NHT, :], pT[0:HT, 1, 0:(NHT - 4) * P].rearrange("p (t n) -> p t n", n=P)).then_inc(ht_v.sem, 1)

            def weighed(n):
                wait(dve, n, down, 1)
                wait(dve, n, w_col, 1)
                wait(dve, n, added, 0)
                dve.tensor_scalar(y[:], pD[:, 0:D], wcol[:, 0:1], None, ALU.mult).then_inc(scaled.sem, 1)

            tokens_in(0)
            tokens_in(1)
            tokens_in(2)
            hidden_of(0)
            with dve.Fori(0, NTILES - 1) as it:
                features(it)
                tokens_in(it + 3)
                hidden_of(it + 1)
                tokens_out(it)
                weighed(it)
            tokens_out(NTILES - 1)
            features(NTILES - 1)
            weighed(NTILES - 1)

        @block.scalar
        def _(act):
            def rows_T(n):
                wait(act, n, xt_p, 1)
                wait(act, n, up_v, 0)
                act.activation(xT[:].rearrange("p c n -> p (c n)"), pX[:, 0:D], ACT.Copy).then_inc(xt.sem, 1)

            def silu_of(n):
                wait(act, n, up_h, 1)
                wait(act, n, hidden, 0)
                act.activation(sl[:], pH[:, :, 0:HH], ACT.Silu).then_inc(silu.sem, 1)

            def features(n):
                wait(act, n, ht_p, 1)
                wait(act, n, down, 0)
                act.activation(hT[:, 0:4, :].rearrange("p t n -> p (t n)"), pT[0:HT, 0, :], ACT.Copy).then_inc(ht_a.sem, 1)

            rows_T(0)
            silu_of(0)
            rows_T(1)
            with act.Fori(0, NTILES - 1) as it:
                silu_of(it + 1)
                features(it)
                rows_T(it + 2)
            features(NTILES - 1)



def mixture(nc, sems, loaded, consts, h2_d, t, out):
    h2_rows = h2_d.rearrange("b t n -> (b t) n")
    xn_d = nc.dram_tensor("xn_scratch", (NT * P + P, D), F32).ap()
    acc_d = nc.dram_tensor("sum_scratch", (NT * P + P, D), F32).ap()
    slot_d = nc.dram_tensor("slot_scratch", (P * NE * NTE, 2), F32).ap()
    with ExitStack() as ctx:
        sb = sbufs(nc, ctx)
        W12 = sb("W12", [P, NE, KC, 2, NHT * HT])
        W3 = sb("W3", [HT, NE, NHT, D])
        carry = sb("carry", [P, NE])
        tile, expert = sb("tile", [1, NLIST], I32), sb("expert", [1, NLIST], I32)
        w_in = Signal(nc, sems, "p4_w_in", 0)
        before = route_and_share(nc, sems, loaded, consts, h2_rows, t["w12"], t["w3"], t["wg"], t["bias"], t["token_ids"], t["firsts"], t["pads"],
                                 (t["tiles"], t["nth"], t["upto"], t["firsts"].unsqueeze(0)), W12, W3, w_in, carry, tile, expert, xn_d, acc_d, slot_d)
        experts(nc, sems, loaded.onward(16 * 9), consts.onward(8), before, t["pads"][:, 0:2], W12, W3, w_in, tile, expert, xn_d, acc_d, slot_d, out)


def kernel(**inputs):
    import numpy as np
    import concourse.bacc as bacc
    from concourse.bass_utils import run_bass_kernel_spmd

    a = {k.replace("L0_", ""): np.asarray(v) for k, v in inputs.items()}
    def stacked(shared, routed):
        return np.concatenate([a[shared][None], a[routed]], 0)

    def padded(x):
        return np.pad(x, [(0, 0), (0, NHT * HT - HF), (0, 0)])

    w12 = np.stack([padded(stacked(f"ffn_Ws{m}", f"ffn_W{m}")) for m in (1, 2)])
    w12 = w12.reshape(2, E1, NHT * HT, KC, P).transpose(4, 1, 3, 0, 2).reshape(P, E1, -1)
    w3 = padded(stacked("ffn_Ws3", "ffn_W3").transpose(0, 2, 1))
    w3 = w3.reshape(E1, NHT, HT, D).transpose(2, 0, 1, 3).reshape(HT, E1, -1)
    arrays = {
        "w12": w12, "w3": w3, "wg": a["ffn_Wg"].T, "bias": a["ffn_routing_bias"],
        "ids": np.ascontiguousarray(a["x"].reshape(NT, P).T),
        "emb0": a["tok_emb0"], "emb1": a["tok_emb1"], "emb2": a["tok_emb2"], "emb3": a["tok_emb3"],
        "projT": np.ascontiguousarray(np.concatenate([a[f"tok_proj{i}"].T for i in range(4)], 0)),
        "wkq": np.concatenate([a["attn_Wk"], a["attn_Wq"]], 1),
        "wvbg": np.concatenate([a["attn_Wv"], a["attn_beta_w"], a["attn_g_w"]], 1),
        "wA": a["attn_wA"], "wB": a["attn_wB"], "conv": a["attn_conv_w"], "gb": a["attn_g_b"],
        "wo": a["attn_Wo"],
        "norms_w": np.stack([a["attn_knorm_w"], a["attn_qnorm_w"]]),
        "token_ids": np.arange(NT * P, dtype=np.float32).reshape(NT, P).T,
        "pads": np.tile(np.stack([NT * P + np.arange(P), np.zeros(P)], 1).astype(np.float32), (1, NE * NTE)),
        "firsts": np.arange(NE, dtype=np.float32) * NTE * P,
        "tiles": np.arange(NTE, dtype=np.float32)[None] * P,
        "nth": np.arange(NLIST, dtype=np.float32)[None],
        "upto": np.tril(np.ones((NE, NE), np.float32)).reshape(1, -1),
    }
    nc = bacc.Bacc("TRN2", target_bir_lowering=False, num_devices=1)
    t = {}
    arrays = {f"in_{n}": np.ascontiguousarray(v) for n, v in arrays.items()}
    for n, v in arrays.items():
        t[n[3:]] = nc.dram_tensor(n, v.shape, mybir.dt.from_np(v.dtype), kind="ExternalInput").ap()
    out = nc.dram_tensor("out", (B, T, D), F32, kind="ExternalOutput").ap()
    build(nc, t, out)
    r = run_bass_kernel_spmd(nc, [arrays], core_ids=[0])
    return r.results[0]["out"]


def build(nc, t, out):
    h_d = nc.dram_tensor("h_scratch", (B, T, D), F32).ap()
    F_d = nc.dram_tensor("heads_scratch", (B, P, NG * NA * 3 * P), F32).ap()
    tm_d = nc.dram_tensor("token_scratch", (B, T, TM), F32).ap()
    with ExitStack() as sems:
        loaded, consts = Signal(nc, sems, "loaded", 1), Signal(nc, sems, "consts", 1)
        embed_and_project(nc, sems, loaded, consts, t["ids"], [t[f"emb{i}"] for i in range(4)], t["projT"], t["wkq"], t["wvbg"],
                          t["wA"], t["wB"], t["conv"], t["gb"], t["norms_w"], h_d, F_d, tm_d)
        xt_d = nc.dram_tensor("xt_scratch", (B, NCB, H, CH, CH), F32).ap()
        bx_d = nc.dram_tensor("bx_scratch", (B, NCB, H, CH, CH), F32).ap()
        h2_d = nc.dram_tensor("h2_scratch", (B, T, D), F32).ap()
        loaded, consts = loaded.onward(16 * 9), consts.onward(9)
        attend(nc, sems, loaded, consts, F_d, tm_d, xt_d, bx_d, h_d, t["wo"], h2_d)
        mixture(nc, sems, loaded.onward(16), consts.onward(8), h2_d, t, out)
```
